# Optimizing a Trainium2 kernel written in Bass

```python
import numpy as np
import jax
import jax.numpy as jnp

def _softmax(x, axis=-1):
    return jax.nn.softmax(x, axis=axis)

def _gelu(x):
    return jax.nn.gelu(x, approximate=True)

def _silu(x):
    return jax.nn.silu(x)

def _sigmoid(x):
    return jax.nn.sigmoid(x)

def _layernorm(x, axis=-1, eps=1e-05):
    m = jnp.mean(x, axis=axis, keepdims=True)
    v = jnp.var(x, axis=axis, keepdims=True)
    return (x - m) / jnp.sqrt(v + eps)

def _scatter_add(tgt, idx, src, axis=0):
    return tgt.at[idx].add(src)

def _segment_sum(src, seg, n):
    return jax.ops.segment_sum(src, seg, n)
kernel_name = 'mk_macaron_d4_jaxref_r8_cdd0c4'

def setup_inputs(seed: int=0):
    np.random.seed(seed)
    _w = jnp.asarray

    def _L0_attn_setup():
        import jax, jax.numpy as jnp
        import numpy as np
        B, T, E, H = (2, 512, 128, 16)
        D = E // H
        EPS = 1e-06

        def _feature_map(x):
            return jnp.where(x > 0, x + 1.0, jnp.exp(x))
        key = jax.random.key(seed)
        ks = jax.random.split(key, 9)
        s = 1.0 / np.sqrt(E)
        return {'x': jax.random.normal(ks[0], (B, T, E), dtype=jnp.float32), 'wq': jax.random.uniform(ks[1], (E, E), jnp.float32, -s, s), 'bq': jax.random.uniform(ks[2], (E,), jnp.float32, -s, s), 'wk': jax.random.uniform(ks[3], (E, E), jnp.float32, -s, s), 'bk': jax.random.uniform(ks[4], (E,), jnp.float32, -s, s), 'wv': jax.random.uniform(ks[5], (E, E), jnp.float32, -s, s), 'bv': jax.random.uniform(ks[6], (E,), jnp.float32, -s, s), 'wo': jax.random.uniform(ks[7], (E, E), jnp.float32, -s, s), 'bo': jax.random.uniform(ks[8], (E,), jnp.float32, -s, s)}
    _L0_attn_in = _L0_attn_setup()

    def _L0_ffn_setup():
        import jax, jax.numpy as jnp
        import numpy as np
        DIM = 128
        HIDDEN = 512
        E = 8
        B, S = (2, 512)
        key = jax.random.key(seed)
        ks = jax.random.split(key, 8)
        sd = 1.0 / np.sqrt(DIM)
        sh = 1.0 / np.sqrt(HIDDEN)
        return {'x': jax.random.normal(ks[0], (B, S, DIM), dtype=jnp.float32), 'router_w': jax.random.uniform(ks[1], (DIM, E), jnp.float32, -sd, sd), 'router_b': jax.random.uniform(ks[2], (E,), jnp.float32, -sd, sd), 'w1': jax.random.uniform(ks[3], (E, DIM, 2 * HIDDEN), jnp.float32, -sd, sd), 'b1': jax.random.uniform(ks[4], (E, 2 * HIDDEN), jnp.float32, -sd, sd), 'w2': jax.random.uniform(ks[5], (E, HIDDEN, DIM), jnp.float32, -sh, sh), 'b2': jax.random.uniform(ks[6], (E, DIM), jnp.float32, -sh, sh)}
    _L0_ffn_in = _L0_ffn_setup()

    def _L1_attn_setup():
        import jax, jax.numpy as jnp
        import numpy as np
        B, N, D_IN, D_OUT, HEADS = (4, 512, 128, 128, 16)
        D_HEAD = D_OUT // HEADS
        key = jax.random.key(seed)
        ks = jax.random.split(key, 5)
        x = jax.random.normal(ks[0], (B, N, D_IN), dtype=jnp.float32)
        s_in = 1.0 / np.sqrt(D_IN)
        s_out = 1.0 / np.sqrt(D_OUT)
        Wq = jax.random.normal(ks[1], (D_IN, D_OUT), dtype=jnp.float32) * s_in
        Wk = jax.random.normal(ks[2], (D_IN, D_OUT), dtype=jnp.float32) * s_in
        Wv = jax.random.normal(ks[3], (D_IN, D_OUT), dtype=jnp.float32) * s_in
        Wo = jax.random.normal(ks[4], (D_OUT, D_OUT), dtype=jnp.float32) * s_out
        bo = jnp.zeros((D_OUT,), dtype=jnp.float32)
        return {'x': x, 'Wq': Wq, 'Wk': Wk, 'Wv': Wv, 'Wo': Wo, 'bo': bo}
    _L1_attn_in = _L1_attn_setup()

    def _L1_ffn_setup():
        import jax, jax.numpy as jnp
        import numpy as np
        B, S, D = (1, 256, 128)
        E, K, F = (64, 8, 96)
        SF = 96
        C = 64
        ROUTED_SCALE = 1.0

        def _moe_forward(x, router_w, w_gate, w_up, w_down, ws_gate_up, ws_down):
            T = x.shape[0]
            logits = x.astype(jnp.float32) @ router_w.T
            probs = jax.nn.softmax(logits, axis=-1)
            topk_w, topk_ids = jax.lax.top_k(probs, K)
            topk_w = topk_w / jnp.sum(topk_w, axis=-1, keepdims=True)
            topk_w = topk_w.astype(x.dtype)
            N = T * K
            flat_e = topk_ids.reshape(-1)
            flat_w = topk_w.reshape(-1)
            tok = jnp.arange(N) // K
            onehot = flat_e[:, None] == jnp.arange(E)[None, :]
            pos = jnp.cumsum(onehot, axis=0)[jnp.arange(N), flat_e] - 1
            valid = pos < C
            idx = jnp.where(valid, flat_e * C + pos, E * C)
            x_buf = jnp.zeros((E * C + 1, x.shape[1]), x.dtype).at[idx].set(x[tok])
            xb = x_buf[:E * C].reshape(E, C, -1)
            g = jnp.einsum('ecd,edf->ecf', xb, w_gate)
            u = jnp.einsum('ecd,edf->ecf', xb, w_up)
            h = jax.nn.silu(g) * u
            y = jnp.einsum('ecf,efd->ecd', h, w_down).reshape(E * C, -1)
            safe = jnp.where(valid, idx, 0)
            contrib = y[safe] * (flat_w * valid.astype(flat_w.dtype))[:, None]
            routed = jax.ops.segment_sum(contrib, tok, num_segments=T)
            routed = routed * ROUTED_SCALE
            gu = x @ ws_gate_up
            sg, su = (gu[:, :SF], gu[:, SF:])
            shared = jax.nn.silu(sg) * su @ ws_down
            return routed + shared
        key = jax.random.key(seed)
        ks = jax.random.split(key, 7)
        w = 0.02
        return {'hidden_states': jax.random.normal(ks[0], (B, S, D), jnp.float32), 'router_w': jax.random.normal(ks[1], (E, D), jnp.float32) * w, 'w_gate': jax.random.normal(ks[2], (E, D, F), jnp.float32) * w, 'w_up': jax.random.normal(ks[3], (E, D, F), jnp.float32) * w, 'w_down': jax.random.normal(ks[4], (E, F, D), jnp.float32) * w, 'ws_gate_up': jax.random.normal(ks[5], (D, 2 * SF), jnp.float32) * w, 'ws_down': jax.random.normal(ks[6], (SF, D), jnp.float32) * w}
    _L1_ffn_in = _L1_ffn_setup()

    def _L2_attn_setup():
        import jax, jax.numpy as jnp
        import numpy as np
        H, DK, DV = (16, 64, 64)
        LN_EPS = 1e-05
        key = jax.random.key(seed)
        ks = jax.random.split(key, 5)
        B, N, D = (4, 512, 128)
        s = 1.0 / np.sqrt(D)
        return {'inputs': jax.random.normal(ks[0], (B, N, D), dtype=jnp.float32), 'W_Q': jax.random.normal(ks[1], (D, H * DK), dtype=jnp.float32) * s, 'W_K': jax.random.normal(ks[2], (D, H * DK), dtype=jnp.float32) * s, 'W_V': jax.random.normal(ks[3], (D, H * DV), dtype=jnp.float32) * s, 'W_fc': jax.random.normal(ks[4], (H * DV, D), dtype=jnp.float32) * s, 'gamma': jnp.ones((D,), dtype=jnp.float32), 'beta': jnp.zeros((D,), dtype=jnp.float32)}
    _L2_attn_in = _L2_attn_setup()

    def _L2_ffn_setup():
        import jax, jax.numpy as jnp
        import numpy as np
        CAP_FACTOR = 1.5
        key = jax.random.key(seed)
        ks = jax.random.split(key, 6)
        E, S, D, M = (48, 4, 128, 128)
        K = D // S
        x = jax.random.normal(ks[0], (4, 512, D), dtype=jnp.float32)
        Wr = jax.random.normal(ks[1], (E, D), dtype=jnp.float32) * 0.02
        W1 = jax.random.normal(ks[2], (E, S, D, M), dtype=jnp.float32) * (1.0 / np.sqrt(D))
        b1 = jnp.zeros((E, S, M), dtype=jnp.float32)
        W2 = jax.random.normal(ks[3], (E, S, M, K), dtype=jnp.float32) * (1.0 / np.sqrt(M))
        b2 = jnp.zeros((E, S, K), dtype=jnp.float32)
        return {'x': x, 'Wr': Wr, 'W1': W1, 'b1': b1, 'W2': W2, 'b2': b2}
    _L2_ffn_in = _L2_ffn_setup()

    def _L3_attn_setup():
        import jax, jax.numpy as jnp
        import numpy as np
        D_MODEL = 128
        N_HEADS = 16
        D_HEAD = D_MODEL // N_HEADS
        key = jax.random.key(seed)
        kx, kq, kk, kv, ko = jax.random.split(key, 5)
        s = 1.0 / np.sqrt(D_MODEL)
        return {'x': jax.random.normal(kx, (4, 256, D_MODEL), dtype=jnp.float32), 'W_q': jax.random.normal(kq, (D_MODEL, D_MODEL), dtype=jnp.float32) * s, 'W_k': jax.random.normal(kk, (D_MODEL, D_MODEL), dtype=jnp.float32) * s, 'W_v': jax.random.normal(kv, (D_MODEL, D_MODEL), dtype=jnp.float32) * s, 'W_o': jax.random.normal(ko, (D_MODEL, D_MODEL), dtype=jnp.float32) * s}
    _L3_attn_in = _L3_attn_setup()

    def _L3_ffn_setup():
        import jax, jax.numpy as jnp
        import numpy as np
        D_IN, D_HID = (128, 512)

        def _ternary(key, shape):
            return jax.random.randint(key, shape, -1, 2).astype(jnp.float32)

        def _tlin(x, w, s):
            return jnp.einsum('bsi,oi->bso', x, w) * s
        key = jax.random.key(seed)
        ks = jax.random.split(key, 12)
        inv = lambda fan: 1.0 / np.sqrt(fan).astype(np.float32)
        return {'x': jax.random.normal(ks[0], (4, 256, D_IN), dtype=jnp.float32), 'w1_w': _ternary(ks[1], (D_HID, D_IN)), 'w1_s': jax.random.uniform(ks[2], (D_HID,), dtype=jnp.float32) * inv(D_IN), 'w2_w': _ternary(ks[3], (D_HID, D_IN)), 'w2_s': jax.random.uniform(ks[4], (D_HID,), dtype=jnp.float32) * inv(D_IN), 'h1_w': _ternary(ks[5], (D_HID, D_HID)), 'h1_s': jax.random.uniform(ks[6], (D_HID,), dtype=jnp.float32) * inv(D_HID), 'h2_w': _ternary(ks[7], (D_HID, D_HID)), 'h2_s': jax.random.uniform(ks[8], (D_HID,), dtype=jnp.float32) * inv(D_HID), 'w3_w': _ternary(ks[9], (D_IN, D_HID)), 'w3_s': jax.random.uniform(ks[10], (D_IN,), dtype=jnp.float32) * inv(D_HID)}
    _L3_ffn_in = _L3_ffn_setup()
    _d = {'L0_attn_x': _L0_attn_in['x'], 'L0_attn_wq': _L0_attn_in['wq'], 'L0_attn_bq': _L0_attn_in['bq'], 'L0_attn_wk': _L0_attn_in['wk'], 'L0_attn_bk': _L0_attn_in['bk'], 'L0_attn_wv': _L0_attn_in['wv'], 'L0_attn_bv': _L0_attn_in['bv'], 'L0_attn_wo': _L0_attn_in['wo'], 'L0_attn_bo': _L0_attn_in['bo'], 'L0_ffn_router_w': _L0_ffn_in['router_w'], 'L0_ffn_router_b': _L0_ffn_in['router_b'], 'L0_ffn_w1': _L0_ffn_in['w1'], 'L0_ffn_b1': _L0_ffn_in['b1'], 'L0_ffn_w2': _L0_ffn_in['w2'], 'L0_ffn_b2': _L0_ffn_in['b2'], 'L1_attn_Wq': _L1_attn_in['Wq'], 'L1_attn_Wk': _L1_attn_in['Wk'], 'L1_attn_Wv': _L1_attn_in['Wv'], 'L1_attn_Wo': _L1_attn_in['Wo'], 'L1_attn_bo': _L1_attn_in['bo'], 'L1_ffn_router_w': _L1_ffn_in['router_w'], 'L1_ffn_w_gate': _L1_ffn_in['w_gate'], 'L1_ffn_w_up': _L1_ffn_in['w_up'], 'L1_ffn_w_down': _L1_ffn_in['w_down'], 'L1_ffn_ws_gate_up': _L1_ffn_in['ws_gate_up'], 'L1_ffn_ws_down': _L1_ffn_in['ws_down'], 'L2_attn_W_Q': _L2_attn_in['W_Q'], 'L2_attn_W_K': _L2_attn_in['W_K'], 'L2_attn_W_V': _L2_attn_in['W_V'], 'L2_attn_W_fc': _L2_attn_in['W_fc'], 'L2_attn_gamma': _L2_attn_in['gamma'], 'L2_attn_beta': _L2_attn_in['beta'], 'L2_ffn_Wr': _L2_ffn_in['Wr'], 'L2_ffn_W1': _L2_ffn_in['W1'], 'L2_ffn_b1': _L2_ffn_in['b1'], 'L2_ffn_W2': _L2_ffn_in['W2'], 'L2_ffn_b2': _L2_ffn_in['b2'], 'L3_attn_W_q': _L3_attn_in['W_q'], 'L3_attn_W_k': _L3_attn_in['W_k'], 'L3_attn_W_v': _L3_attn_in['W_v'], 'L3_attn_W_o': _L3_attn_in['W_o'], 'L3_ffn_w1_w': _L3_ffn_in['w1_w'], 'L3_ffn_w1_s': _L3_ffn_in['w1_s'], 'L3_ffn_w2_w': _L3_ffn_in['w2_w'], 'L3_ffn_w2_s': _L3_ffn_in['w2_s'], 'L3_ffn_h1_w': _L3_ffn_in['h1_w'], 'L3_ffn_h1_s': _L3_ffn_in['h1_s'], 'L3_ffn_h2_w': _L3_ffn_in['h2_w'], 'L3_ffn_h2_s': _L3_ffn_in['h2_s'], 'L3_ffn_w3_w': _L3_ffn_in['w3_w'], 'L3_ffn_w3_s': _L3_ffn_in['w3_s']}
    _x0 = _d['L0_attn_x']
    _d['L0_attn_x'] = jax.random.normal(jax.random.fold_in(jax.random.key(seed), 1), (16, 256, 128), dtype=_x0.dtype)
    del _x0
    return _d

def reference(L0_attn_x, L0_attn_wq, L0_attn_bq, L0_attn_wk, L0_attn_bk, L0_attn_wv, L0_attn_bv, L0_attn_wo, L0_attn_bo, L0_ffn_router_w, L0_ffn_router_b, L0_ffn_w1, L0_ffn_b1, L0_ffn_w2, L0_ffn_b2, L1_attn_Wq, L1_attn_Wk, L1_attn_Wv, L1_attn_Wo, L1_attn_bo, L1_ffn_router_w, L1_ffn_w_gate, L1_ffn_w_up, L1_ffn_w_down, L1_ffn_ws_gate_up, L1_ffn_ws_down, L2_attn_W_Q, L2_attn_W_K, L2_attn_W_V, L2_attn_W_fc, L2_attn_gamma, L2_attn_beta, L2_ffn_Wr, L2_ffn_W1, L2_ffn_b1, L2_ffn_W2, L2_ffn_b2, L3_attn_W_q, L3_attn_W_k, L3_attn_W_v, L3_attn_W_o, L3_ffn_w1_w, L3_ffn_w1_s, L3_ffn_w2_w, L3_ffn_w2_s, L3_ffn_h1_w, L3_ffn_h1_s, L3_ffn_h2_w, L3_ffn_h2_s, L3_ffn_w3_w, L3_ffn_w3_s):

    def _L0_attn_ref(x, wq, bq, wk, bk, wv, bv, wo, bo):
        import jax, jax.numpy as jnp
        import numpy as np
        B, T, E, H = (2, 512, 128, 16)
        D = E // H
        EPS = 1e-06

        def _feature_map(x):
            return jnp.where(x > 0, x + 1.0, jnp.exp(x))
        b, t, e = x.shape
        q = _feature_map(x @ wq + bq).reshape(b, t, H, D)
        k = _feature_map(x @ wk + bk).reshape(b, t, H, D)
        v = (x @ wv + bv).reshape(b, t, H, D)
        qT = jnp.moveaxis(q, 1, 0)
        kT = jnp.moveaxis(k, 1, 0)
        vT = jnp.moveaxis(v, 1, 0)
        S0 = jnp.zeros((b, H, D, D), dtype=x.dtype)
        z0 = jnp.zeros((b, H, D), dtype=x.dtype)

        def step(carry, qkv):
            S, z = carry
            qt, kt, vt = qkv
            S = S + jnp.einsum('bhd,bhe->bhde', kt, vt)
            z = z + kt
            num = jnp.einsum('bhd,bhde->bhe', qt, S)
            den = jnp.einsum('bhd,bhd->bh', qt, z)[..., None] + EPS
            return ((S, z), num / den)
        _, outT = jax.lax.scan(step, (S0, z0), (qT, kT, vT))
        out = jnp.moveaxis(outT, 0, 1).reshape(b, t, e)
        return out @ wo + bo

    def _L0_ffn_ref(x, router_w, router_b, w1, b1, w2, b2):
        import jax, jax.numpy as jnp
        import numpy as np
        DIM = 128
        HIDDEN = 512
        E = 8
        B, S = (2, 512)
        logits = jnp.einsum('bsd,de->bse', x, router_w) + router_b
        probs = jax.nn.softmax(logits, axis=-1)
        top1 = jnp.argmax(probs, axis=-1)
        out = jnp.zeros_like(x)
        for i in range(E):
            h = jnp.einsum('bsd,df->bsf', x, w1[i]) + b1[i]
            a, g = jnp.split(h, 2, axis=-1)
            y = jnp.einsum('bsh,hd->bsd', a * jax.nn.sigmoid(g), w2[i]) + b2[i]
            out = out + jnp.where((top1 == i)[..., None], y, 0.0)
        return out

    def _L1_attn_ref(x, Wq, Wk, Wv, Wo, bo):
        import jax, jax.numpy as jnp
        import numpy as np
        B, N, D_IN, D_OUT, HEADS = (4, 512, 128, 128, 16)
        D_HEAD = D_OUT // HEADS
        q = jax.nn.softmax(jnp.einsum('bni,io->bno', x, Wq), axis=-1)
        k = jax.nn.softmax(jnp.einsum('bni,io->bno', x, Wk), axis=-2)
        v = jnp.einsum('bni,io->bno', x, Wv)
        scale = 1.0 / np.sqrt(D_HEAD).astype(np.float32)
        ctx = jnp.einsum('bnd,bne->bde', k, v) * scale
        y = jnp.einsum('bnd,bde->bne', q, ctx) / jnp.float32(D_OUT)
        return jnp.einsum('bnd,de->bne', y, Wo) + bo

    def _L1_ffn_ref(hidden_states, router_w, w_gate, w_up, w_down, ws_gate_up, ws_down):
        import jax, jax.numpy as jnp
        import numpy as np
        B, S, D = (1, 256, 128)
        E, K, F = (64, 8, 96)
        SF = 96
        C = 64
        ROUTED_SCALE = 1.0

        def _moe_forward(x, router_w, w_gate, w_up, w_down, ws_gate_up, ws_down):
            T = x.shape[0]
            logits = x.astype(jnp.float32) @ router_w.T
            probs = jax.nn.softmax(logits, axis=-1)
            topk_w, topk_ids = jax.lax.top_k(probs, K)
            topk_w = topk_w / jnp.sum(topk_w, axis=-1, keepdims=True)
            topk_w = topk_w.astype(x.dtype)
            N = T * K
            flat_e = topk_ids.reshape(-1)
            flat_w = topk_w.reshape(-1)
            tok = jnp.arange(N) // K
            onehot = flat_e[:, None] == jnp.arange(E)[None, :]
            pos = jnp.cumsum(onehot, axis=0)[jnp.arange(N), flat_e] - 1
            valid = pos < C
            idx = jnp.where(valid, flat_e * C + pos, E * C)
            x_buf = jnp.zeros((E * C + 1, x.shape[1]), x.dtype).at[idx].set(x[tok])
            xb = x_buf[:E * C].reshape(E, C, -1)
            g = jnp.einsum('ecd,edf->ecf', xb, w_gate)
            u = jnp.einsum('ecd,edf->ecf', xb, w_up)
            h = jax.nn.silu(g) * u
            y = jnp.einsum('ecf,efd->ecd', h, w_down).reshape(E * C, -1)
            safe = jnp.where(valid, idx, 0)
            contrib = y[safe] * (flat_w * valid.astype(flat_w.dtype))[:, None]
            routed = jax.ops.segment_sum(contrib, tok, num_segments=T)
            routed = routed * ROUTED_SCALE
            gu = x @ ws_gate_up
            sg, su = (gu[:, :SF], gu[:, SF:])
            shared = jax.nn.silu(sg) * su @ ws_down
            return routed + shared
        b, s, d = hidden_states.shape
        x = hidden_states.reshape(-1, d)
        out = _moe_forward(x, router_w, w_gate, w_up, w_down, ws_gate_up, ws_down)
        return out.reshape(b, s, d)

    def _L2_attn_ref(inputs, W_Q, W_K, W_V, W_fc, gamma, beta):
        import jax, jax.numpy as jnp
        import numpy as np
        H, DK, DV = (16, 64, 64)
        LN_EPS = 1e-05
        B, N, D = inputs.shape
        Q = jax.nn.sigmoid((inputs @ W_Q).reshape(B, N, H, DK))
        K = jax.nn.sigmoid((inputs @ W_K).reshape(B, N, H, DK))
        V = (inputs @ W_V).reshape(B, N, H, DV)
        KV = jnp.einsum('bnhk,bnhv->bhkv', K, V)
        num = jnp.einsum('bnhk,bhkv->bnhv', Q, KV)
        k_sum = K.sum(axis=1)
        den = jnp.einsum('bnhk,bhk->bnh', Q, k_sum)[..., None] + 1e-08
        out = (num / den).reshape(B, N, H * DV) @ W_fc
        x = out + inputs
        mu = x.mean(axis=-1, keepdims=True)
        var = jnp.mean((x - mu) ** 2, axis=-1, keepdims=True)
        return (x - mu) * jax.lax.rsqrt(var + LN_EPS) * gamma + beta

    def _L2_ffn_ref(x, Wr, W1, b1, W2, b2):
        import jax, jax.numpy as jnp
        import numpy as np
        CAP_FACTOR = 1.5
        orig_shape = x.shape
        D = x.shape[-1]
        E = Wr.shape[0]
        xf = x.reshape(-1, D)
        T = xf.shape[0]
        cap = int(CAP_FACTOR * T / E)
        logits = xf @ Wr.T
        vals, idx = jax.lax.top_k(logits.T, cap)
        w = jax.nn.softmax(vals, axis=-1)
        xg = xf[idx]
        h = jax.nn.gelu(jnp.einsum('ecd,esdm->ecsm', xg, W1) + b1[:, None], approximate=False)
        y = jnp.einsum('ecsm,esmk->ecsk', h, W2) + b2[:, None]
        y = y.reshape(E, cap, D) * w[..., None]
        out = jnp.zeros_like(xf).at[idx.reshape(-1)].add(y.reshape(-1, D))
        return out.reshape(orig_shape)

    def _L3_attn_ref(x, W_q, W_k, W_v, W_o):
        import jax, jax.numpy as jnp
        import numpy as np
        D_MODEL = 128
        N_HEADS = 16
        D_HEAD = D_MODEL // N_HEADS
        B, L, _ = x.shape

        def heads(h):
            return h.reshape(B, L, N_HEADS, D_HEAD).transpose(0, 2, 1, 3)
        q = heads(x @ W_q.T)
        k = heads(x @ W_k.T)
        v = heads(x @ W_v.T)
        scores = jnp.einsum('bhqd,bhkd->bhqk', q, k) / jnp.sqrt(jnp.float32(D_HEAD))
        attn = jax.nn.softmax(scores, axis=-1)
        ctx = jnp.einsum('bhqk,bhkd->bhqd', attn, v)
        ctx = ctx.transpose(0, 2, 1, 3).reshape(B, L, D_MODEL)
        return ctx @ W_o.T

    def _L3_ffn_ref(x, w1_w, w1_s, w2_w, w2_s, h1_w, h1_s, h2_w, h2_s, w3_w, w3_s):
        import jax, jax.numpy as jnp
        import numpy as np
        D_IN, D_HID = (128, 512)

        def _ternary(key, shape):
            return jax.random.randint(key, shape, -1, 2).astype(jnp.float32)

        def _tlin(x, w, s):
            return jnp.einsum('bsi,oi->bso', x, w) * s
        h = jax.nn.silu(_tlin(x, w1_w, w1_s)) * _tlin(x, w2_w, w2_s)
        h = jax.nn.gelu(_tlin(h, h1_w, h1_s), approximate=False)
        h = jax.nn.gelu(_tlin(h, h2_w, h2_s), approximate=False)
        return _tlin(h, w3_w, w3_s)
    x = L0_attn_x
    x = x + 0.5 * _L0_ffn_ref(_layernorm(x, axis=-1), L0_ffn_router_w, L0_ffn_router_b, L0_ffn_w1, L0_ffn_b1, L0_ffn_w2, L0_ffn_b2)
    x = x + _L0_attn_ref(_layernorm(x, axis=-1), L0_attn_wq, L0_attn_bq, L0_attn_wk, L0_attn_bk, L0_attn_wv, L0_attn_bv, L0_attn_wo, L0_attn_bo)
    x = x + 0.5 * _L0_ffn_ref(_layernorm(x, axis=-1), L0_ffn_router_w, L0_ffn_router_b, L0_ffn_w1, L0_ffn_b1, L0_ffn_w2, L0_ffn_b2)
    x = x + 0.5 * _L1_ffn_ref(_layernorm(x, axis=-1), L1_ffn_router_w, L1_ffn_w_gate, L1_ffn_w_up, L1_ffn_w_down, L1_ffn_ws_gate_up, L1_ffn_ws_down)
    x = x + _L1_attn_ref(_layernorm(x, axis=-1), L1_attn_Wq, L1_attn_Wk, L1_attn_Wv, L1_attn_Wo, L1_attn_bo)
    x = x + 0.5 * _L1_ffn_ref(_layernorm(x, axis=-1), L1_ffn_router_w, L1_ffn_w_gate, L1_ffn_w_up, L1_ffn_w_down, L1_ffn_ws_gate_up, L1_ffn_ws_down)
    x = x + 0.5 * _L2_ffn_ref(_layernorm(x, axis=-1), L2_ffn_Wr, L2_ffn_W1, L2_ffn_b1, L2_ffn_W2, L2_ffn_b2)
    x = x + _L2_attn_ref(_layernorm(x, axis=-1), L2_attn_W_Q, L2_attn_W_K, L2_attn_W_V, L2_attn_W_fc, L2_attn_gamma, L2_attn_beta)
    x = x + 0.5 * _L2_ffn_ref(_layernorm(x, axis=-1), L2_ffn_Wr, L2_ffn_W1, L2_ffn_b1, L2_ffn_W2, L2_ffn_b2)
    x = x + 0.5 * _L3_ffn_ref(_layernorm(x, axis=-1), L3_ffn_w1_w, L3_ffn_w1_s, L3_ffn_w2_w, L3_ffn_w2_s, L3_ffn_h1_w, L3_ffn_h1_s, L3_ffn_h2_w, L3_ffn_h2_s, L3_ffn_w3_w, L3_ffn_w3_s)
    x = x + _L3_attn_ref(_layernorm(x, axis=-1), L3_attn_W_q, L3_attn_W_k, L3_attn_W_v, L3_attn_W_o)
    x = x + 0.5 * _L3_ffn_ref(_layernorm(x, axis=-1), L3_ffn_w1_w, L3_ffn_w1_s, L3_ffn_w2_w, L3_ffn_w2_s, L3_ffn_h1_w, L3_ffn_h1_s, L3_ffn_h2_w, L3_ffn_h2_s, L3_ffn_w3_w, L3_ffn_w3_s)
    return x

_drawn_inputs = setup_inputs


def setup_inputs(seed=0):
    import zlib

    import numpy as np

    out = dict(_drawn_inputs(seed))
    spreads = {'L1_attn_bo': (0.0, 0.1),
     'L2_attn_gamma': (1.0, 0.2),
     'L2_attn_beta': (0.0, 0.1),
     'L2_ffn_b1': (0.0, 0.1),
     'L2_ffn_b2': (0.0, 0.1)}
    factors = {}
    for name, (base, spread) in spreads.items():
        noise = np.random.default_rng([zlib.crc32(name.encode()), seed]).standard_normal(out[name].shape)
        drawn = base * np.exp(spread * noise) if base else spread * noise
        out[name] = jnp.asarray(drawn.astype(out[name].dtype))
    for name, factor in factors.items():
        out[name] = (out[name] * factor).astype(out[name].dtype)
    return out
```

```python
from contextlib import ExitStack, contextmanager

import concourse.bass as bass
from concourse import mybir

F32 = mybir.dt.float32
BF16 = mybir.dt.bfloat16
U32 = mybir.dt.uint32
ALU = mybir.AluOpType
ACT = mybir.ActivationFunctionType
AX = mybir.AxisListType

P = 128
D = 128
B, N = 16, 256
TOKENS = B * N
TILES = TOKENS // P
CT = 4
CW = CT * P
CHUNKS = TILES // CT


class Signal:

    def __init__(self, sem, ahead):
        self.sem = sem
        self.ahead = ahead

    def past(self, n):
        return n + 1 + self.ahead


class Stage:

    count = 0

    def __init__(self, nc, ctx):
        Stage.count += 1
        self.prefix = f"s{Stage.count}_"
        self.nc = nc
        self.ctx = ctx
        self.made = []
        self.pools = []

    def sig(self, name, ahead=0):
        s = Signal(self.ctx.enter_context(self.nc.semaphore(self.prefix + name)), ahead)
        self.made.append(s)
        return s

    def pool_dmas(self, core):
        self.pools = core.pool_dmas
        return self.pools

    def reset_pool_dmas(self, pool):
        nums = [s.sem.num for s in self.pools]
        pool.dma_reset(range(min(nums), max(nums) + 1))

    def sb(self, name, shape, dt=F32):
        return self.ctx.enter_context(self.nc.sbuf_tensor(self.prefix + name, shape, dt))

    def ps(self, name, shape, dt=F32):
        return self.ctx.enter_context(self.nc.psum_tensor(self.prefix + name, shape, dt))

    def ready(self):
        nums = [s.sem.num for s in self.made]
        self.nc.sync.sem_clear(range(min(nums), max(nums) + 1))
        if self.pools:
            nums = [s.sem.num for s in self.pools]
            self.nc.sync.sem_clear(range(min(nums), max(nums) + 1))
        for s in self.made:
            if s.ahead:
                self.nc.sync.sem_inc(s.sem, s.ahead)
        self.nc.all_engine_barrier()


@contextmanager
def stage(nc):
    with ExitStack() as ctx:
        yield Stage(nc, ctx)


def rows(t, first, count=1):
    return t[:, bass.ds(first, count), :]


class Core:

    def __init__(self, nc, ctx, inputs, out):
        self.nc = nc
        self.w = inputs
        self.out = out

        def sb(name, shape, dt=F32):
            return ctx.enter_context(nc.sbuf_tensor(name, shape, dt))

        self.pool_dmas = [Signal(ctx.enter_context(nc.semaphore(f"pool_dma{n}")), 0) for n in range(6)]
        self.x = sb("x", [P, TILES, D])
        self.ident = sb("ident", [P, P])
        self.sums = sb("sums", [P, TILES, 6])
        self.mean = sb("mean", [P, TILES])
        self.rstd = sb("rstd", [P, TILES])
        self.ln_t = sb("ln_t", [P, 3, TILES])
        self.xn = sb("xn", [P, 2, CT, D])
        self.xnt = sb("xnt", [P, 2, CW])
        self.all_xn = sb("all_xn", [P, TILES, D])
        self.rows_dram = nc.dram_tensor("rows_dram", (40 * P, D), F32, kind="Internal").ap()
        self.table_dram = nc.dram_tensor("table_dram", (TOKENS + 64, D + 64), F32, kind="Internal").ap()
        self.acc_dram = nc.dram_tensor("acc_dram", (2 * (TOKENS + 64), D), F32, kind="Internal").ap()
        self.sums_dram = nc.dram_tensor("sums_dram", (40 * P, D), F32, kind="Internal").ap()



def ln_signals(s, tp_banks=2):
    s.tp_banks = tp_banks
    s.xn_ready = s.sig("xn_ready")
    s.tp_ready = s.sig("tp_ready", 2)
    s.xnt_ready = s.sig("xnt_ready", 2)
    s.sd_ready = s.sig("sd_ready")
    s.var_ready = s.sig("var_ready")
    s.tp = s.ps("tp", [P, tp_banks, CW])


def ln_scales_dve(dve, core, s, ln_eps=1e-5):
    me, mo = core.sums[:, :, 1], core.sums[:, :, 4]
    t0, t1, t2 = (core.ln_t[:, i, :] for i in range(3))
    dve.tensor_tensor(t0, me, mo, ALU.add)
    dve.tensor_tensor(t1, me, mo, ALU.subtract)
    dve.tensor_tensor(t2, core.sums[:, :, 2], core.sums[:, :, 5], ALU.add)
    dve.drain()
    dve.tensor_scalar(core.mean[:, :], t0, 0.5, None, ALU.mult)
    dve.tensor_tensor(t1, t1, t1, ALU.mult)
    dve.tensor_scalar(t2, t2, 1.0 / D, ln_eps, ALU.mult, ALU.add)
    dve.drain()
    dve.scalar_tensor_tensor(t2, t1, 0.25, t2, ALU.mult, ALU.add).then_inc(s.var_ready.sem, 1)
    dve.wait_ge(s.sd_ready.sem, s.sd_ready.past(0))
    dve.reciprocal(t1, t0)
    dve.drain()
    dve.tensor_tensor(t0, t1, t1, ALU.mult)
    dve.drain()
    dve.tensor_tensor(t0, t0, t2, ALU.mult)
    dve.drain()
    dve.tensor_scalar(t0, t0, -0.5, 1.5, ALU.mult, ALU.add)
    dve.drain()
    dve.tensor_tensor(core.rstd[:, :], t0, t1, ALU.mult)
    dve.drain()


def ln_scales_act(act, core, s):
    act.wait_ge(s.var_ready.sem, s.var_ready.past(0))
    act.activation(core.ln_t[:, 0, :], core.ln_t[:, 2, :], ACT.Sqrt).then_inc(s.sd_ready.sem, 1)


def ln_dve(dve, core, s, c, u, copied=None):
    dve.wait_ge(s.tp_ready.sem, s.tp_ready.past(c - 2))
    if copied:
        dve.wait_ge(copied.sem, copied.past(c - 2))
    for j in range(CT):
        t = c * CT + j
        last = dve.tensor_scalar(core.xn[:, u, j, :], core.x[:, bass.ds(t, 1), :],
                                 core.mean[:, bass.ds(t, 1)], core.rstd[:, bass.ds(t, 1)],
                                 ALU.subtract, ALU.mult)
    last.then_inc(s.xn_ready.sem, 1)


def ln_pe(pe, core, s, c, u):
    pe.wait_ge(s.xn_ready.sem, s.xn_ready.past(c))
    pe.wait_ge(s.xnt_ready.sem, s.xnt_ready.past(c - s.tp_banks))
    for j in range(CT):
        last = pe.transpose(s.tp[:, u % s.tp_banks, j * P:(j + 1) * P], core.xn[:, u, j, :], core.ident[:, :])
    last.then_inc(s.tp_ready.sem, 1)


def ln_act(act, core, s, c, u):
    act.wait_ge(s.tp_ready.sem, s.tp_ready.past(c))
    act.activation(core.xnt[:, u, :], s.tp[:, u % s.tp_banks, :], ACT.Copy).then_inc(s.xnt_ready.sem, 1)


def new_sums_dve(dve, core, c, tiles=range(CT)):
    for j in tiles:
        t = c * CT + j
        last = dve.bn_stats(core.sums[:, bass.ds(t, 1), :], core.x[:, bass.ds(t, 1), :])
    return last


def each_pair(eng, first, last, body):
    assert first % 2 == 0 and last % 2 == 0
    with eng.Fori(first // 2, last // 2) as pair:
        for u in range(2):
            body(pair * 2 + u, u)



HEADS = 16
DH = D // HEADS
GROUPS = 4
HW = DH + 1


def head_masks(core, s):
    s.head = s.sb("head", [P, HEADS])
    s.group = s.sb("group", [P, GROUPS])
    s.place = s.sb("place", [P, GROUPS])
    s.head_step = s.sig("head_step")


def head_masks_pool(pool, s):
    pool.memset(s.head[:, :], 1.0).then_inc(s.head_step.sem, 1)
    pool.wait_ge(s.head_step.sem, 1)
    pool.affine_select(out=s.head[:, :], in_=s.head[:, :], compare_op=ALU.is_ge, fill=0.0,
                       base=0, pattern=[[-DH, HEADS]], channel_multiplier=1).then_inc(s.head_step.sem, 1)
    pool.wait_ge(s.head_step.sem, 2)
    pool.affine_select(out=s.head[:, :], in_=s.head[:, :], compare_op=ALU.is_ge, fill=0.0,
                       base=DH - 1, pattern=[[DH, HEADS]], channel_multiplier=-1).then_inc(s.head_step.sem, 1)


def head_masks_dve(dve, s):
    dve.wait_ge(s.head_step.sem, 3)
    by = s.head[:, :].rearrange("p (g j) -> p g j", g=GROUPS)
    dve.tensor_reduce(s.group[:, :], by, AX.X, ALU.add)
    dve.tensor_reduce(s.place[:, :], by.rearrange("p g j -> p j g"), AX.X, ALU.add).then_inc(s.head_step.sem, 1)


MASKS_READY = 4



def l0_ffn(core):
    nc, w = core.nc, core.w
    EXPERTS, _, WIDE = w["L0_ffn_w1"].shape
    HID = WIDE // 2
    HB = HID // P
    SLOTS = TILES + EXPERTS
    I32 = mybir.dt.int32
    with stage(nc) as s:
        ln_signals(s, 1)
        wr = s.sb("wr", [P, EXPERTS])
        rb = s.sb("rb", [P, EXPERTS])
        w1 = s.sb("w1", [P, EXPERTS, WIDE])
        b1 = s.sb("b1", [P, EXPERTS, WIDE])
        w2 = s.sb("w2", [P, EXPERTS, HB, P])
        b2 = s.sb("b2", [P, EXPERTS, P])
        earlier = s.sb("earlier", [P, P])
        ones = s.sb("ones", [P, P])
        rev_i = s.sb("rev_i", [P, EXPERTS], I32)
        rev = s.sb("rev", [P, EXPERTS])
        first_i = s.sb("first_i", [P, SLOTS], I32)
        first = s.sb("first", [P, SLOTS])
        zero = s.sb("zero", [P, EXPERTS, TILES])
        logits = s.sb("logits", [P, TILES, EXPERTS])
        best = s.sb("best", [P, TILES])
        hot = s.sb("hot", [P, TILES, EXPERTS])
        tot = s.sb("tot", [P, EXPERTS, TILES])
        run = s.sb("run", [P, EXPERTS, TILES])
        start = s.sb("start", [P, EXPERTS])
        padded_i = s.sb("padded_i", [P, EXPERTS], I32)
        padded = s.sb("padded", [P, EXPERTS])
        pad_end = s.sb("pad_end", [P, EXPERTS])
        later = s.sb("later", [P, SLOTS, EXPERTS])
        owner = s.sb("owner", [P, SLOTS])
        owner_i = s.sb("owner_i", [P, SLOTS], I32)
        pos = s.sb("pos", [P, TILES])
        pos_i = s.sb("pos_i", [P, TILES], U32)
        xs = s.sb("xs", [P, 2, D])
        xst = s.sb("xst", [P, 2, P])
        ab = s.sb("ab", [P, 2, HID])
        gb = s.sb("gb", [P, 2, HID])
        hs = s.sb("hs", [P, 2, HID])
        ht = s.sb("ht", [P, 2, HB, P])
        yo = s.sb("yo", [P, 2, D])
        ha = s.ps("ha", [P, 2, HID])
        hg = s.ps("hg", [P, 2, HID])
        htp = s.ps("htp", [P, 2, HB, P])
        yp = s.ps("yp", [P, CW])
        w_loaded = s.sig("w_loaded")
        router_loaded = s.sig("router_loaded")
        filled = s.sig("filled")
        cleared = s.sig("cleared")
        rows_zeroed = s.sig("rows_zeroed")
        copied = s.sig("copied", 2)
        routed = s.sig("routed")
        logits_kept = s.sig("logits_kept", 1)
        hot_ready = s.sig("hot_ready")
        counted = s.sig("counted")
        pos_ready = s.sig("pos_ready")
        owner_ready = s.sig("owner_ready")
        scattered, *gathered = s.pool_dmas(core)[0:5]
        xs_loaded = [s.sig(f"xs_loaded{u}") for u in range(2)]
        xt_done = s.sig("xt_done", 2)
        xst_kept = s.sig("xst_kept", 1)
        h_done = s.sig("h_done")
        biased = s.sig("biased", 2)
        sig_done = s.sig("sig_done")
        gated = s.sig("gated")
        ht_done = s.sig("ht_done")
        ht_kept = s.sig("ht_kept", 2)
        y_done = s.sig("y_done")
        y_kept = s.sig("y_kept", 1)
        stored = [s.sig(f"stored{u}", 16) for u in range(2)]
        s.ready()
        xt = s.tp[:, 0, 0:P]
        rows_dram, sums_dram = core.rows_dram, core.sums_dram
        block = s.ctx.enter_context(nc.Block())

        def each_slot(eng, body):
            with eng.Fori(0, SLOTS // 2 - 1) as pair:
                for u in range(2):
                    body(pair * 2 + u, pair, u, True)
            body(SLOTS - 2, SLOTS // 2 - 1, 0, True)
            body(SLOTS - 1, SLOTS // 2 - 1, 1, False)

        @block.sync
        def _(sp):
            sp.dma_start(wr[:, :], w["L0_ffn_router_w"]).then_inc(router_loaded.sem, 16)
            sp.dma_start(rb[:, :], w["L0_ffn_router_b"].partition_broadcast(P)).then_inc(router_loaded.sem, 16)
            sp.dma_start(w1[:, :, :], w["L0_ffn_w1"].rearrange("e d f -> d e f")).then_inc(w_loaded.sem, 16)
            sp.dma_start(w2[:, :, :, :], w["L0_ffn_w2"].rearrange("e (a p) n -> p e a n", p=P)).then_inc(w_loaded.sem, 16)
            for e in range(EXPERTS):
                sp.dma_start(b1[:, e, :], w["L0_ffn_b1"][e].partition_broadcast(P)).then_inc(w_loaded.sem, 16)
                sp.dma_start(b2[:, e, :], w["L0_ffn_b2"][e].partition_broadcast(P)).then_inc(w_loaded.sem, 16)
            sp.wait_ge(filled.sem, 1)
            for n in range(SLOTS // 2):
                sp.dma_start(rows_dram[n * 2 * P:(n + 1) * 2 * P, :].rearrange("(a p) d -> p a d", p=P),
                             zero[:, :, :].rearrange("p a b -> p (a b)").rearrange("p (a d) -> p a d", a=2)).then_inc(rows_zeroed.sem, 16)
            sp.wait_ge(scattered.sem, 16 * TILES)
            for u in range(2):
                sp.dma_start(xs[:, u, :], rows_dram[u * P:(u + 1) * P, :]).then_inc(xs_loaded[u].sem, 16)

            def body(i, pair, u, more):
                if more:
                    sp.wait_ge(xt_done.sem, xt_done.past(i))
                    sp.dma_start(xs[:, u, :], rows_dram[bass.ds(i * P + 2 * P, P), :]).then_inc(xs_loaded[u].sem, 16)
                sp.wait_ge(y_kept.sem, y_kept.past(i))
                sp.dma_start(sums_dram[bass.ds(i * P, P), :], yo[:, u, :]).then_inc(stored[u].sem, 16)

            with sp.Fori(0, SLOTS // 2 - 1) as pair:
                for u in range(2):
                    body(pair * 2 + u, pair, u, True)
            for u in range(2):
                body(SLOTS - 2 + u, SLOTS // 2 - 1, u, False)

        @block.gpsimd
        def _(pool):
            pool.memset(ones[:, :], 1.0).then_inc(cleared.sem, 1)
            pool.memset(earlier[:, :], 1.0).then_inc(cleared.sem, 1)
            pool.memset(zero[:, :, :], 0.0).then_inc(cleared.sem, 1)
            pool.iota(rev_i[:, :], pattern=[[-1, EXPERTS]], base=EXPERTS, channel_multiplier=0).then_inc(cleared.sem, 1)
            pool.iota(first_i[:, :], pattern=[[P, SLOTS]], base=0, channel_multiplier=0).then_inc(cleared.sem, 1)
            pool.wait_ge(cleared.sem, 5)
            pool.affine_select(out=earlier[:, :], in_=earlier[:, :], compare_op=ALU.is_gt, fill=0.0,
                               base=0, pattern=[[1, P]], channel_multiplier=-1).then_inc(filled.sem, 1)

            def copy(c, u):
                pool.wait_ge(s.xn_ready.sem, s.xn_ready.past(c))
                pool.tensor_copy(rows(core.all_xn, c * CT, CT), core.xn[:, u, :, :]).then_inc(copied.sem, 1)

            each_pair(pool, 0, CHUNKS, copy)
            pool.wait_ge(rows_zeroed.sem, 16 * (SLOTS // 2))
            pool.wait_ge(pos_ready.sem, 1)
            pool.wait_ge(copied.sem, copied.past(CHUNKS - 1))
            for t in range(TILES):
                pool.indirect_dma_start(rows_dram, bass.IndirectOffsetOnAxis(ap=pos_i[:, t:t + 1], axis=0),
                                        core.all_xn[:, t, :], None).then_inc(scattered.sem, 16)

            for u in range(2):
                pool.wait_ge(stored[u].sem, 16 + 16 * (SLOTS // 2))
            pool.wait_ge(scattered.sem, 16 * TILES)
            for t in range(TILES):
                pool.indirect_dma_start(core.all_xn[:, t, :], None, sums_dram,
                                        bass.IndirectOffsetOnAxis(ap=pos_i[:, t:t + 1], axis=0)).then_inc(gathered[t // 8].sem, 16)
            for q in range(4):
                pool.wait_ge(gathered[q].sem, 16 * 8)
            s.reset_pool_dmas(pool)

        @block.vector
        def _(dve):
            ln_scales_dve(dve, core, s)
            ln_dve(dve, core, s, 0, 0, copied)
            dve.wait_ge(router_loaded.sem, 32)

            def route(c, u, more=True):
                if more:
                    ln_dve(dve, core, s, c + 1, 1 - u, copied)
                dve.wait_ge(routed.sem, routed.past(c))
                dve.tensor_tensor(rows(logits, c * CT, CT), yp[:, 0:CT * EXPERTS].rearrange("p (t e) -> p t e", e=EXPERTS),
                                  rb[:, :].unsqueeze(1).to_broadcast([P, CT, EXPERTS]), ALU.add).then_inc(logits_kept.sem, 1)

            each_pair(dve, 0, CHUNKS - 2, route)
            route(CHUNKS - 2, 0)
            route(CHUNKS - 1, 1, False)
            dve.drain()
            dve.wait_ge(filled.sem, 1)
            dve.tensor_copy(rev[:, :], rev_i[:, :])
            dve.tensor_copy(first[:, :], first_i[:, :])
            dve.tensor_reduce(best[:, :], logits[:, :, :], AX.X, ALU.max)
            dve.drain()

            def by_tile(v):
                return v[:, :].unsqueeze(2).to_broadcast([P, TILES, EXPERTS])

            def by_expert(v, n, last):
                return v[:, :].unsqueeze(1 if last else 2).to_broadcast([P, n, EXPERTS] if last else [P, EXPERTS, n])

            dve.tensor_tensor(hot[:, :, :], logits[:, :, :], by_tile(best), ALU.is_equal)
            dve.drain()
            dve.tensor_tensor(hot[:, :, :], hot[:, :, :], by_expert(rev, TILES, True), ALU.mult)
            dve.drain()
            dve.tensor_reduce(best[:, :], hot[:, :, :], AX.X, ALU.max)
            dve.drain()
            dve.tensor_tensor(hot[:, :, :], by_tile(best), by_expert(rev, TILES, True), ALU.is_equal).then_inc(hot_ready.sem, 1)
            dve.wait_ge(counted.sem, 1)
            dve.tensor_copy(tot[:, :, :], hg[:, 0, 0:TILES * EXPERTS].rearrange("p (t e) -> p e t", e=EXPERTS))
            dve.drain()
            flat = lambda t: t[:, :, :].rearrange("p a b -> p (a b)")
            dve.tensor_tensor_scan(flat(run), flat(tot), flat(zero), 0.0, ALU.add, ALU.add)
            dve.memset(start[:, 0:1], 0.0)
            dve.drain()
            dve.tensor_copy(start[:, 1:EXPERTS], run[:, 0:EXPERTS - 1, TILES - 1])
            dve.drain()
            dve.tensor_tensor(padded[:, :], run[:, :, TILES - 1], start[:, :], ALU.subtract)
            dve.drain()
            dve.tensor_scalar(padded_i[:, :], padded[:, :], float(P - 1), None, ALU.add)
            dve.drain()
            dve.tensor_scalar(padded_i[:, :], padded_i[:, :], -P, None, ALU.bitwise_and)
            dve.drain()
            dve.tensor_copy(padded[:, :], padded_i[:, :])
            dve.drain()
            dve.tensor_tensor_scan(pad_end[:, :], padded[:, :], zero[:, 0, 0:EXPERTS], 0.0, ALU.add, ALU.add)
            dve.drain()
            dve.tensor_tensor(padded[:, :], pad_end[:, :], padded[:, :], ALU.subtract)
            dve.drain()
            dve.tensor_tensor(padded[:, :], padded[:, :], start[:, :], ALU.subtract)
            dve.tensor_tensor(run[:, :, :], run[:, :, :], tot[:, :, :], ALU.subtract)
            dve.drain()
            dve.tensor_tensor(run[:, :, :], run[:, :, :], by_expert(padded, TILES, False), ALU.add)
            dve.drain()
            dve.tensor_tensor(run[:, :, :], run[:, :, :], ha[:, 0, 0:TILES * EXPERTS].rearrange("p (t e) -> p e t", e=EXPERTS), ALU.add)
            dve.drain()
            dve.tensor_tensor(hot[:, :, :], hot[:, :, :], run[:, :, :].rearrange("p e t -> p t e"), ALU.mult)
            dve.drain()
            dve.tensor_reduce(pos[:, :], hot[:, :, :], AX.X, ALU.add)
            dve.drain()
            dve.tensor_copy(pos_i[:, :], pos[:, :]).then_inc(pos_ready.sem, 1)
            dve.tensor_tensor(later[:, :, :], first[:, :].unsqueeze(2).to_broadcast([P, SLOTS, EXPERTS]),
                              by_expert(pad_end, SLOTS, True), ALU.is_ge)
            dve.drain()
            dve.tensor_reduce(owner[:, :], later[:, :, :], AX.X, ALU.add)
            dve.drain()
            dve.tensor_scalar(owner_i[:, :], owner[:, :], float(EXPERTS - 1), None, ALU.min).then_inc(owner_ready.sem, 1)
            dve.wait_ge(owner_ready.sem, 1)
            dve.wait_ge(w_loaded.sem, 16 * (2 + 2 * EXPERTS))

            def bias(i, u):
                e = dve.value_load(owner_i[0:1, bass.ds(i, 1)], min_val=0, max_val=EXPERTS - 1)
                dve.wait_ge(h_done.sem, h_done.past(i))
                dve.tensor_tensor(gb[:, u, :], hg[:, u, :], b1[:, bass.ds(e, 1), HID:WIDE], ALU.add)
                dve.tensor_tensor(ab[:, u, :], ha[:, u, :], b1[:, bass.ds(e, 1), 0:HID], ALU.add).then_inc(biased.sem, 1)

            bias(0, 0)

            def body(i, pair, u, more):
                if more:
                    bias(i + 1, 1 - u)
                dve.wait_ge(sig_done.sem, sig_done.past(i))
                dve.tensor_tensor(hs[:, u, :], ab[:, u, :], gb[:, u, :], ALU.mult).then_inc(gated.sem, 1)
                e = dve.value_load(owner_i[0:1, bass.ds(i, 1)], min_val=0, max_val=EXPERTS - 1)
                dve.wait_ge(stored[u].sem, 16 * pair + 16)
                dve.wait_ge(y_done.sem, y_done.past(i))
                dve.tensor_tensor(yo[:, u, :], yp[:, 0:P], b2[:, bass.ds(e, 1), :], ALU.add).then_inc(y_kept.sem, 1)

            each_slot(dve, body)
            for q in range(4):
                dve.wait_ge(gathered[q].sem, 16 * 8)
                for c in (2 * q, 2 * q + 1):
                    xc = rows(core.x, c * CT, CT)
                    dve.scalar_tensor_tensor(xc.rearrange("p a b -> p (a b)"), rows(core.all_xn, c * CT, CT).rearrange("p a b -> p (a b)"),
                                             0.5, xc.rearrange("p a b -> p (a b)"), ALU.mult, ALU.add)
                    dve.drain()
                    new_sums_dve(dve, core, c)

        @block.scalar
        def _(act):
            ln_scales_act(act, core, s)
            each_pair(act, 0, CHUNKS, lambda c, u: ln_act(act, core, s, c, u))

            def keep_xst(i, u):
                act.wait_ge(xt_done.sem, xt_done.past(i))
                act.activation(xst[:, u, :], xt, ACT.Copy).then_inc(xst_kept.sem, 1)

            def gate(i, u):
                act.wait_ge(biased.sem, biased.past(i))
                act.activation(gb[:, u, :], gb[:, u, :], ACT.Sigmoid).then_inc(sig_done.sem, 1)

            keep_xst(0, 0)
            gate(0, 0)

            def body(i, pair, u, more):
                if more:
                    keep_xst(i + 1, 1 - u)
                    gate(i + 1, 1 - u)
                act.wait_ge(ht_done.sem, ht_done.past(i))
                act.activation(ht[:, u, :, :], htp[:, u, :, :], ACT.Copy).then_inc(ht_kept.sem, 1)

            each_slot(act, body)

        @block.tensor
        def _(pe):
            ln_pe(pe, core, s, 0, 0)
            pe.wait_ge(router_loaded.sem, 32)

            def route(c, u, more=True):
                if more:
                    ln_pe(pe, core, s, c + 1, 1 - u)
                pe.wait_ge(s.xnt_ready.sem, s.xnt_ready.past(c))
                pe.wait_ge(logits_kept.sem, logits_kept.past(c - 1))
                for j in range(CT):
                    last = pe.matmul(yp[:, j * EXPERTS:(j + 1) * EXPERTS], core.xnt[:, u, j * P:(j + 1) * P], wr[:, :],
                                     start=True, stop=True)
                last.then_inc(routed.sem, 1)

            each_pair(pe, 0, CHUNKS - 2, route)
            route(CHUNKS - 2, 0)
            route(CHUNKS - 1, 1, False)
            pe.wait_ge(filled.sem, 1)
            pe.wait_ge(hot_ready.sem, 1)
            hot_flat = hot[:, :, :].rearrange("p t e -> p (t e)")
            pe.matmul(ha[:, 0, 0:TILES * EXPERTS], earlier[:, :], hot_flat, start=True, stop=True)
            pe.matmul(hg[:, 0, 0:TILES * EXPERTS], ones[:, :], hot_flat, start=True, stop=True).then_inc(counted.sem, 1)
            pe.wait_ge(owner_ready.sem, 1)
            pe.wait_ge(w_loaded.sem, 16 * (2 + 2 * EXPERTS))

            def up(i, pair, u):
                pe.wait_ge(xs_loaded[u].sem, 16 * pair + 16)
                pe.wait_ge(xst_kept.sem, xst_kept.past(i - 1))
                pe.transpose(xt, xs[:, u, :], core.ident[:, :]).then_inc(xt_done.sem, 1)
                e = pe.value_load(owner_i[0:1, bass.ds(i, 1)], min_val=0, max_val=EXPERTS - 1)
                pe.wait_ge(xst_kept.sem, xst_kept.past(i))
                pe.wait_ge(biased.sem, biased.past(i - 2))
                pe.matmul(hg[:, u, :], xst[:, u, :], w1[:, bass.ds(e, 1), HID:WIDE], start=True, stop=True)
                pe.matmul(ha[:, u, :], xst[:, u, :], w1[:, bass.ds(e, 1), 0:HID], start=True, stop=True).then_inc(h_done.sem, 1)

            up(0, 0, 0)

            def body(i, pair, u, more):
                if more:
                    up(i + 1, pair + u, 1 - u)
                pe.wait_ge(gated.sem, gated.past(i))
                pe.wait_ge(ht_kept.sem, ht_kept.past(i - 2))
                for f in range(HB):
                    last = pe.transpose(htp[:, u, f, :], hs[:, u, f * P:(f + 1) * P], core.ident[:, :])
                last.then_inc(ht_done.sem, 1)
                e = pe.value_load(owner_i[0:1, bass.ds(i, 1)], min_val=0, max_val=EXPERTS - 1)
                pe.wait_ge(ht_kept.sem, ht_kept.past(i))
                pe.wait_ge(y_kept.sem, y_kept.past(i - 1))
                for f in range(HB):
                    last = pe.matmul(yp[:, 0:P], ht[:, u, f, :], w2[:, bass.ds(e, 1), f, :], start=f == 0, stop=f == HB - 1)
                last.then_inc(y_done.sem, 1)

            each_slot(pe, body)



def l0_attn(core):
    nc, w = core.nc, core.w
    NT = N // P
    with stage(nc) as s:
        ln_signals(s, 1)
        head_masks(core, s)
        wm = {m: s.sb(f"w_{m}", [P, P]) for m in ("wq", "wk", "wv", "wo")}
        bq, bk = s.sb("bq", [P, 1]), s.sb("bk", [P, 1])
        bv, bo = s.sb("bv", [P, P]), s.sb("bo", [P, P])
        causal = s.sb("causal", [P, P])
        block_mask = s.sb("block_mask", [P, HEADS, HW])
        low = s.sb("low", [P, 2, CW])
        kt = s.sb("kt", [P, CW])
        qt = s.sb("qt", [P, 2, CW])
        kg = s.sb("kg", [P, 2, GROUPS, CW])
        qj = s.sb("qj", [P, 2, GROUPS, CW])
        kn = s.sb("kn", [P, 2, CT, P])
        v1 = s.sb("v1", [P, 2, CT, HEADS, HW])
        att = s.sb("att", [P, NT, HEADS, P])
        state = s.sb("state", [P, HEADS, HW])
        den = s.sb("den", [P, NT, HEADS])
        o = s.sb("o", [P, NT, P])
        ot = s.sb("ot", [P, NT, P])
        pj = s.ps("pj", [P, 2, CW])
        sc = s.ps("sc", [P, 2, GROUPS, P])
        ob = [s.ps(f"ob{i}", [P, NT, HEADS, HW]) for i in range(2)]
        mb = s.ps("mb", [P, 2, NT * P])
        w_loaded = s.sig("w_loaded")
        filled = s.sig("filled")
        cleared = s.sig("cleared")
        projected = s.sig("projected")
        low_ready = s.sig("low_ready")
        low_exp = s.sig("low_exp")
        feature_ready = s.sig("feature_ready")
        split_done = s.sig("split_done")
        v_kept = s.sig("v_kept", 1)
        kn_kept = s.sig("kn_kept", 1)
        state_done = s.sig("state_done")
        state_kept = s.sig("state_kept")
        sc_done = s.sig("sc_done")
        att_ready = s.sig("att_ready", 2)
        av_done = s.sig("av_done")
        o_ready = s.sig("o_ready", 2)
        o_turned = s.sig("o_turned")
        ot_kept = s.sig("ot_kept")
        y_done = s.sig("y_done")
        x_added = s.sig("x_added", 1)
        s.ready()
        block = s.ctx.enter_context(nc.Block())

        @block.sync
        def _(sp):
            for m, t in wm.items():
                sp.dma_start(t[:, :], w[f"L0_attn_{m}"]).then_inc(w_loaded.sem, 16)
            for t, m in ((bq, "bq"), (bk, "bk")):
                sp.dma_start(t[:, :], w[f"L0_attn_{m}"].rearrange("(p a) -> p a", a=1)).then_inc(w_loaded.sem, 16)
            for t, m in ((bv, "bv"), (bo, "bo")):
                sp.dma_start(t[:, :], w[f"L0_attn_{m}"].partition_broadcast(P)).then_inc(w_loaded.sem, 16)

        @block.gpsimd
        def _(pool):
            head_masks_pool(pool, s)
            pool.memset(causal[:, :], 1.0).then_inc(cleared.sem, 1)
            pool.memset(block_mask[:, :, :], 1.0).then_inc(cleared.sem, 1)
            pool.wait_ge(cleared.sem, 2)
            pool.affine_select(out=causal[:, :], in_=causal[:, :], compare_op=ALU.is_ge, fill=0.0,
                               base=0, pattern=[[1, P]], channel_multiplier=-1).then_inc(filled.sem, 1)
            pool.affine_select(out=block_mask[:, :, :], in_=block_mask[:, :, :], compare_op=ALU.is_ge, fill=0.0,
                               base=0, pattern=[[-DH, HEADS], [0, HW]], channel_multiplier=1).then_inc(cleared.sem, 1)
            pool.wait_ge(cleared.sem, 3)
            pool.affine_select(out=block_mask[:, :, :], in_=block_mask[:, :, :], compare_op=ALU.is_ge, fill=0.0,
                               base=DH - 1, pattern=[[DH, HEADS], [0, HW]], channel_multiplier=-1).then_inc(filled.sem, 1)
            pool.memset(v1[:, :, :, :, DH:HW], 1.0).then_inc(filled.sem, 1)

        @block.vector
        def _(dve):
            def features(c, u):
                for n, (bias, t) in enumerate(((bk, kt[:, :]), (bq, qt[:, u, :]))):
                    dve.wait_ge(projected.sem, projected.past(4 * c + n))
                    dve.tensor_scalar(low[:, n, :], pj[:, n, :], bias[:, :], 0.0, ALU.add, ALU.min).then_inc(low_ready.sem, 1)
                    dve.tensor_scalar(t, pj[:, n, :], bias[:, :], 0.0, ALU.add, ALU.max)
                    dve.drain()
                    dve.wait_ge(low_exp.sem, low_exp.past(2 * c + n))
                    dve.tensor_tensor(t, t, low[:, n, :], ALU.add).then_inc(feature_ready.sem, 1)
                dve.wait_ge(projected.sem, projected.past(4 * c + 2))
                for j in range(CT):
                    last = dve.tensor_tensor(v1[:, u, j, :, 0:DH], pj[:, 0, j * P:(j + 1) * P].rearrange("p (h e) -> p h e", h=HEADS),
                                             bv[:, :].rearrange("p (h e) -> p h e", h=HEADS), ALU.add)
                last.then_inc(v_kept.sem, 1)

            def mask_scores(c, i, t):
                for g in range(GROUPS):
                    n = 16 * c + (NT * i + t) * GROUPS + g
                    dve.wait_ge(sc_done.sem, sc_done.past(n))
                    dve.tensor_tensor(att[:, t, g * GROUPS:(g + 1) * GROUPS, :], sc[:, g % 2, :, :],
                                      causal[:, :].unsqueeze(1).to_broadcast([P, GROUPS, P]), ALU.mult).then_inc(att_ready.sem, 1)

            def keep_state(c, i):
                dve.wait_ge(state_done.sem, state_done.past(2 * c + i))
                dve.tensor_tensor(state[:, :, :], mb[:, 0, 0:HEADS * HW].rearrange("p (h e) -> p h e", h=HEADS),
                                  block_mask[:, :, :], ALU.mult).then_inc(state_kept.sem, 1)

            def normalise(c, i):
                dve.wait_ge(av_done.sem, av_done.past(2 * c + i))
                dve.tensor_scalar(den[:, :, :], ob[i][:, :, :, DH], 1e-6, None, ALU.add)
                dve.drain()
                dve.reciprocal(den[:, :, :], den[:, :, :])
                dve.drain()
                for t in range(NT):
                    last = dve.tensor_tensor(o[:, t, :].rearrange("p (h e) -> p h e", h=HEADS), ob[i][:, t, :, 0:DH],
                                             den[:, t, :].unsqueeze(2).to_broadcast([P, HEADS, DH]), ALU.mult)
                last.then_inc(o_ready.sem, 1)

            def add(c, i):
                xs = rows(core.x, c * CT + i * NT, NT)
                dve.tensor_tensor(xs, xs, bo[:, :].unsqueeze(1).to_broadcast([P, NT, P]), ALU.add)
                dve.drain()
                dve.wait_ge(y_done.sem, y_done.past(2 * c + i))
                dve.tensor_tensor(xs, xs, mb[:, 1, :].rearrange("p (t e) -> p t e", t=NT), ALU.add).then_inc(x_added.sem, 1)
                dve.drain()
                new_sums_dve(dve, core, c, range(i * NT, i * NT + NT))

            head_masks_dve(dve, s)
            ln_scales_dve(dve, core, s)
            ln_dve(dve, core, s, 0, 0)
            dve.wait_ge(w_loaded.sem, 128)
            features(0, 0)
            dve.wait_ge(filled.sem, filled.past(2))

            def body(c, u, more=True):
                if more:
                    ln_dve(dve, core, s, c + 1, 1 - u)
                mask_scores(c, 0, 0)
                keep_state(c, 0)
                mask_scores(c, 0, 1)
                normalise(c, 0)
                if more:
                    features(c + 1, 1 - u)
                keep_state(c, 1)
                mask_scores(c, 1, 0)
                add(c, 0)
                mask_scores(c, 1, 1)
                normalise(c, 1)
                add(c, 1)

            each_pair(dve, 0, CHUNKS - 2, body)
            body(CHUNKS - 2, 0)
            body(CHUNKS - 1, 1, False)

        @block.scalar
        def _(act):
            def split(c, u):
                for n in range(2):
                    act.wait_ge(low_ready.sem, low_ready.past(2 * c + n))
                    act.activation(low[:, n, :], low[:, n, :], ACT.Exp).then_inc(low_exp.sem, 1)
                for n, (t, to, mask) in enumerate(((kt[:, :], kg, s.group), (qt[:, u, :], qj, s.place))):
                    act.wait_ge(feature_ready.sem, feature_ready.past(2 * c + n))
                    for g in range(GROUPS):
                        last = act.activation(to[:, u, g, :], t, ACT.Copy, scale=mask[:, g:g + 1])
                    last.then_inc(split_done.sem, 1)

            def keep_kn(c, u):
                act.wait_ge(projected.sem, projected.past(4 * c + 3))
                act.activation(kn[:, u, :, :], pj[:, 1, :].rearrange("p (t e) -> p t e", t=CT), ACT.Copy).then_inc(kn_kept.sem, 1)

            def keep_ot(c, i):
                act.wait_ge(o_turned.sem, o_turned.past(2 * c + i))
                act.activation(ot[:, :, :], mb[:, 0, :].rearrange("p (t e) -> p t e", t=NT), ACT.Copy).then_inc(ot_kept.sem, 1)

            ln_scales_act(act, core, s)
            ln_act(act, core, s, 0, 0)
            act.wait_ge(s.head_step.sem, MASKS_READY)
            split(0, 0)
            keep_kn(0, 0)

            def body(c, u, more=True):
                if more:
                    ln_act(act, core, s, c + 1, 1 - u)
                    split(c + 1, 1 - u)
                keep_ot(c, 0)
                if more:
                    keep_kn(c + 1, 1 - u)
                keep_ot(c, 1)

            each_pair(act, 0, CHUNKS - 2, body)
            body(CHUNKS - 2, 0)
            body(CHUNKS - 1, 1, False)

        @block.tensor
        def _(pe):
            def project(c, u):
                pe.wait_ge(s.xnt_ready.sem, s.xnt_ready.past(c))
                pe.wait_ge(v_kept.sem, v_kept.past(c - 1))
                pe.matmul(pj[:, 0, :], wm["wk"][:, :], core.xnt[:, u, :], start=True, stop=True).then_inc(projected.sem, 1)
                pe.wait_ge(kn_kept.sem, kn_kept.past(c - 1))
                pe.matmul(pj[:, 1, :], wm["wq"][:, :], core.xnt[:, u, :], start=True, stop=True).then_inc(projected.sem, 1)
                pe.wait_ge(feature_ready.sem, feature_ready.past(2 * c))
                for j in range(CT):
                    last = pe.matmul(pj[:, 0, j * P:(j + 1) * P], core.xnt[:, u, j * P:(j + 1) * P], wm["wv"][:, :],
                                     start=True, stop=True)
                last.then_inc(projected.sem, 1)

            def turn_k(c):
                pe.wait_ge(feature_ready.sem, feature_ready.past(2 * c + 1))
                for j in range(CT):
                    last = pe.transpose(pj[:, 1, j * P:(j + 1) * P], kt[:, j * P:(j + 1) * P], core.ident[:, :])
                last.then_inc(projected.sem, 1)

            def scores(c, u, i, t):
                j = NT * i + t
                pe.wait_ge(split_done.sem, split_done.past(2 * c + 1))
                for g in range(GROUPS):
                    n = 16 * c + j * GROUPS + g
                    pe.wait_ge(att_ready.sem, att_ready.past(n - 2))
                    pe.matmul(sc[:, g % 2, :, :], kg[:, u, g, j * P:(j + 1) * P], qj[:, u, :, j * P:(j + 1) * P],
                              start=True, stop=True).then_inc(sc_done.sem, 1)

            def first_state(c, u, i):
                pe.wait_ge(kn_kept.sem, kn_kept.past(c))
                pe.wait_ge(v_kept.sem, v_kept.past(c))
                pe.wait_ge(x_added.sem, x_added.past(2 * c - 1))
                if i == 1:
                    pe.wait_ge(state_kept.sem, state_kept.past(2 * c))
                pe.matmul(mb[:, 0, 0:HEADS * HW], kn[:, u, NT * i, :], v1[:, u, NT * i, :, :].rearrange("p h e -> p (h e)"),
                          start=True, stop=True).then_inc(state_done.sem, 1)

            def values(c, u, i):
                pe.wait_ge(o_ready.sem, o_ready.past(2 * c + i - 2))
                for t in range(NT):
                    j = NT * i + t
                    pe.wait_ge(att_ready.sem, att_ready.past(16 * c + j * GROUPS + 3))
                    if t:
                        pe.wait_ge(state_kept.sem, state_kept.past(2 * c + i))
                        pe.matmul(ob[i][:, t, :, :].rearrange("p h e -> p (h e)"), qt[:, u, j * P:(j + 1) * P],
                                  state[:, :, :].rearrange("p h e -> p (h e)"), start=True, stop=False, skip_group_check=True)
                    for h in range(HEADS):
                        last = pe.matmul(ob[i][:, t, h, :], att[:, t, h, :], v1[:, u, j, h, :],
                                         start=not t, stop=True, skip_group_check=bool(t))
                last.then_inc(av_done.sem, 1)

            def out_product(c, i):
                n = 2 * c + i
                pe.wait_ge(o_ready.sem, o_ready.past(n))
                pe.wait_ge(state_kept.sem, state_kept.past(2 * c + 1))
                pe.wait_ge(x_added.sem, x_added.past(n - 1))
                for t in range(NT):
                    last = pe.transpose(mb[:, 0, t * P:(t + 1) * P], o[:, t, :], core.ident[:, :])
                last.then_inc(o_turned.sem, 1)
                pe.wait_ge(ot_kept.sem, ot_kept.past(n))
                for t in range(NT):
                    last = pe.matmul(mb[:, 1, t * P:(t + 1) * P], ot[:, t, :], wm["wo"][:, :], start=True, stop=True)
                last.then_inc(y_done.sem, 1)

            ln_pe(pe, core, s, 0, 0)
            pe.wait_ge(w_loaded.sem, 128)
            project(0, 0)
            turn_k(0)
            pe.wait_ge(filled.sem, filled.past(2))

            def body(c, u, more=True):
                scores(c, u, 0, 0)
                first_state(c, u, 0)
                scores(c, u, 0, 1)
                values(c, u, 0)
                if more:
                    ln_pe(pe, core, s, c + 1, 1 - u)
                    project(c + 1, 1 - u)
                first_state(c, u, 1)
                scores(c, u, 1, 0)
                out_product(c, 0)
                scores(c, u, 1, 1)
                values(c, u, 1)
                if more:
                    turn_k(c + 1)
                out_product(c, 1)

            each_pair(pe, 0, CHUNKS - 2, body)
            body(CHUNKS - 2, 0)
            body(CHUNKS - 1, 1, False)



def l1_ffn(core):
    nc, w = core.nc, core.w
    EXPERTS, _, F = w["L1_ffn_w_gate"].shape
    CAP = 64
    PAIRS = EXPERTS // 2
    TOP = 8
    RING = 4
    HALF = TILES // 2
    ROUNDS = CAP // TOP
    LOW = -3.0e38
    with stage(nc) as s:
        ln_signals(s, 1)
        wr_raw = s.sb("wr_raw", [EXPERTS, D])
        wr = s.sb("wr", [P, EXPERTS])
        wsgu = s.sb("wsgu", [P, 2 * F])
        wsd = s.sb("wsd", [F, P])
        tok_i = s.sb("tok_i", [P, TILES], mybir.dt.int32)
        order = s.sb("order", [P, TILES])
        part_i = s.sb("part_i", [P, 1], mybir.dt.int32)
        part = s.sb("part", [P, 1])
        upper = s.sb("upper", [P, 1])
        slot = s.sb("slot", [P, 1])
        region = s.sb("region", [P, 1])
        zero = s.sb("zero", [P, CT, 2 * D])
        lr = s.sb("lr", [P, CT, EXPERTS])
        top = s.sb("top", [P, CT, TOP])
        rest = s.sb("rest", [P, CT, EXPERTS])
        wts = s.sb("wts", [P, TILES, EXPERTS])
        mask = s.sb("mask", [P, TILES, EXPERTS])
        keys = s.sb("keys", [P, HALF, 2, EXPERTS])
        wsum = s.sb("wsum", [P, TILES])
        sg = s.sb("sg", [F, CW])
        hsh = s.sb("hsh", [F, CW])
        keyt = s.sb("keyt", [P, HALF * P])
        found = s.sb("found", [P, CAP])
        both = s.sb("both", [EXPERTS, 2 * CAP])
        firsts = s.sb("firsts", [EXPERTS, 3 * CAP])
        token = s.sb("token", [P, PAIRS])
        empty = s.sb("empty", [P, PAIRS])
        from_i = s.sb("from_i", [P, PAIRS], U32)
        to_i = s.sb("to_i", [P, PAIRS], U32)
        wg = s.sb("wg", [P, RING, 2, F])
        wu = s.sb("wu", [P, RING, 2, F])
        wd = s.sb("wd", [F, RING, 2, P])
        xg = s.sb("xg", [P, RING, D + EXPERTS])
        xgt = s.sb("xgt", [P, 2, P])
        gs = s.sb("gs", [F, 2, P])
        hp = s.sb("hp", [F, 2, 2 * P])
        yo = s.sb("yo", [P, RING, D])
        acc_b = s.sb("acc_b", [P, TILES, D])
        gu = s.ps("gu", [P, 2, CW])
        ly = s.ps("ly", [P, 2, CW])
        kt = s.ps("kt", [P, 2, CW])
        lg, ysh = ly[:, 0, 0:CT * EXPERTS], ly[:, 1, :]
        w_loaded = s.sig("w_loaded")
        filled = s.sig("filled")
        hp_clear = s.sig("hp_clear")
        zeroed = s.sig("zeroed")
        wr_turned = s.sig("wr_turned")
        wr_kept = s.sig("wr_kept")
        copied = s.sig("copied", 2)
        routed = s.sig("routed")
        logits_kept = s.sig("logits_kept", 1)
        shared_up = s.sig("shared_up")
        silu_done = s.sig("silu_done", 1)
        shared_h = s.sig("shared_h", 1)
        shared_y = s.sig("shared_y")
        shared_added = s.sig("shared_added", 1)
        chosen = s.sig("chosen")
        exp_done = s.sig("exp_done")
        keys_turned = s.sig("keys_turned")
        keys_kept = s.sig("keys_kept", 2)
        weighted = s.sig("weighted")
        found_ready = s.sig("found_ready")
        moved = s.sig("moved")
        firsts_ready = s.sig("firsts_ready")
        listed = s.sig("listed")
        index_ready = s.sig("index_ready")
        rows_stored = s.sig("rows_stored")
        ring_loaded = [s.sig(f"ring_loaded{q}") for q in range(RING)]
        added, *xg_loaded = s.pool_dmas(core)[0:1 + RING]
        xt_done = s.sig("xt_done")
        xt_kept = s.sig("xt_kept", 1)
        gu_done = s.sig("gu_done")
        gated = s.sig("gated", 2)
        h_done = s.sig("h_done", 2)
        y_done = s.sig("y_done")
        y_kept = s.sig("y_kept", 2)
        acc_loaded = [s.sig(f"acc_loaded{q}") for q in range(4)]
        s.ready()
        table, sums = core.table_dram, core.acc_dram
        ROWS = TOKENS + CAP
        block = s.ctx.enter_context(nc.Block())

        @block.sync
        def _(sp):
            for t, m in ((wr_raw, "router_w"), (wsgu, "ws_gate_up"), (wsd, "ws_down")):
                sp.dma_start(t[:, :], w[f"L1_ffn_{m}"]).then_inc(w_loaded.sem, 16)

            def load(n, q):
                for t, m in ((wg, "w_gate"), (wu, "w_up"), (wd, "w_down")):
                    sp.dma_start(t[:, q, :, :], w[f"L1_ffn_{m}"].rearrange("(b n) i o -> n i b o", b=2)[bass.ds(n, 1)].rearrange("n i b o -> i (n b) o")).then_inc(ring_loaded[q].sem, 16)

            for q in range(RING):
                load(q, q)
            sp.wait_ge(filled.sem, 3)
            zrows = zero[:, :, :].rearrange("p a (b d) -> p (a b) d", d=D)
            for n in range(2 * ROWS // P // 8):
                sp.dma_start(sums[n * 8 * P:(n + 1) * 8 * P, :].rearrange("(a p) d -> p a d", p=P), zrows).then_inc(zeroed.sem, 16)
            sp.dma_start(sums[2 * ROWS - P:2 * ROWS, :], zrows[:, 0, :]).then_inc(zeroed.sem, 16)
            sp.dma_start(table[TOKENS:ROWS, :], zero[0:CAP, 0, 0:D + EXPERTS]).then_inc(zeroed.sem, 16)
            sp.wait_ge(copied.sem, copied.past(CHUNKS - 1))
            sp.dma_start(table[0:TOKENS, 0:D].rearrange("(t p) d -> p t d", p=P), core.all_xn[:, :, :]).then_inc(rows_stored.sem, 16)
            sp.wait_ge(weighted.sem, 1)
            with nc.allow_non_contiguous_dma("the weights of a token stand by its row"):
                sp.dma_start(table[0:TOKENS, D:D + EXPERTS].rearrange("(t p) d -> p t d", p=P), wts[:, :, :]).then_inc(rows_stored.sem, 16)

            with sp.Fori(0, PAIRS // RING - 1) as ring:
                for q in range(RING):
                    sp.wait_ge(y_done.sem, y_done.past(ring * RING + q))
                    load(ring * RING + q + RING, q)
            sp.wait_ge(added.sem, 16 * PAIRS)
            for q in range(4):
                for b, t in ((0, core.all_xn), (1, acc_b)):
                    sp.dma_start(t[:, q * 8:(q + 1) * 8, :],
                                 sums[b * ROWS + q * 8 * P:b * ROWS + (q + 1) * 8 * P, :].rearrange("(t p) d -> p t d", p=P)).then_inc(acc_loaded[q].sem, 16)

        @block.gpsimd
        def _(pool):
            pool.memset(zero[:, :, :], 0.0).then_inc(filled.sem, 1)
            pool.iota(tok_i[:, :], pattern=[[-P, TILES]], base=TOKENS, channel_multiplier=-1).then_inc(filled.sem, 1)
            pool.iota(part_i[:, :], pattern=[[0, 1]], base=0, channel_multiplier=1).then_inc(filled.sem, 1)
            pool.memset(hp[:, :, :], 0.0).then_inc(hp_clear.sem, 1)

            def copy(c, u):
                pool.wait_ge(s.xn_ready.sem, s.xn_ready.past(c))
                pool.tensor_copy(rows(core.all_xn, c * CT, CT), core.xn[:, u, :, :]).then_inc(copied.sem, 1)

            each_pair(pool, 0, CHUNKS, copy)
            pool.wait_ge(index_ready.sem, 1)
            pool.wait_ge(rows_stored.sem, 32)
            pool.wait_ge(zeroed.sem, 16 * (2 * ROWS // P // 8 + 2))

            def gather(n):
                if n >= RING:
                    pool.wait_ge(y_kept.sem, y_kept.past(n - RING))
                pool.indirect_dma_start(xg[:, n % RING, :], None, table,
                                        bass.IndirectOffsetOnAxis(ap=from_i[:, n:n + 1], axis=0)).then_inc(xg_loaded[n % RING].sem, 16)

            for n in range(RING):
                gather(n)
            for n in range(PAIRS):
                pool.wait_ge(y_kept.sem, y_kept.past(n))
                if n + RING < PAIRS:
                    gather(n + RING)
                if n > 0:
                    pool.wait_ge(added.sem, 16 * n)
                pool.indirect_dma_start(sums, bass.IndirectOffsetOnAxis(ap=to_i[:, n:n + 1], axis=0),
                                        yo[:, n % RING, :], None, compute_op=ALU.add).then_inc(added.sem, 16)
            for q in range(RING):
                pool.wait_ge(xg_loaded[q].sem, 16 * (PAIRS // RING))
            pool.wait_ge(added.sem, 16 * PAIRS)
            s.reset_pool_dmas(pool)

        @block.vector
        def _(dve):
            ln_scales_dve(dve, core, s)
            ln_dve(dve, core, s, 0, 0, copied)
            dve.wait_ge(filled.sem, 3)
            dve.tensor_copy(order[:, :], tok_i[:, :])
            dve.tensor_copy(part[:, :], part_i[:, :])
            dve.drain()
            dve.tensor_scalar(upper[:, :], part[:, :], float(CAP), None, ALU.is_ge)
            dve.drain()
            dve.scalar_tensor_tensor(slot[:, :], upper[:, :], -float(CAP), part[:, :], ALU.mult, ALU.add)
            dve.tensor_scalar(region[:, :], upper[:, :], float(ROWS), None, ALU.mult)

            def route(c, u, half, more=True):
                if more:
                    ln_dve(dve, core, s, c + 1, 1 - u, copied)
                dve.wait_ge(routed.sem, routed.past(c))
                dve.tensor_copy(lr[:, :, :], lg.rearrange("p (t e) -> p t e", e=EXPERTS)).then_inc(logits_kept.sem, 1)
                dve.drain()
                for j in range(CT):
                    dve.max(top[:, j, :], lr[:, j, :])
                dve.drain()
                for j in range(CT):
                    dve.match_replace(rest[:, j, :], top[:, j, :], lr[:, j, :], LOW)
                dve.tensor_tensor(rows(wts, c * CT, CT), lr[:, :, :], top[:, :, 0:1].to_broadcast([P, CT, EXPERTS]), ALU.subtract)
                dve.drain()
                dve.tensor_tensor(rows(mask, c * CT, CT), rest[:, :, :], lr[:, :, :], ALU.not_equal)
                dve.drain()
                dve.wait_ge(silu_done.sem, silu_done.past(c))
                dve.tensor_tensor(hsh[:, :], sg[:, :], gu[0:F, 1, :], ALU.mult).then_inc(shared_h.sem, 1)
                dve.tensor_tensor(keys[:, bass.ds(c * CT - half * HALF, CT), half, :], rows(mask, c * CT, CT),
                                  order[:, bass.ds(c * CT, CT)].unsqueeze(2).to_broadcast([P, CT, EXPERTS]), ALU.mult).then_inc(chosen.sem, 1)
                dve.wait_ge(shared_y.sem, shared_y.past(c))
                xc = rows(core.x, c * CT, CT).rearrange("p a b -> p (a b)")
                dve.scalar_tensor_tensor(xc, ysh, 0.5, xc, ALU.mult, ALU.add).then_inc(shared_added.sem, 1)

            each_pair(dve, 0, CHUNKS // 2, lambda c, u: route(c, u, 0))
            each_pair(dve, CHUNKS // 2, CHUNKS - 2, lambda c, u: route(c, u, 1))
            route(CHUNKS - 2, 0, 1)
            route(CHUNKS - 1, 1, 1, False)
            dve.drain()
            flat = lambda t: t[:, :, :].rearrange("p a b -> p (a b)")
            dve.wait_ge(exp_done.sem, 1)
            dve.tensor_tensor(flat(wts), flat(wts), flat(mask), ALU.mult)
            dve.drain()
            dve.tensor_reduce(wsum[:, :], wts[:, :, :], AX.X, ALU.add)
            dve.drain()
            dve.reciprocal(wsum[:, :], wsum[:, :])
            dve.drain()
            dve.tensor_tensor(wts[:, :, :], wts[:, :, :], wsum[:, :].unsqueeze(2).to_broadcast([P, TILES, EXPERTS]), ALU.mult).then_inc(weighted.sem, 1)
            dve.wait_ge(keys_kept.sem, keys_kept.past(3))
            for r in range(ROUNDS):
                dve.max(found[:, r * TOP:(r + 1) * TOP], keyt[:, :])
                dve.drain()
                if r < ROUNDS - 1:
                    dve.match_replace(keyt[:, :], found[:, r * TOP:(r + 1) * TOP], keyt[:, :], 0.0)
                    dve.drain()
            dve.memset(firsts[:, :], 0.0).then_inc(found_ready.sem, 1)
            dve.wait_ge(moved.sem, 1)
            dve.tensor_copy(both[:, :], kt[0:EXPERTS, 0, 0:2 * CAP])
            dve.drain()
            for r in range(ROUNDS):
                dve.max(firsts[:, CAP + r * TOP:CAP + (r + 1) * TOP], both[:, :])
                dve.drain()
                if r < ROUNDS - 1:
                    dve.match_replace(both[:, :], firsts[:, CAP + r * TOP:CAP + (r + 1) * TOP], both[:, :], 0.0)
                    dve.drain()
            dve.sem_inc(firsts_ready.sem, 1)
            dve.wait_ge(listed.sem, 1)
            dve.tensor_scalar(token[:, :], kt[:, 1, 0:PAIRS], -1.0, float(TOKENS), ALU.mult, ALU.add)
            dve.tensor_scalar(empty[:, :], kt[:, 1, 0:PAIRS], 0.0, slot[:, 0:1], ALU.is_equal, ALU.mult)
            dve.drain()
            dve.tensor_tensor(token[:, :], token[:, :], empty[:, :], ALU.add)
            dve.drain()
            dve.tensor_copy(from_i[:, :], token[:, :])
            dve.tensor_scalar(to_i[:, :], token[:, :], region[:, 0:1], None, ALU.add).then_inc(index_ready.sem, 1)
            dve.wait_ge(hp_clear.sem, 1)

            def gate(n, q):
                dve.wait_ge(gated.sem, gated.past(n))
                u = q % 2
                dve.tensor_tensor(hp[:, u, 0:CAP], gs[:, u, 0:CAP], gu[0:F, u, P:P + CAP], ALU.mult)
                dve.tensor_tensor(hp[:, u, P + CAP:2 * P], gs[:, u, CAP:P], gu[0:F, u, P + CAP:2 * P], ALU.mult).then_inc(h_done.sem, 1)

            def keep(n, q, reuse):
                dve.wait_ge(y_done.sem, y_done.past(n))
                if reuse:
                    dve.wait_ge(added.sem, (n - RING + 1) * 16)
                e = D + n
                dve.tensor_scalar(yo[0:CAP, q, :], ly[0:CAP, q % 2, 0:P], xg[0:CAP, q, bass.ds(e, 1)], None, ALU.mult)
                dve.tensor_scalar(yo[CAP:P, q, :], ly[CAP:P, q % 2, 0:P], xg[CAP:P, q, bass.ds(e + PAIRS, 1)], None, ALU.mult).then_inc(y_kept.sem, 1)

            def ring_body(n0, reuse, last=False):
                for q in range(RING):
                    if not (last and q == RING - 1):
                        gate(n0 + q + 1, (q + 1) % RING)
                    keep(n0 + q, q, reuse)

            gate(0, 0)
            ring_body(0, False)
            with dve.Fori(1, PAIRS // RING - 1) as ring:
                ring_body(ring * RING, True)
            ring_body(PAIRS - RING, True, True)
            for q in range(4):
                dve.wait_ge(acc_loaded[q].sem, 32)
                c8 = slice(q * 8, (q + 1) * 8)
                dve.tensor_tensor(acc_b[:, c8, :], acc_b[:, c8, :], core.all_xn[:, c8, :], ALU.add)
                dve.drain()
                dve.scalar_tensor_tensor(core.x[:, c8, :].rearrange("p a b -> p (a b)"), acc_b[:, c8, :].rearrange("p a b -> p (a b)"), 0.5,
                                         core.x[:, c8, :].rearrange("p a b -> p (a b)"), ALU.mult, ALU.add)
                dve.drain()
                for c in (2 * q, 2 * q + 1):
                    new_sums_dve(dve, core, c)

        @block.scalar
        def _(act):
            act.wait_ge(wr_turned.sem, 1)
            act.activation(wr[:, :], kt[:, 0, 0:EXPERTS], ACT.Copy).then_inc(wr_kept.sem, 1)
            ln_scales_act(act, core, s)
            ln_act(act, core, s, 0, 0)

            def body(c, u, more=True):
                if more:
                    ln_act(act, core, s, c + 1, 1 - u)
                act.wait_ge(shared_up.sem, shared_up.past(c))
                act.wait_ge(shared_h.sem, shared_h.past(c - 1))
                act.activation(sg[:, :], gu[0:F, 0, :], ACT.Silu).then_inc(silu_done.sem, 1)

            each_pair(act, 0, CHUNKS - 2, body)
            body(CHUNKS - 2, 0)
            body(CHUNKS - 1, 1, False)
            for g in range(4):
                act.wait_ge(keys_turned.sem, keys_turned.past(g))
                act.activation(keyt[:, g * CW:(g + 1) * CW], kt[:, g % 2, :], ACT.Copy).then_inc(keys_kept.sem, 1)
            act.wait_ge(chosen.sem, chosen.past(CHUNKS - 1))
            act.activation(wts[:, :, :], wts[:, :, :], ACT.Exp).then_inc(exp_done.sem, 1)

            def turn(n, q):
                act.wait_ge(xt_done.sem, xt_done.past(n))
                act.activation(xgt[:, q % 2, :], s.tp[:, 0, 0:P], ACT.Copy).then_inc(xt_kept.sem, 1)

            def gate(n, q):
                u = q % 2
                act.wait_ge(gu_done.sem, gu_done.past(n))
                act.wait_ge(h_done.sem, h_done.past(n - 2))
                act.activation(gs[:, u, :], gu[0:F, u, 0:P], ACT.Silu).then_inc(gated.sem, 1)

            turn(0, 0)

            def ring_body(n0, last=False):
                for q in range(RING):
                    if not (last and q == RING - 1):
                        turn(n0 + q + 1, q + 1)
                    gate(n0 + q, q)

            with act.Fori(0, PAIRS // RING - 1) as ring:
                ring_body(ring * RING)
            ring_body(PAIRS - RING, True)

        @block.tensor
        def _(pe):
            pe.wait_ge(w_loaded.sem, 48)
            pe.transpose(kt[:, 0, 0:EXPERTS], wr_raw[:, :], core.ident[0:EXPERTS, 0:EXPERTS]).then_inc(wr_turned.sem, 1)
            ln_pe(pe, core, s, 0, 0)
            pe.wait_ge(wr_kept.sem, 1)

            def body(c, u, more=True):
                if more:
                    ln_pe(pe, core, s, c + 1, 1 - u)
                pe.wait_ge(s.xnt_ready.sem, s.xnt_ready.past(c))
                pe.wait_ge(logits_kept.sem, logits_kept.past(c - 1))
                for j in range(CT):
                    last = pe.matmul(lg[:, j * EXPERTS:(j + 1) * EXPERTS], core.xnt[:, u, j * P:(j + 1) * P], wr[:, :],
                                     start=True, stop=True)
                last.then_inc(routed.sem, 1)
                pe.wait_ge(shared_h.sem, shared_h.past(c - 1))
                pe.matmul(gu[0:F, 0, :], wsgu[:, 0:F], core.xnt[:, u, :], start=True, stop=True)
                pe.matmul(gu[0:F, 1, :], wsgu[:, F:2 * F], core.xnt[:, u, :], start=True, stop=True).then_inc(shared_up.sem, 1)
                pe.wait_ge(shared_h.sem, shared_h.past(c))
                pe.wait_ge(shared_added.sem, shared_added.past(c - 1))
                for j in range(CT):
                    last = pe.matmul(ysh[:, j * P:(j + 1) * P], hsh[:, j * P:(j + 1) * P], wsd[:, :], start=True, stop=True)
                last.then_inc(shared_y.sem, 1)

            each_pair(pe, 0, CHUNKS - 2, body)
            body(CHUNKS - 2, 0)
            body(CHUNKS - 1, 1, False)
            pe.wait_ge(chosen.sem, chosen.past(CHUNKS - 1))
            for g in range(4):
                pe.wait_ge(keys_kept.sem, keys_kept.past(g - 2))
                for j in range(CT):
                    last = pe.transpose(kt[:, g % 2, j * P:(j + 1) * P], keys[:, g * CT + j, :, :].rearrange("p h e -> p (h e)"), core.ident[:, :])
                last.then_inc(keys_turned.sem, 1)
            pe.wait_ge(found_ready.sem, 1)
            pe.wait_ge(keys_kept.sem, keys_kept.past(3))
            for half in range(2):
                last = pe.matmul(kt[0:EXPERTS, 0, half * CAP:(half + 1) * CAP], core.ident[:, half * EXPERTS:(half + 1) * EXPERTS],
                                 found[:, :], start=True, stop=True)
            last.then_inc(moved.sem, 1)
            pe.wait_ge(firsts_ready.sem, 1)
            pe.matmul(kt[:, 1, 0:PAIRS], firsts[:, CAP:3 * CAP], core.ident[0:EXPERTS, 0:PAIRS], start=True, stop=False)
            pe.matmul(kt[:, 1, 0:PAIRS], firsts[:, 0:2 * CAP], core.ident[0:EXPERTS, PAIRS:2 * PAIRS], start=False, stop=True).then_inc(listed.sem, 1)
            pe.wait_ge(index_ready.sem, 1)

            def turn(n, ring, q):
                pe.wait_ge(xg_loaded[q].sem, ring * 16 + 16)
                pe.wait_ge(xt_kept.sem, xt_kept.past(n - 1))
                pe.transpose(s.tp[:, 0, 0:P], xg[:, q, 0:D], core.ident[:, :]).then_inc(xt_done.sem, 1)

            def up(n, ring, q):
                u = q % 2
                pe.wait_ge(ring_loaded[q].sem, ring * 48 + 48)
                pe.wait_ge(xt_kept.sem, xt_kept.past(n))
                pe.wait_ge(h_done.sem, h_done.past(n - 2))
                for b in range(2):
                    cols = xgt[:, u, b * CAP:(b + 1) * CAP]
                    pe.matmul(gu[0:F, u, b * CAP:(b + 1) * CAP], wg[:, q, b, :], cols, start=True, stop=True)
                    last = pe.matmul(gu[0:F, u, P + b * CAP:P + (b + 1) * CAP], wu[:, q, b, :], cols, start=True, stop=True)
                last.then_inc(gu_done.sem, 1)

            def down(n, q):
                u = q % 2
                pe.wait_ge(h_done.sem, h_done.past(n))
                pe.wait_ge(y_kept.sem, y_kept.past(n - 2))
                for b in range(2):
                    last = pe.matmul(ly[:, u, 0:P], hp[:, u, b * P:(b + 1) * P], wd[:, q, b, :], start=b == 0, stop=b == 1)
                last.then_inc(y_done.sem, 1)

            turn(0, 0, 0)
            up(0, 0, 0)
            turn(1, 0, 1)

            def ring_body(n0, ring, last=False):
                for q in range(RING):
                    if not (last and q == RING - 1):
                        up(n0 + q + 1, ring + (q + 1) // RING, (q + 1) % RING)
                    if not (last and q >= RING - 2):
                        turn(n0 + q + 2, ring + (q + 2) // RING, (q + 2) % RING)
                    down(n0 + q, q)

            with pe.Fori(0, PAIRS // RING - 1) as ring:
                ring_body(ring * RING, ring)
            ring_body(PAIRS - RING, PAIRS // RING - 1, True)



def l1_attn(core):
    nc, w = core.nc, core.w
    BATCHES = CW // N
    CTX_SCALE = 1.0 / (8.0 ** 0.5) / D
    with stage(nc) as s:
        ln_signals(s)
        wm = {m: s.sb(f"w_{m}", [P, P]) for m in ("Wq", "Wk", "Wv", "Wo")}
        bias = s.sb("bias", [P, P])
        ke = s.sb("ke", [P, BATCHES, N])
        qe = s.sb("qe", [P, CT, P])
        kn = s.sb("kn", [P, CT, P])
        qt = s.sb("qt", [P, CT, P])
        vs = s.sb("vs", [P, 2, CT, P])
        ctxt = s.sb("ctxt", [P, BATCHES, P])
        mix = s.sb("mix", [P, BATCHES, P])
        kmax = s.sb("kmax", [P, BATCHES])
        qmax = s.sb("qmax", [P, CT])
        ksum = s.sb("ksum", [P, 2, BATCHES])
        qsum = s.sb("qsum", [P, 2, CT])
        kp, qp, vp, ktp, qtp = (s.ps(n, [P, CT, P]) for n in ("kp", "qp", "vp", "ktp", "qtp"))
        cm = s.ps("cm", [P, 2, BATCHES, P])
        w_loaded = s.sig("w_loaded")
        projected = s.sig("projected")
        max_ready = s.sig("max_ready")
        exp_done = s.sig("exp_done", 2)
        turned = s.sig("turned")
        turn_kept = s.sig("turn_kept", 2)
        v_kept = s.sig("v_kept", 1)
        sums_inverted = s.sig("sums_inverted")
        ctx_done = s.sig("ctx_done")
        ctx_kept = s.sig("ctx_kept")
        mix_done = s.sig("mix_done")
        mix_kept = s.sig("mix_kept", 1)
        y_done = s.sig("y_done")
        x_added = s.sig("x_added", 1)
        s.ready()
        block = s.ctx.enter_context(nc.Block())

        @block.sync
        def _(sp):
            for m, t in wm.items():
                sp.dma_start(t[:, :], w[f"L1_attn_{m}"]).then_inc(w_loaded.sem, 16)
            sp.dma_start(bias[:, :], w["L1_attn_bo"].partition_broadcast(P)).then_inc(w_loaded.sem, 16)

        @block.vector
        def _(dve):
            def maxima(c, u):
                dve.wait_ge(projected.sem, projected.past(3 * c))
                dve.tensor_reduce(kmax[:, :], kp[:, :, :].rearrange("p (b t) n -> p b (t n)", b=BATCHES), AX.X, ALU.max,
                                  negate=True).then_inc(max_ready.sem, 1)
                dve.wait_ge(projected.sem, projected.past(3 * c + 1))
                dve.tensor_reduce(qmax[:, :], qp[:, :, :], AX.X, ALU.max, negate=True).then_inc(max_ready.sem, 1)
                dve.wait_ge(projected.sem, projected.past(3 * c + 2))
                dve.tensor_copy(vs[:, u, :, :], vp[:, :, :]).then_inc(v_kept.sem, 1)

            def invert(c, u):
                dve.wait_ge(exp_done.sem, exp_done.past(2 * c + 1))
                dve.reciprocal(ksum[:, u, :], ksum[:, u, :])
                dve.reciprocal(qsum[:, u, :], qsum[:, u, :])
                dve.drain()
                dve.tensor_scalar(ksum[:, u, :], ksum[:, u, :], CTX_SCALE, None, ALU.mult)

            ln_scales_dve(dve, core, s)
            ln_dve(dve, core, s, 0, 0)
            ln_dve(dve, core, s, 1, 1)
            maxima(0, 0)
            invert(0, 0)
            dve.wait_ge(w_loaded.sem, 80)

            def body(c, u, ahead=2):
                if ahead > 0:
                    maxima(c + 1, 1 - u)
                dve.wait_ge(ctx_done.sem, ctx_done.past(c))
                dve.tensor_copy(ctxt[:, :, :], cm[:, 0, :, :]).then_inc(ctx_kept.sem, 1)
                dve.wait_ge(mix_done.sem, mix_done.past(c))
                for b in range(BATCHES):
                    last = dve.tensor_scalar(mix[:, b, :], cm[:, 1, b, :], ksum[:, u, b:b + 1], None, ALU.mult)
                last.then_inc(mix_kept.sem, 1)
                if ahead > 0:
                    invert(c + 1, 1 - u)
                if ahead > 1:
                    ln_dve(dve, core, s, c + 2, u)
                xs = rows(core.x, c * CT, CT)
                dve.tensor_tensor(xs, xs, bias[:, :].unsqueeze(1).to_broadcast([P, CT, P]), ALU.add)
                dve.drain()
                dve.wait_ge(y_done.sem, y_done.past(c))
                for j in range(CT):
                    xj = core.x[:, bass.ds(c * CT + j, 1), :]
                    last = dve.scalar_tensor_tensor(xj, vp[:, j:j + 1, :], qsum[:, u, j:j + 1], xj, ALU.mult, ALU.add)
                last.then_inc(x_added.sem, 1)
                dve.drain()
                new_sums_dve(dve, core, c)

            each_pair(dve, 0, CHUNKS - 2, body)
            body(CHUNKS - 2, 0, 1)
            body(CHUNKS - 1, 1, 0)

        @block.scalar
        def _(act):
            def exps(c, u):
                act.wait_ge(max_ready.sem, max_ready.past(2 * c))
                kv = kp[:, :, :].rearrange("p (b t) n -> p b (t n)", b=BATCHES)
                for b in range(BATCHES):
                    last = act.activation(ke[:, b, :], kv[:, b, :], ACT.Exp, bias=kmax[:, b:b + 1],
                                          accum_out=ksum[:, u, b:b + 1])
                last.then_inc(exp_done.sem, 1)
                act.wait_ge(max_ready.sem, max_ready.past(2 * c + 1))
                for j in range(CT):
                    last = act.activation(qe[:, j, :], qp[:, j, :], ACT.Exp, bias=qmax[:, j:j + 1],
                                          accum_out=qsum[:, u, j:j + 1])
                last.then_inc(exp_done.sem, 1)

            ln_scales_act(act, core, s)
            ln_act(act, core, s, 0, 0)
            exps(0, 0)
            ln_act(act, core, s, 1, 1)

            def body(c, u, ahead=2):
                act.wait_ge(turned.sem, turned.past(2 * c))
                act.activation(kn[:, :, :], ktp[:, :, :], ACT.Copy).then_inc(turn_kept.sem, 1)
                act.wait_ge(turned.sem, turned.past(2 * c + 1))
                act.activation(qt[:, :, :], qtp[:, :, :], ACT.Copy).then_inc(turn_kept.sem, 1)
                if ahead > 0:
                    act.wait_ge(x_added.sem, x_added.past(c - 1))
                    exps(c + 1, 1 - u)
                if ahead > 1:
                    ln_act(act, core, s, c + 2, u)

            each_pair(act, 0, CHUNKS - 2, body)
            body(CHUNKS - 2, 0, 1)
            body(CHUNKS - 1, 1, 0)

        @block.tensor
        def _(pe):
            def project(c, u):
                pe.wait_ge(s.xnt_ready.sem, s.xnt_ready.past(c))
                pe.wait_ge(exp_done.sem, exp_done.past(2 * c - 2))
                pe.matmul(kp[:, :, :].rearrange("p t n -> p (t n)"), wm["Wk"][:, :], core.xnt[:, u, :],
                          start=True, stop=True).then_inc(projected.sem, 1)
                pe.wait_ge(exp_done.sem, exp_done.past(2 * c - 1))
                for j in range(CT):
                    last = pe.matmul(qp[:, j, :], core.xnt[:, u, j * P:(j + 1) * P], wm["Wq"][:, :],
                                     start=True, stop=True)
                last.then_inc(projected.sem, 1)
                pe.wait_ge(v_kept.sem, v_kept.past(c - 1))
                pe.wait_ge(x_added.sem, x_added.past(c - 2))
                for j in range(CT):
                    last = pe.matmul(vp[:, j, :], core.xnt[:, u, j * P:(j + 1) * P], wm["Wv"][:, :],
                                     start=True, stop=True)
                last.then_inc(projected.sem, 1)

            ln_pe(pe, core, s, 0, 0)
            pe.wait_ge(w_loaded.sem, 80)
            project(0, 0)
            ln_pe(pe, core, s, 1, 1)

            def body(c, u, ahead=2):
                pe.wait_ge(exp_done.sem, exp_done.past(2 * c))
                for j in range(CT):
                    last = pe.transpose(ktp[:, j, :], ke[:, :, :].rearrange("p b n -> p (b n)")[:, j * P:(j + 1) * P], core.ident[:, :])
                last.then_inc(turned.sem, 1)
                pe.wait_ge(exp_done.sem, exp_done.past(2 * c + 1))
                for j in range(CT):
                    last = pe.transpose(qtp[:, j, :], qe[:, j, :], core.ident[:, :])
                last.then_inc(turned.sem, 1)
                if ahead > 0:
                    project(c + 1, 1 - u)
                pe.wait_ge(turn_kept.sem, turn_kept.past(2 * c))
                pe.wait_ge(v_kept.sem, v_kept.past(c))
                pe.wait_ge(mix_kept.sem, mix_kept.past(c - 1))
                for b in range(BATCHES):
                    for t in range(N // P):
                        j = b * (N // P) + t
                        last = pe.matmul(cm[:, 0, b, :], vs[:, u, j, :], kn[:, j, :], start=t == 0, stop=t == N // P - 1)
                last.then_inc(ctx_done.sem, 1)
                pe.wait_ge(ctx_kept.sem, ctx_kept.past(c))
                for b in range(BATCHES):
                    last = pe.matmul(cm[:, 1, b, :], ctxt[:, b, :], wm["Wo"][:, :], start=True, stop=True)
                last.then_inc(mix_done.sem, 1)
                pe.wait_ge(mix_kept.sem, mix_kept.past(c))
                pe.wait_ge(turn_kept.sem, turn_kept.past(2 * c + 1))
                if ahead > 0:
                    pe.wait_ge(v_kept.sem, v_kept.past(c + 1))
                for j in range(CT):
                    last = pe.matmul(vp[:, j, :], qt[:, j, :], mix[:, j // (N // P), :], start=True, stop=True)
                last.then_inc(y_done.sem, 1)
                if ahead > 1:
                    ln_pe(pe, core, s, c + 2, u)

            each_pair(pe, 0, CHUNKS - 2, body)
            body(CHUNKS - 2, 0, 1)
            body(CHUNKS - 1, 1, 0)



def l2_ffn(core):
    nc, w = core.nc, core.w
    EXPERTS, S, _, _ = w["L2_ffn_W1"].shape
    K = D // S
    CAP = int(1.5 * TOKENS / EXPERTS)
    assert CAP == P
    TOP = 8
    RING = 4
    UP = 64
    HALF = TOKENS // 2
    LOW = -3.0e38
    with stage(nc) as s:
        ln_signals(s, 1)
        wr_raw = s.sb("wr_raw", [EXPERTS, D])
        wr = s.sb("wr", [P, P])
        b1_raw = s.sb("b1_raw", [EXPERTS, S * P])
        b1 = s.sb("b1", [P, S, EXPERTS])
        b2 = s.sb("b2", [P, EXPERTS, D])
        zero = s.sb("zero", [P, 8, D])
        own = s.sb("own", [P, S])
        lt = s.sb("lt", [P, HALF])
        vals = s.sb("vals", [P, CAP])
        poss = s.sb("poss", [P, CAP], U32)
        posf = s.sb("posf", [P, CAP])
        vals1 = s.sb("vals1", [EXPERTS, CAP])
        posf1 = s.sb("posf1", [EXPERTS, CAP])
        first = s.sb("first", [EXPERTS, CAP])
        big = s.sb("big", [EXPERTS, 1])
        esum = s.sb("esum", [EXPERTS, 1])
        prob = s.sb("prob", [EXPERTS, CAP])
        prob_s = s.sb("prob_s", [P, EXPERTS])
        from_i = s.sb("from_i", [P, EXPERTS], U32)
        to_i = s.sb("to_i", [P, EXPERTS], U32)
        w1 = s.sb("w1", [P, RING, S, P])
        w2 = s.sb("w2", [P, RING, S, K])
        w2b = s.sb("w2b", [P, RING, S, D])
        xg = s.sb("xg", [P, RING, D])
        xgt = s.sb("xgt", [P, 2, P])
        h = s.sb("h", [P, 2, S, P])
        yb = s.sb("yb", [P, 2, D])
        yo = s.sb("yo", [P, RING, D])
        acc_b = s.sb("acc_b", [P, TILES, D])
        lp = s.ps("lp", [P, 2, CW])
        hu = s.ps("hu", [P, 2, CW])
        yp = s.ps("yp", [P, 2, CW])
        w_loaded = s.sig("w_loaded")
        filled = s.sig("filled")
        zeroed = s.sig("zeroed")
        wr_turned = s.sig("wr_turned")
        wr_kept = s.sig("wr_kept")
        copied = s.sig("copied", 2)
        routed = s.sig("routed")
        logits_kept = s.sig("logits_kept", 2)
        best_found = s.sig("best_found")
        moved = s.sig("moved")
        merged = s.sig("merged")
        exp_done = s.sig("exp_done")
        listed = s.sig("listed")
        slots_turned = s.sig("slots_turned")
        index_ready = s.sig("index_ready")
        rows_stored = s.sig("rows_stored")
        ring_loaded = [s.sig(f"ring_loaded{q}") for q in range(RING)]
        dmas = s.pool_dmas(core)
        added, xg_loaded = dmas[0:2], dmas[2:2 + RING]
        w2_spread = s.sig("w2_spread")
        xt_done = s.sig("xt_done")
        xt_kept = s.sig("xt_kept", 1)
        h_done = s.sig("h_done")
        gelu_done = s.sig("gelu_done", 2)
        y_done = s.sig("y_done", RING)
        y_kept = s.sig("y_kept", 2)
        acc_loaded = [s.sig(f"acc_loaded{q}") for q in range(4)]
        s.ready()
        table, sums = core.rows_dram[0:TOKENS, :], core.acc_dram
        ROWS = TOKENS
        block = s.ctx.enter_context(nc.Block())

        @block.sync
        def _(sp):
            sp.dma_start(wr_raw[:, :], w["L2_ffn_Wr"]).then_inc(w_loaded.sem, 16)
            sp.dma_start(b1_raw[:, :], w["L2_ffn_b1"].rearrange("e s m -> e (s m)")).then_inc(w_loaded.sem, 16)

            def load(n, q):
                sp.dma_start(w1[:, q, :, :], w["L2_ffn_W1"][bass.ds(n, 1)].rearrange("n s d m -> d (n s) m")).then_inc(ring_loaded[q].sem, 16)
                sp.dma_start(w2[:, q, :, :].rearrange("p j k -> p (j k)"),
                             w["L2_ffn_W2"][bass.ds(n, 1)].rearrange("n s (a j) k -> (n s a) (j k)", j=S)).then_inc(ring_loaded[q].sem, 16)

            for q in range(RING):
                load(q, q)
            sp.dma_start(b2[:, :, :].rearrange("p e d -> p (e d)"),
                         w["L2_ffn_b2"].rearrange("e s k -> (e s k)").partition_broadcast(P)).then_inc(w_loaded.sem, 16)
            sp.wait_ge(filled.sem, 1)
            for n in range(2 * ROWS // P // 8):
                sp.dma_start(sums[n * 8 * P:(n + 1) * 8 * P, :].rearrange("(a p) d -> p a d", p=P), zero[:, :, :]).then_inc(zeroed.sem, 16)
            sp.wait_ge(copied.sem, copied.past(CHUNKS - 1))
            sp.dma_start(table.rearrange("(t p) d -> p t d", p=P), core.all_xn[:, :, :]).then_inc(rows_stored.sem, 16)
            sp.wait_ge(best_found.sem, 1)
            sp.dma_start(vals1[:, :], vals[UP:UP + EXPERTS, :]).then_inc(moved.sem, 16)
            sp.dma_start(posf1[:, :], posf[UP:UP + EXPERTS, :]).then_inc(moved.sem, 16)

            with sp.Fori(0, EXPERTS // RING - 1) as ring:
                for q in range(RING):
                    sp.wait_ge(y_done.sem, y_done.past(ring * RING + q))
                    load(ring * RING + q + RING, q)
            for q in range(2):
                sp.wait_ge(added[q].sem, 16 * EXPERTS // 2)
            for q in range(4):
                for b, t in ((0, core.all_xn), (1, acc_b)):
                    sp.dma_start(t[:, q * 8:(q + 1) * 8, :],
                                 sums[b * ROWS + q * 8 * P:b * ROWS + (q + 1) * 8 * P, :].rearrange("(t p) d -> p t d", p=P)).then_inc(acc_loaded[q].sem, 16)

        @block.gpsimd
        def _(pool):
            pool.memset(zero[:, :, :], 0.0).then_inc(filled.sem, 1)
            pool.memset(own[:, :], 1.0).then_inc(filled.sem, 1)
            pool.wait_ge(filled.sem, 2)
            pool.affine_select(out=own[:, :], in_=own[:, :], compare_op=ALU.is_ge, fill=0.0,
                               base=0, pattern=[[-K, S]], channel_multiplier=1).then_inc(filled.sem, 1)
            pool.wait_ge(filled.sem, 3)
            pool.affine_select(out=own[:, :], in_=own[:, :], compare_op=ALU.is_ge, fill=0.0,
                               base=K - 1, pattern=[[K, S]], channel_multiplier=-1).then_inc(filled.sem, 1)

            def copy(c, u):
                pool.wait_ge(s.xn_ready.sem, s.xn_ready.past(c))
                pool.tensor_copy(rows(core.all_xn, c * CT, CT), core.xn[:, u, :, :]).then_inc(copied.sem, 1)

            each_pair(pool, 0, CHUNKS, copy)
            pool.wait_ge(index_ready.sem, 1)
            pool.wait_ge(rows_stored.sem, 16)
            pool.wait_ge(zeroed.sem, 16 * (2 * ROWS // P // 8))

            def gather(n):
                if n >= RING:
                    pool.wait_ge(xt_done.sem, xt_done.past(n - RING))
                pool.indirect_dma_start(xg[:, n % RING, :], None, table,
                                        bass.IndirectOffsetOnAxis(ap=from_i[:, n:n + 1], axis=0)).then_inc(xg_loaded[n % RING].sem, 16)

            for n in range(RING):
                gather(n)
            for n in range(EXPERTS):
                if n + RING < EXPERTS:
                    gather(n + RING)
                pool.wait_ge(y_kept.sem, y_kept.past(n))
                q = n % 2
                if n > 1:
                    pool.wait_ge(added[q].sem, 16 * (n // 2))
                pool.indirect_dma_start(sums, bass.IndirectOffsetOnAxis(ap=to_i[:, n:n + 1], axis=0),
                                        yo[:, n % RING, :], None, compute_op=ALU.add).then_inc(added[q].sem, 16)
            for q in range(RING):
                pool.wait_ge(xg_loaded[q].sem, 16 * (EXPERTS // RING))
            for q in range(2):
                pool.wait_ge(added[q].sem, 16 * (EXPERTS // 2))
            s.reset_pool_dmas(pool)

        @block.vector
        def _(dve):
            ln_scales_dve(dve, core, s)
            ln_dve(dve, core, s, 0, 0, copied)
            dve.wait_ge(wr_kept.sem, 1)
            dve.memset(lt[32:64, :], LOW)
            dve.memset(lt[96:P, :], LOW).then_inc(wr_kept.sem, 1)

            def ln(c, u):
                ln_dve(dve, core, s, c + 1, 1 - u, copied)

            each_pair(dve, 0, CHUNKS - 2, ln)
            ln(CHUNKS - 2, 0)
            dve.wait_ge(logits_kept.sem, logits_kept.past(CHUNKS - 1))
            for r in range(CAP // TOP):
                got = vals[:, r * TOP:(r + 1) * TOP]
                dve.max(got, lt[:, :])
                dve.drain()
                dve.max_index(poss[:, r * TOP:(r + 1) * TOP], got, lt[:, :])
                if r < CAP // TOP - 1:
                    dve.match_replace(lt[:, :], got, lt[:, :], LOW)
                    dve.drain()
            dve.drain()
            dve.tensor_copy(posf[0:UP, :], poss[0:UP, :])
            dve.tensor_scalar(posf[UP:P, :], poss[UP:P, :], float(HALF), None, ALU.add).then_inc(best_found.sem, 1)
            dve.wait_ge(moved.sem, 32)
            v0, p0 = vals[0:EXPERTS, :], posf[0:EXPERTS, :]
            v1, p1 = vals1[:, ::-1], posf1[:, ::-1]
            dve.tensor_tensor(first[:, :], v0, v1, ALU.is_ge)
            dve.tensor_tensor(big[:, :], vals[0:EXPERTS, 0:1], vals1[:, 0:1], ALU.max)
            dve.tensor_tensor(prob[:, :], v0, v1, ALU.max)
            dve.tensor_tensor(p0, p0, p1, ALU.subtract)
            dve.drain()
            dve.tensor_tensor(p0, p0, first[:, :], ALU.mult)
            dve.tensor_scalar(big[:, :], big[:, :], -1.0, None, ALU.mult).then_inc(merged.sem, 1)
            dve.drain()
            dve.tensor_tensor(p0, p0, p1, ALU.add)
            dve.wait_ge(exp_done.sem, 1)
            dve.reciprocal(esum[:, :], esum[:, :])
            dve.drain()
            dve.tensor_scalar(prob[:, :], prob[:, :], esum[:, 0:1], None, ALU.mult).then_inc(listed.sem, 1)
            dve.wait_ge(slots_turned.sem, 1)
            dve.tensor_copy(from_i[:, :], lp[:, 0, 0:EXPERTS])
            dve.tensor_copy(to_i[:, ::2], lp[:, 0, 0:EXPERTS:2])
            dve.tensor_scalar(to_i[:, 1::2], lp[:, 0, 1:EXPERTS:2], float(ROWS), None, ALU.add).then_inc(index_ready.sem, 1)
            dve.tensor_copy(prob_s[:, :], lp[:, 1, 0:EXPERTS])
            dve.drain()
            dve.wait_ge(filled.sem, 4)

            def spread(n, ring, q):
                dve.wait_ge(ring_loaded[q].sem, ring * 32 + 32)
                dve.wait_ge(y_done.sem, y_done.past(n - RING))
                dve.tensor_tensor(w2b[:, q, :, :].rearrange("p j (s k) -> p j s k", s=S),
                                  w2[:, q, :, :].unsqueeze(2).to_broadcast([P, S, S, K]),
                                  own[:, :].unsqueeze(1).unsqueeze(3).to_broadcast([P, S, S, K]), ALU.mult).then_inc(w2_spread.sem, 1)

            def keep(n, ring, q, reuse):
                u = q % 2
                dve.wait_ge(y_done.sem, y_done.past(n))
                dve.tensor_tensor(yb[:, u, :], yp[:, u, 0:D], b2[:, bass.ds(n, 1), :], ALU.add)
                dve.drain()
                if reuse:
                    dve.wait_ge(added[u].sem, (ring * (RING // 2) + q // 2 - 1) * 16)
                dve.tensor_scalar(yo[:, q, :], yb[:, u, :], prob_s[:, bass.ds(n, 1)], None, ALU.mult).then_inc(y_kept.sem, 1)

            def ring_body(ring, reuse=True, last=False):
                for q in range(RING):
                    if not (last and q == RING - 1):
                        spread(ring * RING + q + 1, ring + (q + 1) // RING, (q + 1) % RING)
                    keep(ring * RING + q, ring, q, reuse)

            dve.wait_ge(w_loaded.sem, 48)
            spread(0, 0, 0)
            ring_body(0, False)
            with dve.Fori(1, EXPERTS // RING - 1) as ring:
                ring_body(ring)
            ring_body(EXPERTS // RING - 1, last=True)
            for q in range(4):
                dve.wait_ge(acc_loaded[q].sem, 32)
                c8 = slice(q * 8, (q + 1) * 8)
                dve.tensor_tensor(acc_b[:, c8, :], acc_b[:, c8, :], core.all_xn[:, c8, :], ALU.add)
                dve.drain()
                dve.scalar_tensor_tensor(core.x[:, c8, :].rearrange("p a b -> p (a b)"), acc_b[:, c8, :].rearrange("p a b -> p (a b)"), 0.5,
                                         core.x[:, c8, :].rearrange("p a b -> p (a b)"), ALU.mult, ALU.add)
                dve.drain()
                for c in (2 * q, 2 * q + 1):
                    new_sums_dve(dve, core, c)

        @block.scalar
        def _(act):
            act.wait_ge(wr_turned.sem, 1)
            act.activation(wr[:, 0:UP], lp[:, 0, 0:UP], ACT.Copy)
            act.activation(wr[:, UP:P], lp[:, 0, 0:UP], ACT.Copy)
            act.activation(b1[:, :, :], lp[:, 1, 0:S * UP].rearrange("p (j e) -> p j e", e=UP)[:, :, 0:EXPERTS], ACT.Copy).then_inc(wr_kept.sem, 1)
            ln_scales_act(act, core, s)
            ln_act(act, core, s, 0, 0)

            def body(c, u, half, more=True):
                if more:
                    ln_act(act, core, s, c + 1, 1 - u)
                act.wait_ge(routed.sem, routed.past(c))
                lo = half * UP
                act.activation(lt[lo:lo + EXPERTS, bass.ds((c - half * (CHUNKS // 2)) * CW, CW)], lp[lo:lo + EXPERTS, u, :],
                               ACT.Copy).then_inc(logits_kept.sem, 1)

            act.wait_ge(wr_kept.sem, 2)
            each_pair(act, 0, CHUNKS // 2, lambda c, u: body(c, u, 0))
            each_pair(act, CHUNKS // 2, CHUNKS - 2, lambda c, u: body(c, u, 1))
            body(CHUNKS - 2, 0, 1)
            body(CHUNKS - 1, 1, 1, False)
            act.wait_ge(merged.sem, 1)
            act.activation(prob[:, :], prob[:, :], ACT.Exp, bias=big[:, 0:1], accum_out=esum[:, 0:1]).then_inc(exp_done.sem, 1)

            def turn(n, q):
                act.wait_ge(xt_done.sem, xt_done.past(n))
                act.activation(xgt[:, q % 2, :], s.tp[:, 0, 0:P], ACT.Copy).then_inc(xt_kept.sem, 1)

            def gelu(n, q):
                u = q % 2
                act.wait_ge(h_done.sem, h_done.past(n))
                act.wait_ge(y_done.sem, y_done.past(n - 2))
                for j in range(S):
                    last = act.activation(h[:, u, j, :], hu[:, u, j * P:(j + 1) * P], ACT.Gelu, bias=b1[:, j, bass.ds(n, 1)])
                last.then_inc(gelu_done.sem, 1)

            turn(0, 0)

            def ring_body(n0, last=False):
                for q in range(RING):
                    if not (last and q == RING - 1):
                        turn(n0 + q + 1, q + 1)
                    gelu(n0 + q, q)

            with act.Fori(0, EXPERTS // RING - 1) as ring:
                ring_body(ring * RING)
            ring_body(EXPERTS - RING, True)

        @block.tensor
        def _(pe):
            pe.wait_ge(w_loaded.sem, 48)
            pe.transpose(lp[:, 0, 0:EXPERTS], wr_raw[:, :], core.ident[0:EXPERTS, 0:EXPERTS])
            pe.matmul(lp[:, 0, EXPERTS:UP], wr_raw[:, :], core.ident[0:EXPERTS, 0:UP - EXPERTS], start=True, stop=True)
            for j in range(S):
                last = pe.transpose(lp[:, 1, j * UP:j * UP + EXPERTS], b1_raw[:, j::S], core.ident[0:EXPERTS, 0:EXPERTS])
            last.then_inc(wr_turned.sem, 1)
            ln_pe(pe, core, s, 0, 0)
            pe.wait_ge(wr_kept.sem, 1)

            def body(c, u, more=True):
                if more:
                    ln_pe(pe, core, s, c + 1, 1 - u)
                pe.wait_ge(s.xnt_ready.sem, s.xnt_ready.past(c))
                pe.wait_ge(logits_kept.sem, logits_kept.past(c - 2))
                pe.matmul(lp[:, u, :], wr[:, :], core.xnt[:, u, :], start=True, stop=True).then_inc(routed.sem, 1)

            each_pair(pe, 0, CHUNKS - 2, body)
            body(CHUNKS - 2, 0)
            body(CHUNKS - 1, 1, False)
            pe.wait_ge(logits_kept.sem, logits_kept.past(CHUNKS - 1))
            pe.wait_ge(listed.sem, 1)
            pe.transpose(lp[:, 0, 0:EXPERTS], posf[0:EXPERTS, :], core.ident[0:EXPERTS, 0:EXPERTS])
            pe.transpose(lp[:, 1, 0:EXPERTS], prob[:, :], core.ident[0:EXPERTS, 0:EXPERTS]).then_inc(slots_turned.sem, 1)

            def turn(n, ring, q):
                pe.wait_ge(xg_loaded[q].sem, ring * 16 + 16)
                pe.wait_ge(xt_kept.sem, xt_kept.past(n - 1))
                pe.transpose(s.tp[:, 0, 0:P], xg[:, q, :], core.ident[:, :]).then_inc(xt_done.sem, 1)

            def up(n, ring, q):
                u = q % 2
                pe.wait_ge(ring_loaded[q].sem, ring * 32 + 32)
                pe.wait_ge(xt_kept.sem, xt_kept.past(n))
                pe.wait_ge(gelu_done.sem, gelu_done.past(n - 2))
                for j in range(S):
                    last = pe.matmul(hu[:, u, j * P:(j + 1) * P], w1[:, q, :, :].rearrange("p s m -> p (s m)")[:, j::S],
                                     xgt[:, u, :], start=True, stop=True)
                last.then_inc(h_done.sem, 1)

            def down(n, q):
                u = q % 2
                pe.wait_ge(w2_spread.sem, w2_spread.past(n))
                pe.wait_ge(gelu_done.sem, gelu_done.past(n))
                pe.wait_ge(y_kept.sem, y_kept.past(n - 2))
                for j in range(S):
                    last = pe.matmul(yp[:, u, 0:D], h[:, u, j, :], w2b[:, q, j, :], start=j == 0, stop=j == S - 1)
                last.then_inc(y_done.sem, 1)

            turn(0, 0, 0)
            up(0, 0, 0)
            turn(1, 0, 1)

            def ring_body(n0, ring, last=False):
                for q in range(RING):
                    if not (last and q == RING - 1):
                        up(n0 + q + 1, ring + (q + 1) // RING, (q + 1) % RING)
                    if not (last and q >= RING - 2):
                        turn(n0 + q + 2, ring + (q + 2) // RING, (q + 2) % RING)
                    down(n0 + q, q)

            with pe.Fori(0, EXPERTS // RING - 1) as ring:
                ring_body(ring * RING, ring)
            ring_body(EXPERTS - RING, EXPERTS // RING - 1, True)



def l2_attn(core):
    nc, w = core.nc, core.w
    HV = 64
    PAIRS = w["L2_attn_W_Q"].shape[1] // P
    HALVES = PAIRS * P // CW
    PH = CW // P
    NT = N // P
    KV_GROUPS = ((0, 1, 2), (3, 4, 5), (6, 7))
    with stage(nc) as s:
        ln_signals(s, 1)
        wq = s.sb("wq", [P, PAIRS * P])
        wk = s.sb("wk", [P, PAIRS * P])
        wv = s.sb("wv", [P, PAIRS * P])
        wfc = s.sb("wfc", [P, PAIRS, P])
        gamma = s.sb("gamma", [P, P])
        beta = s.sb("beta", [P, P])
        same = s.sb("same_head", [P, P])
        qt = s.sb("qt", [P, 2, PAIRS, CW])
        ks = s.sb("ks", [P, NT, PAIRS * P])
        vs = s.sb("vs", [P, NT, PAIRS, P + 1])
        kvs = s.sb("kvs", [P, PAIRS, P])
        kss = s.sb("kss", [P, PAIRS, P])
        den = s.sb("den", [P, 2, N])
        ot = s.sb("ot", [P, PAIRS, N])
        guard = s.sb("guard", [P, 1])
        r = s.sb("r", [P, 2, NT, P])
        rs = s.sb("rs", [P, NT, 6])
        rm = s.sb("rm", [P, NT, 2])
        rv = s.sb("rv", [P, NT])
        rd = s.sb("rd", [P, NT])
        power = s.sb("power", [P, NT])
        pj = s.ps("pj", [P, 2, CW])
        kv = s.ps("kv", [P, 2, CW])
        nd = s.ps("nd", [P, 2, 2, N])
        y = s.ps("y", [P, 2, NT, P])
        w_loaded = s.sig("w_loaded")
        vectors_loaded = s.sig("vectors_loaded")
        filled = s.sig("filled")
        masked = s.sig("masked")
        projected = s.sig("projected")
        act_kept = s.sig("act_kept", 1)
        v_kept = s.sig("v_kept", 1)
        kv_done = s.sig("kv_done")
        kvs_ready = s.sig("kvs_ready", 2)
        nd_done = s.sig("nd_done")
        den_kept = s.sig("den_kept")
        o_ready = s.sig("o_ready", 2)
        y_done = s.sig("y_done")
        x_added = s.sig("x_added", 1)
        rv_ready = s.sig("rv_ready")
        rd_ready = s.sig("rd_ready")
        s.ready()
        block = s.ctx.enter_context(nc.Block())

        @block.sync
        def _(sp):
            for t, m in ((wq, "W_Q"), (wk, "W_K"), (wv, "W_V")):
                sp.dma_start(t[:, :], w[f"L2_attn_{m}"]).then_inc(w_loaded.sem, 16)
            sp.dma_start(wfc[:, :, :], w["L2_attn_W_fc"].rearrange("(a p) n -> p a n", p=P)).then_inc(w_loaded.sem, 16)
            for t, m in ((gamma, "gamma"), (beta, "beta")):
                sp.dma_start(t[:, :], w[f"L2_attn_{m}"].partition_broadcast(P)).then_inc(vectors_loaded.sem, 16)

        @block.gpsimd
        def _(pool):
            pool.memset(vs[:, :, :, P:P + 1], 1.0).then_inc(filled.sem, 1)
            pool.memset(guard[:, :], 1e-8).then_inc(filled.sem, 1)
            pool.memset(same[:, :], 0.0).then_inc(masked.sem, 1)
            pool.wait_ge(masked.sem, masked.past(0))
            pool.memset(same[0:HV, 0:HV], 1.0).then_inc(filled.sem, 1)
            pool.memset(same[HV:P, HV:P], 1.0).then_inc(filled.sem, 1)
            pool.wait_ge(filled.sem, filled.past(3))
            pool.memset(power[:, :], -0.5)
            pool.drain()
            with pool.Fori(0, B) as b:
                pool.wait_ge(rv_ready.sem, rv_ready.past(b))
                pool.tensor_tensor(rd[:, :], rv[:, :], power[:, :], ALU.pow).then_inc(rd_ready.sem, 1)

        @block.vector
        def _(dve):
            def keep_v(c, i):
                for t in range(NT):
                    for h in range(HALVES):
                        n = t * HALVES + h
                        dve.wait_ge(projected.sem, projected.past(24 * c + 8 + 8 * i + 2 * n + 1))
                        dve.tensor_copy(vs[:, t, h * PH:(h + 1) * PH, 0:P],
                                        pj[:, 1, :].rearrange("p (a v) -> p a v", v=P)).then_inc(v_kept.sem, 1)

            def keep_kv(c, i, g):
                m = 6 * c + 3 * i + g
                pairs = KV_GROUPS[g]
                bank = (3 * i + g) % 2
                dve.wait_ge(kv_done.sem, kv_done.past(m))
                src = kv[:, bank, 0:len(pairs) * (P + 1)].rearrange("p (a v) -> p a v", v=P + 1)
                dve.tensor_tensor(kvs[:, pairs[0]:pairs[-1] + 1, :], src[:, :, 0:P],
                                  same[:, :].unsqueeze(1).to_broadcast([P, len(pairs), P]), ALU.mult)
                for n, p in enumerate(pairs):
                    last = dve.tensor_scalar(kss[:, p, :], same[:, :], src[:, n, P:P + 1], None, ALU.mult)
                last.then_inc(kvs_ready.sem, 1)

            def divide(c, i, p):
                n = PAIRS * (2 * c + i) + p
                dve.wait_ge(den_kept.sem, den_kept.past(n))
                dve.reciprocal(den[:, p % 2, :], den[:, p % 2, :])
                dve.drain()
                dve.tensor_tensor(ot[:, p, :], nd[:, p % 2, 0, :], den[:, p % 2, :], ALU.mult).then_inc(o_ready.sem, 1)

            def add(c, i):
                n = 2 * c + i
                for t in range(NT):
                    j = c * CT + i * NT + t
                    dve.tensor_scalar(r[:, i, t, :], core.x[:, bass.ds(j, 1), :], core.mean[:, bass.ds(j, 1)],
                                      core.rstd[:, bass.ds(j, 1)], ALU.subtract, ALU.mult)
                dve.drain()
                dve.wait_ge(y_done.sem, y_done.past(n))
                dve.tensor_tensor(r[:, i, :, :], r[:, i, :, :], y[:, i, :, :], ALU.add).then_inc(x_added.sem, 1)
                dve.drain()
                for t in range(NT):
                    dve.bn_stats(rs[:, t, :], r[:, i, t, :])
                dve.drain()
                for t in range(NT):
                    dve.bn_aggr(rm[:, t, :], rs[:, t, :])
                dve.drain()
                dve.tensor_scalar(rv[:, :], rm[:, :, 1], 1e-5, None, ALU.add).then_inc(rv_ready.sem, 1)
                dve.wait_ge(rd_ready.sem, rd_ready.past(n))
                for t in range(NT):
                    dve.tensor_scalar(r[:, i, t, :], r[:, i, t, :], rm[:, t, 0:1], rd[:, t:t + 1], ALU.subtract, ALU.mult)
                dve.drain()
                for v, op in ((gamma, ALU.mult), (beta, ALU.add)):
                    dve.tensor_tensor(r[:, i, :, :], r[:, i, :, :], v[:, :].unsqueeze(1).to_broadcast([P, NT, P]), op)
                    dve.drain()
                xs = rows(core.x, c * CT + i * NT, NT)
                dve.tensor_tensor(xs, xs, r[:, i, :, :], ALU.add)
                dve.drain()
                new_sums_dve(dve, core, c, range(i * NT, i * NT + NT))

            ln_scales_dve(dve, core, s)
            ln_dve(dve, core, s, 0, 0)
            dve.wait_ge(vectors_loaded.sem, 32)
            dve.wait_ge(filled.sem, filled.past(3))

            def body(c, u, more=True):
                if more:
                    ln_dve(dve, core, s, c + 1, 1 - u)
                for i in range(2):
                    keep_v(c, i)
                    if i == 1:
                        add(c, 0)
                    keep_kv(c, i, 0)
                    keep_kv(c, i, 1)
                    for p in range(PAIRS):
                        divide(c, i, p)
                        if p == 2:
                            keep_kv(c, i, 2)
                add(c, 1)

            each_pair(dve, 0, CHUNKS - 2, body)
            body(CHUNKS - 2, 0)
            body(CHUNKS - 1, 1, False)

        @block.scalar
        def _(act):
            def keep_q(c, u):
                for p in range(PAIRS):
                    act.wait_ge(projected.sem, projected.past(24 * c + p))
                    act.activation(qt[:, u, p, :], pj[:, p % 2, :], ACT.Sigmoid).then_inc(act_kept.sem, 1)

            ln_scales_act(act, core, s)
            ln_act(act, core, s, 0, 0)
            keep_q(0, 0)
            act.wait_ge(filled.sem, filled.past(3))

            def body(c, u, more=True):
                for i in range(2):
                    for t in range(NT):
                        for h in range(HALVES):
                            n = t * HALVES + h
                            act.wait_ge(projected.sem, projected.past(24 * c + 8 + 8 * i + 2 * n))
                            act.activation(ks[:, t, h * CW:(h + 1) * CW], pj[:, 0, :], ACT.Sigmoid).then_inc(act_kept.sem, 1)
                    for p in range(PAIRS):
                        act.wait_ge(nd_done.sem, nd_done.past(PAIRS * (2 * c + i) + p))
                        act.activation(den[:, p % 2, :], nd[:, p % 2, 1, :], ACT.Identity,
                                       bias=guard[:, :]).then_inc(den_kept.sem, 1)
                if more:
                    ln_act(act, core, s, c + 1, 1 - u)
                    keep_q(c + 1, 1 - u)

            each_pair(act, 0, CHUNKS - 2, body)
            body(CHUNKS - 2, 0)
            body(CHUNKS - 1, 1, False)

        @block.tensor
        def _(pe):
            def q_groups(c, u):
                pe.wait_ge(s.xnt_ready.sem, s.xnt_ready.past(c))
                for p in range(PAIRS):
                    if p == 1:
                        pe.wait_ge(v_kept.sem, v_kept.past(8 * c - 1))
                    else:
                        pe.wait_ge(act_kept.sem, act_kept.past(16 * c + max(p - 2, -1)))
                    pe.matmul(pj[:, p % 2, :], wq[:, p * P:(p + 1) * P], core.xnt[:, u, :],
                              start=True, stop=True).then_inc(projected.sem, 1)

            def kv_groups(c, u, i):
                for t in range(NT):
                    x_tile = core.xnt[:, u, (i * NT + t) * P:(i * NT + t + 1) * P]
                    for h in range(HALVES):
                        n = t * HALVES + h
                        pe.wait_ge(act_kept.sem, act_kept.past(16 * c + 8 + 4 * i + n - 1 - (i == 0 and n == 0)))
                        pe.matmul(pj[:, 0, :], x_tile, wk[:, h * CW:(h + 1) * CW], start=True, stop=True).then_inc(projected.sem, 1)
                        if i == 0 and n == 0:
                            pe.wait_ge(act_kept.sem, act_kept.past(16 * c + 7))
                        else:
                            pe.wait_ge(v_kept.sem, v_kept.past(8 * c + 4 * i + n - 1))
                        pe.matmul(pj[:, 1, :], x_tile, wv[:, h * CW:(h + 1) * CW], start=True, stop=True).then_inc(projected.sem, 1)

            def kv_products(c, i, g):
                m = 6 * c + 3 * i + g
                pe.wait_ge(kvs_ready.sem, kvs_ready.past(m - 2))
                for n, p in enumerate(KV_GROUPS[g]):
                    for t in range(NT):
                        last = pe.matmul(kv[:, (3 * i + g) % 2, n * (P + 1):(n + 1) * (P + 1)],
                                         ks[:, t, p * P:(p + 1) * P], vs[:, t, p, :], start=t == 0, stop=t == NT - 1)
                last.then_inc(kv_done.sem, 1)

            def q_products(c, u, i, p):
                n = PAIRS * (2 * c + i) + p
                pe.wait_ge(kvs_ready.sem, kvs_ready.past(6 * c + 3 * i + min(p // 3, 2)))
                pe.wait_ge(o_ready.sem, o_ready.past(n - 2))
                q = qt[:, u, p, i * N:(i + 1) * N]
                pe.matmul(nd[:, p % 2, 0, :], kvs[:, p, :], q, start=True, stop=True)
                pe.matmul(nd[:, p % 2, 1, :], kss[:, p, :], q, start=True, stop=True).then_inc(nd_done.sem, 1)

            def out_product(c, i):
                n = 2 * c + i
                pe.wait_ge(o_ready.sem, o_ready.past(PAIRS * n + PAIRS - 1))
                pe.wait_ge(x_added.sem, x_added.past(n - 1))
                for t in range(NT):
                    for p in range(PAIRS):
                        last = pe.matmul(y[:, i, t, :], ot[:, p, t * P:(t + 1) * P], wfc[:, p, :],
                                         start=p == 0, stop=p == PAIRS - 1)
                last.then_inc(y_done.sem, 1)

            ln_pe(pe, core, s, 0, 0)
            pe.wait_ge(w_loaded.sem, 64)
            q_groups(0, 0)
            pe.wait_ge(filled.sem, filled.past(3))

            def body(c, u, more=True):
                for i in range(2):
                    kv_groups(c, u, i)
                    if i == 1:
                        out_product(c, 0)
                    pe.wait_ge(act_kept.sem, act_kept.past(16 * c + 11 + 4 * i))
                    pe.wait_ge(v_kept.sem, v_kept.past(8 * c + 3 + 4 * i))
                    kv_products(c, i, 0)
                    kv_products(c, i, 1)
                    for p in range(PAIRS):
                        q_products(c, u, i, p)
                        if p == 2:
                            kv_products(c, i, 2)
                if more:
                    ln_pe(pe, core, s, c + 1, 1 - u)
                    q_groups(c + 1, 1 - u)
                out_product(c, 1)

            each_pair(pe, 0, CHUNKS - 2, body)
            body(CHUNKS - 2, 0)
            body(CHUNKS - 1, 1, False)



def l3_ffn(core):
    nc, w = core.nc, core.w
    HID = 512
    HB = HID // P
    mats = [("w1", HB, P, 1.0), ("w2", HB, P, 1.0), ("h1", HB, HID, 1.0), ("h2", HB, HID, 1.0),
            ("w3", 1, HID, 0.5)]
    with stage(nc) as s:
        ln_signals(s)
        raw = {m: s.sb(f"raw_{m}", [P, ob, width]) for m, ob, width, _ in mats}
        scl = {m: s.sb(f"scl_{m}", [P, ob]) for m, ob, _, _ in mats}
        wt = {m: s.sb(f"wt_{m}", [P, width // P, ob * P]) for m, ob, width, _ in mats}
        g = s.sb("g", [P, HB, CW])
        ha = s.sb("ha", [P, HB, CW])
        hb = s.sb("hb", [P, HB, CW])
        hc = s.sb("hc", [P, HB, CW])
        z = s.ps("z", [P, 4, CW])
        y = s.ps("y", [P, 2, CT, P])
        w_loaded = [s.sig(f"w_loaded_{m}") for m, *_ in mats]
        w_scaled = s.sig("w_scaled")
        wt_turned = s.sig("wt_turned", 4)
        wt_kept = s.sig("wt_kept", 4)
        group_done = s.sig("group_done")
        act_done = s.sig("act_done", 12)
        gated = s.sig("gated", 4)
        y_done = s.sig("y_done")
        x_added = s.sig("x_added", 2)
        s.ready()
        blocks = [(m, o, i) for m, ob, width, _ in mats for o in range(ob) for i in range(width // P)]
        quads = [blocks[n:n + 4] for n in range(0, len(blocks), 4)]
        block = s.ctx.enter_context(nc.Block())

        @block.sync
        def _(sp):
            for (m, ob, _, _), loaded in zip(mats, w_loaded):
                sp.dma_start(raw[m][:, :, :], w[f"L3_ffn_{m}_w"].rearrange("(a p) i -> p a i", p=P)).then_inc(loaded.sem, 16)
                with nc.allow_non_contiguous_dma("one scale a row"):
                    sp.dma_start(scl[m][:, :], w[f"L3_ffn_{m}_s"].rearrange("(a p) -> p a", p=P)).then_inc(loaded.sem, 16)

        @block.vector
        def _(dve):
            for (m, ob, _, half), loaded in zip(mats, w_loaded):
                dve.wait_ge(loaded.sem, 32)
                for o in range(ob):
                    last = dve.tensor_scalar(raw[m][:, o, :], raw[m][:, o, :], scl[m][:, o:o + 1], half,
                                             ALU.mult, ALU.mult)
                last.then_inc(w_scaled.sem, 1)
            ln_scales_dve(dve, core, s)
            ln_dve(dve, core, s, 0, 0)

            def body(c, u, more=True):
                if more:
                    ln_dve(dve, core, s, c + 1, 1 - u)
                for f in range(HB):
                    dve.wait_ge(act_done.sem, act_done.past(12 * c + f))
                    dve.wait_ge(group_done.sem, group_done.past(16 * c + 2 * f + 1))
                    dve.tensor_tensor(ha[:, f, :], g[:, f, :], z[:, (2 * f + 1) % 4, :],
                                      ALU.mult).then_inc(gated.sem, 1)
                dve.wait_ge(y_done.sem, y_done.past(c))
                xs = rows(core.x, c * CT, CT)
                dve.tensor_tensor(xs, xs, y[:, u, :, :], ALU.add).then_inc(x_added.sem, 1)
                dve.wait_ge(x_added.sem, x_added.past(c))
                new_sums_dve(dve, core, c)

            each_pair(dve, 0, CHUNKS - 2, body)
            body(CHUNKS - 2, 0)
            body(CHUNKS - 1, 1, False)

        @block.scalar
        def _(act):
            for n, quad in enumerate(quads):
                act.wait_ge(wt_turned.sem, wt_turned.past(n))
                for q, (m, o, i) in enumerate(quad):
                    last = act.activation(wt[m][:, i, o * P:(o + 1) * P], z[:, n % 4, q * P:(q + 1) * P], ACT.Copy)
                last.then_inc(wt_kept.sem, 1)
            ln_scales_act(act, core, s)
            ln_act(act, core, s, 0, 0)

            def body(c, u, more=True):
                for f in range(HB):
                    act.wait_ge(group_done.sem, group_done.past(16 * c + 2 * f))
                    act.activation(g[:, f, :], z[:, 2 * f % 4, :], ACT.Silu).then_inc(act_done.sem, 1)
                if more:
                    ln_act(act, core, s, c + 1, 1 - u)
                for layer, h in ((8, hb), (12, hc)):
                    for o in range(HB):
                        act.wait_ge(group_done.sem, group_done.past(16 * c + layer + o))
                        act.activation(h[:, o, :], z[:, o, :], ACT.Gelu).then_inc(act_done.sem, 1)

            each_pair(act, 0, CHUNKS - 2, body)
            body(CHUNKS - 2, 0)
            body(CHUNKS - 1, 1, False)

        @block.tensor
        def _(pe):
            for n, quad in enumerate(quads):
                names = [m for m, *_ in mats]
                pe.wait_ge(w_scaled.sem, w_scaled.past(max(names.index(m) for m, _, _ in quad)))
                pe.wait_ge(wt_kept.sem, wt_kept.past(n - 4))
                for q, (m, o, i) in enumerate(quad):
                    last = pe.transpose(z[:, n % 4, q * P:(q + 1) * P], raw[m][:, o, i * P:(i + 1) * P], core.ident[:, :])
                last.then_inc(wt_turned.sem, 1)
            pe.wait_ge(wt_kept.sem, wt_kept.past(len(quads) - 1))
            ln_pe(pe, core, s, 0, 0)

            def body(c, u, more=True):
                pe.wait_ge(s.xnt_ready.sem, s.xnt_ready.past(c))
                for f in range(HB):
                    for half, m in enumerate(("w1", "w2")):
                        if f < 2:
                            pe.wait_ge(act_done.sem, act_done.past(12 * (c - 1) + 8 + 2 * f + half))
                        elif half == 0:
                            pe.wait_ge(act_done.sem, act_done.past(12 * c + f - 2))
                        else:
                            pe.wait_ge(gated.sem, gated.past(4 * c + f - 2))
                        pe.matmul(z[:, (2 * f + half) % 4, :], wt[m][:, 0, f * P:(f + 1) * P], core.xnt[:, u, :],
                                  start=True, stop=True).then_inc(group_done.sem, 1)
                if more:
                    ln_pe(pe, core, s, c + 1, 1 - u)
                pe.wait_ge(act_done.sem, act_done.past(12 * c + 2))
                for o in range(HB):
                    for f in range(HB):
                        if o == 0:
                            pe.wait_ge(gated.sem, gated.past(4 * c + f))
                        last = pe.matmul(z[:, o, :], wt["h1"][:, f, o * P:(o + 1) * P], ha[:, f, :],
                                         start=f == 0, stop=f == HB - 1)
                    last.then_inc(group_done.sem, 1)
                for o in range(HB):
                    for f in range(HB):
                        if o == 0:
                            pe.wait_ge(act_done.sem, act_done.past(12 * c + 4 + f))
                        last = pe.matmul(z[:, o, :], wt["h2"][:, f, o * P:(o + 1) * P], hb[:, f, :],
                                         start=f == 0, stop=f == HB - 1)
                    last.then_inc(group_done.sem, 1)
                pe.wait_ge(x_added.sem, x_added.past(c - 2))
                for j in range(CT):
                    for f in range(HB):
                        if j == 0:
                            pe.wait_ge(act_done.sem, act_done.past(12 * c + 8 + f))
                        last = pe.matmul(y[:, u, j, :], hc[:, f, j * P:(j + 1) * P], wt["w3"][:, f, :],
                                         start=f == 0, stop=f == HB - 1)
                last.then_inc(y_done.sem, 1)

            each_pair(pe, 0, CHUNKS - 2, body)
            body(CHUNKS - 2, 0)
            body(CHUNKS - 1, 1, False)



def l3_attn(core):
    nc, w = core.nc, core.w
    NT = N // P
    TERMS = 3
    PARTS = 2 * NT * GROUPS
    with stage(nc) as s:
        ln_signals(s, 1)
        head_masks(core, s)
        names = ("W_q", "W_k", "W_v", "W_o")
        raw = {m: s.sb(f"raw_{m}", [P, P]) for m in names}
        wt = {m: s.sb(f"wt_{m}", [P, P]) for m in names}
        ident_b = s.sb("ident_b", [P, P], BF16)
        pick = s.sb("pick", [TERMS * HEADS, HEADS, P], BF16)
        kt = s.sb("kt", [P, CW])
        qt = s.sb("qt", [P, CW])
        kg = s.sb("kg", [P, 2, GROUPS, CW])
        qj = s.sb("qj", [P, 2, GROUPS, CW])
        v1 = s.sb("v1", [P, 2, CT, HEADS, HW])
        mx = s.sb("mx", [P, 2, NT, GROUPS, GROUPS])
        rest = s.sb("rest", [P, 2, NT, HEADS])
        m3 = s.sb("m3", [P, 2, NT, P // HEADS, HEADS], BF16)
        nm = s.sb("nm", [P, 2, N], BF16)
        e = s.sb("e", [P, NT, HEADS, N])
        den = s.sb("den", [P, NT, HEADS])
        o = s.sb("o", [P, NT, P])
        ot = s.sb("ot", [P, NT, P])
        pj = s.ps("pj", [P, CW])
        sa = s.ps("sa", [P, 2, 2, N])
        sc = s.ps("sc", [P, 2, 2, N])
        ob = s.ps("ob", [P, NT, HEADS, HW])
        mb = s.ps("mb", [P, 2, NT * P])
        nm_ps = s.tp[:, 0, 0:P].bitcast(BF16)
        w_loaded = s.sig("w_loaded")
        w_turned = s.sig("w_turned")
        w_kept = s.sig("w_kept")
        ident_ready = s.sig("ident_ready")
        cleared = s.sig("cleared")
        filled = s.sig("filled")
        scaled = s.sig("scaled")
        projected = s.sig("projected")
        pj_kept = s.sig("pj_kept", 1)
        split_done = s.sig("split_done")
        sa_done = s.sig("sa_done")
        max_done = s.sig("max_done", 2)
        m3_ready = s.sig("m3_ready")
        nm_turned = s.sig("nm_turned")
        nm_kept = s.sig("nm_kept", 1)
        sc_done = s.sig("sc_done")
        exp_done = s.sig("exp_done", 2)
        av_done = s.sig("av_done")
        o_ready = s.sig("o_ready", 1)
        o_turned = s.sig("o_turned")
        ot_kept = s.sig("ot_kept")
        y_done = s.sig("y_done")
        x_added = s.sig("x_added", 1)
        s.ready()
        block = s.ctx.enter_context(nc.Block())

        @block.sync
        def _(sp):
            for m in names:
                sp.dma_start(raw[m][:, :], w[f"L3_attn_{m}"]).then_inc(w_loaded.sem, 16)

        @block.gpsimd
        def _(pool):
            head_masks_pool(pool, s)
            pool.memset(pick[:, :, :], 0.0).then_inc(cleared.sem, 1)
            for term in range(TERMS):
                pool.wait_ge(cleared.sem, term + 1)
                pool.affine_select(out=pick[:, :, :], in_=pick[:, :, :], compare_op=ALU.not_equal, fill=1.0,
                                   base=-term * HEADS, pattern=[[-1, HEADS], [0, P]], channel_multiplier=1).then_inc(cleared.sem, 1)
            pool.wait_ge(cleared.sem, TERMS + 1)
            pool.memset(v1[:, :, :, :, DH:HW], 1.0).then_inc(filled.sem, 1)

        @block.vector
        def _(dve):
            def keep(c, u):
                for n, t in enumerate((kt, qt)):
                    dve.wait_ge(projected.sem, projected.past(3 * c + n))
                    dve.tensor_copy(t[:, :], pj[:, :]).then_inc(pj_kept.sem, 1)
                dve.wait_ge(projected.sem, projected.past(3 * c + 2))
                for j in range(CT):
                    last = dve.tensor_copy(v1[:, u, j, :, 0:DH], pj[:, j * P:(j + 1) * P].rearrange("p (h e) -> p h e", h=HEADS))
                last.then_inc(pj_kept.sem, 1)

            def maxima(c, i):
                b = 2 * c + i
                for t in range(NT):
                    for j in range(GROUPS):
                        for half in range(2):
                            n = (t * GROUPS + j) * 2 + half
                            dve.wait_ge(sa_done.sem, sa_done.past(PARTS * b + n))
                            dve.tensor_reduce(mx[:, i, t, 2 * half:2 * half + 2, j], sa[:, n % 2, :, :], AX.X,
                                              ALU.max).then_inc(max_done.sem, 1)
                m = mx[:, i, :, :, :].rearrange("p t g j -> p t (g j)")
                dve.drain()
                dve.tensor_scalar(m3[:, i, :, 0, :], m, -1.0, None, ALU.mult)
                dve.drain()
                dve.scalar_tensor_tensor(rest[:, i, :, :], m, -1.0, m3[:, i, :, 0, :], ALU.mult, ALU.subtract)
                dve.drain()
                dve.tensor_copy(m3[:, i, :, 1, :], rest[:, i, :, :])
                dve.drain()
                dve.tensor_tensor(m3[:, i, :, 2, :], rest[:, i, :, :], m3[:, i, :, 1, :], ALU.subtract).then_inc(m3_ready.sem, 1)

            def normalise(c, i):
                dve.wait_ge(av_done.sem, av_done.past(2 * c + i))
                dve.reciprocal(den[:, :, :], ob[:, :, :, DH])
                dve.drain()
                for t in range(NT):
                    last = dve.tensor_tensor(o[:, t, :].rearrange("p (h e) -> p h e", h=HEADS), ob[:, t, :, 0:DH],
                                             den[:, t, :].unsqueeze(2).to_broadcast([P, HEADS, DH]), ALU.mult)
                last.then_inc(o_ready.sem, 1)

            def add(c, i):
                xs = rows(core.x, c * CT + i * NT, NT)
                dve.wait_ge(y_done.sem, y_done.past(2 * c + i))
                dve.tensor_tensor(xs, xs, mb[:, 1, :].rearrange("p (t e) -> p t e", t=NT), ALU.add).then_inc(x_added.sem, 1)
                dve.drain()
                new_sums_dve(dve, core, c, range(i * NT, i * NT + NT))

            dve.memset(m3[:, :, :, TERMS:, :], 0.0)
            dve.tensor_copy(ident_b[:, :], core.ident[:, :]).then_inc(ident_ready.sem, 1)
            head_masks_dve(dve, s)
            dve.drain()
            dve.tensor_scalar(s.place[:, :], s.place[:, :], 1.0 / DH ** 0.5, None, ALU.mult).then_inc(scaled.sem, 1)
            ln_scales_dve(dve, core, s)
            ln_dve(dve, core, s, 0, 0)
            dve.wait_ge(filled.sem, filled.past(0))
            keep(0, 0)
            maxima(0, 0)

            def body(c, u, more=True):
                if more:
                    ln_dve(dve, core, s, c + 1, 1 - u)
                maxima(c, 1)
                if more:
                    keep(c + 1, 1 - u)
                normalise(c, 0)
                if more:
                    maxima(c + 1, 0)
                add(c, 0)
                normalise(c, 1)
                add(c, 1)

            each_pair(dve, 0, CHUNKS - 2, body)
            body(CHUNKS - 2, 0)
            body(CHUNKS - 1, 1, False)

        @block.scalar
        def _(act):
            def split(c, u):
                for n, (t, to, mask) in enumerate(((kt, kg, s.group), (qt, qj, s.place))):
                    act.wait_ge(pj_kept.sem, pj_kept.past(3 * c + n))
                    for g in range(GROUPS):
                        last = act.activation(to[:, u, g, :], t[:, :], ACT.Copy, scale=mask[:, g:g + 1])
                    last.then_inc(split_done.sem, 1)

            def exps(c, i):
                for k in range(NT):
                    for g in range(GROUPS):
                        for half in range(2):
                            n = (k * GROUPS + g) * 2 + half
                            h = g * GROUPS + 2 * half
                            act.wait_ge(sc_done.sem, sc_done.past(PARTS * (2 * c + i) + n))
                            act.activation(e[:, k, h:h + 2, :], sc[:, n % 2, :, :], ACT.Exp).then_inc(exp_done.sem, 1)

            def keep_nm(c, i):
                act.wait_ge(nm_turned.sem, nm_turned.past(2 * c + i))
                act.activation(nm[:, i, :], nm_ps[:, :], ACT.Copy).then_inc(nm_kept.sem, 1)

            def keep_ot(c, i):
                act.wait_ge(o_turned.sem, o_turned.past(2 * c + i))
                act.activation(ot[:, :, :], mb[:, 0, :].rearrange("p (t e) -> p t e", t=NT), ACT.Copy).then_inc(ot_kept.sem, 1)

            act.wait_ge(w_turned.sem, 1)
            for n, m in enumerate(names):
                last = act.activation(wt[m][:, :], mb[:, n // 2, n % 2 * P:(n % 2 + 1) * P], ACT.Copy)
            last.then_inc(w_kept.sem, 1)
            ln_scales_act(act, core, s)
            ln_act(act, core, s, 0, 0)
            act.wait_ge(scaled.sem, 1)
            split(0, 0)
            keep_nm(0, 0)

            def body(c, u, more=True):
                exps(c, 0)
                keep_nm(c, 1)
                if more:
                    ln_act(act, core, s, c + 1, 1 - u)
                    split(c + 1, 1 - u)
                keep_ot(c, 0)
                exps(c, 1)
                if more:
                    keep_nm(c + 1, 0)
                keep_ot(c, 1)

            each_pair(act, 0, CHUNKS - 2, body)
            body(CHUNKS - 2, 0)
            body(CHUNKS - 1, 1, False)

        @block.tensor
        def _(pe):
            def project(c, u):
                pe.wait_ge(s.xnt_ready.sem, s.xnt_ready.past(c))
                for n, m in enumerate(("W_k", "W_q")):
                    pe.wait_ge(pj_kept.sem, pj_kept.past(3 * c + n - 1))
                    pe.matmul(pj[:, :], wt[m][:, :], core.xnt[:, u, :], start=True, stop=True).then_inc(projected.sem, 1)
                pe.wait_ge(pj_kept.sem, pj_kept.past(3 * c + 1))
                for j in range(CT):
                    last = pe.matmul(pj[:, j * P:(j + 1) * P], core.xnt[:, u, j * P:(j + 1) * P], wt["W_v"][:, :],
                                     start=True, stop=True)
                last.then_inc(projected.sem, 1)

            def row_scores(c, u, i):
                pe.wait_ge(split_done.sem, split_done.past(2 * c + 1))
                for t in range(NT):
                    for j in range(GROUPS):
                        for half in range(2):
                            n = (t * GROUPS + j) * 2 + half
                            pe.wait_ge(max_done.sem, max_done.past(PARTS * (2 * c + i) + n - 2))
                            pe.matmul(sa[:, n % 2, :, :], qj[:, u, j, (i * NT + t) * P:(i * NT + t + 1) * P],
                                      kg[:, u, 2 * half:2 * half + 2, i * N:(i + 1) * N], start=True, stop=True).then_inc(sa_done.sem, 1)

            def turn_maxima(c, i):
                b = 2 * c + i
                pe.wait_ge(m3_ready.sem, m3_ready.past(b))
                for t in range(NT):
                    last = pe.transpose(nm_ps[:, t * P:(t + 1) * P],
                                        m3[:, i, t, :, :].rearrange("p a h -> p (a h)"), ident_b[:, :])
                last.then_inc(nm_turned.sem, 1)

            def key_scores(c, u, i):
                pe.wait_ge(nm_kept.sem, nm_kept.past(2 * c + i))
                for k in range(NT):
                    for g in range(GROUPS):
                        for half in range(2):
                            n = (k * GROUPS + g) * 2 + half
                            h = g * GROUPS + 2 * half
                            pe.wait_ge(exp_done.sem, exp_done.past(PARTS * (2 * c + i) + n - 2))
                            pe.matmul(sc[:, n % 2, :, :], kg[:, u, g, (i * NT + k) * P:(i * NT + k + 1) * P],
                                      qj[:, u, 2 * half:2 * half + 2, i * N:(i + 1) * N], start=True, stop=False, skip_group_check=True)
                            pe.matmul(sc[:, n % 2, 0, :], pick[:, h, :], nm[0:TERMS * HEADS, i, :], start=False, stop=False, skip_group_check=True)
                            pe.matmul(sc[:, n % 2, 1, :], pick[:, h + 1, :], nm[0:TERMS * HEADS, i, :], start=False, stop=True,
                                      skip_group_check=True).then_inc(sc_done.sem, 1)

            def values(c, u, i):
                b = 2 * c + i
                pe.wait_ge(o_ready.sem, o_ready.past(b - 1))
                pe.wait_ge(exp_done.sem, exp_done.past(PARTS * b + PARTS - 1))
                for t in range(NT):
                    for h in range(HEADS):
                        for k in range(NT):
                            last = pe.matmul(ob[:, t, h, :], e[:, k, h, t * P:(t + 1) * P], v1[:, u, i * NT + k, h, :],
                                             start=k == 0, stop=k == NT - 1)
                last.then_inc(av_done.sem, 1)

            def out_product(c, i):
                n = 2 * c + i
                pe.wait_ge(o_ready.sem, o_ready.past(n))
                pe.wait_ge(x_added.sem, x_added.past(n - 1))
                for t in range(NT):
                    last = pe.transpose(mb[:, 0, t * P:(t + 1) * P], o[:, t, :], core.ident[:, :])
                last.then_inc(o_turned.sem, 1)
                pe.wait_ge(ot_kept.sem, ot_kept.past(n))
                for t in range(NT):
                    last = pe.matmul(mb[:, 1, t * P:(t + 1) * P], ot[:, t, :], wt["W_o"][:, :], start=True, stop=True)
                last.then_inc(y_done.sem, 1)

            pe.wait_ge(w_loaded.sem, 16 * len(names))
            for n, m in enumerate(names):
                last = pe.transpose(mb[:, n // 2, n % 2 * P:(n % 2 + 1) * P], raw[m][:, :], core.ident[:, :])
            last.then_inc(w_turned.sem, 1)
            ln_pe(pe, core, s, 0, 0)
            pe.wait_ge(w_kept.sem, 1)
            project(0, 0)
            row_scores(0, 0, 0)
            pe.wait_ge(ident_ready.sem, 1)
            turn_maxima(0, 0)
            pe.wait_ge(cleared.sem, TERMS + 1)
            pe.wait_ge(filled.sem, 1)

            def body(c, u, more=True):
                row_scores(c, u, 1)
                key_scores(c, u, 0)
                turn_maxima(c, 1)
                if more:
                    pe.wait_ge(nm_kept.sem, nm_kept.past(2 * c + 1))
                    ln_pe(pe, core, s, c + 1, 1 - u)
                    project(c + 1, 1 - u)
                values(c, u, 0)
                if more:
                    row_scores(c + 1, 1 - u, 0)
                out_product(c, 0)
                key_scores(c, u, 1)
                if more:
                    pe.wait_ge(s.xnt_ready.sem, s.xnt_ready.past(c + 1))
                    turn_maxima(c + 1, 0)
                values(c, u, 1)
                out_product(c, 1)

            each_pair(pe, 0, CHUNKS - 2, body)
            body(CHUNKS - 2, 0)
            body(CHUNKS - 1, 1, False)



def begin(core):
    nc = core.nc
    with stage(nc) as s:
        x_loaded = s.sig("x_loaded")
        id_clear = s.sig("id_clear")
        s.ready()
        block = s.ctx.enter_context(nc.Block())

        @block.sync
        def _(sp):
            sp.dma_start(core.x[:, :, :], core.w["L0_attn_x"].rearrange("b (n p) d -> p (b n) d", p=P)).then_inc(x_loaded.sem, 16)

        @block.gpsimd
        def _(pool):
            pool.memset(core.ident[:, :], 0.0).then_inc(id_clear.sem, 1)
            pool.wait_ge(id_clear.sem, 1)
            pool.affine_select(out=core.ident[:, :], in_=core.ident[:, :], compare_op=ALU.not_equal, fill=1.0,
                               base=0, pattern=[[-1, P]], channel_multiplier=1)

        @block.vector
        def _(dve):
            dve.wait_ge(x_loaded.sem, 16)
            with dve.Fori(0, CHUNKS) as c:
                new_sums_dve(dve, core, c)


def end(core):
    nc = core.nc
    with stage(nc) as s:
        out_stored = s.sig("out_stored")
        s.ready()
        block = s.ctx.enter_context(nc.Block())

        @block.sync
        def _(sp):
            sp.dma_start(core.out.rearrange("b (n p) d -> p (b n) d", p=P), core.x[:, :, :]).then_inc(out_stored.sem, 16)
            sp.wait_ge(out_stored.sem, 16)


STAGES = [l0_ffn, l0_attn, l0_ffn, l1_ffn, l1_attn, l1_ffn, l2_ffn, l2_attn, l2_ffn, l3_ffn, l3_attn, l3_ffn]


def build(nc, inputs, out):
    with ExitStack() as ctx:
        core = Core(nc, ctx, inputs, out)
        begin(core)
        for run in STAGES:
            run(core)
        end(core)



def kernel(**inputs):
    import numpy as _np
    import concourse.bacc as _bacc
    from concourse import mybir as _mybir
    from concourse.bass_utils import run_bass_kernel_spmd as _run

    nc = _bacc.Bacc("TRN2", target_bir_lowering=False, num_devices=1)
    arrays, aps = {}, {}
    for name, value in inputs.items():
        a = _np.ascontiguousarray(value)
        arrays[f"in_{name}_dram"] = a
        aps[name] = nc.dram_tensor(f"in_{name}_dram", a.shape, _mybir.dt.from_np(a.dtype), kind="ExternalInput").ap()
    shape = inputs["L0_attn_x"].shape
    out = nc.dram_tensor("out_0_dram", shape, _mybir.dt.float32, kind="ExternalOutput").ap()
    build(nc, aps, out)
    r = _run(nc, [arrays], core_ids=[0])
    return r.results[0]["out_0_dram"]
```

```python
from contextlib import ExitStack, contextmanager

import concourse.bass as bass
from concourse import mybir

F32 = mybir.dt.float32
BF16 = mybir.dt.bfloat16
U32 = mybir.dt.uint32
ALU = mybir.AluOpType
ACT = mybir.ActivationFunctionType
AX = mybir.AxisListType

P = 128
D = 128
B, N = 16, 256
TOKENS = B * N
TILES = TOKENS // P
CT = 4
CW = CT * P
CHUNKS = TILES // CT


class Signal:

    def __init__(self, sem, ahead):
        self.sem = sem
        self.ahead = ahead

    def past(self, n):
        return n + 1 + self.ahead


class Stage:

    count = 0

    def __init__(self, nc, ctx):
        Stage.count += 1
        self.prefix = f"s{Stage.count}_"
        self.nc = nc
        self.ctx = ctx
        self.made = []
        self.pools = []

    def sig(self, name, ahead=0):
        s = Signal(self.ctx.enter_context(self.nc.semaphore(self.prefix + name)), ahead)
        self.made.append(s)
        return s

    def pool_dmas(self, core):
        self.pools = core.pool_dmas
        return self.pools

    def reset_pool_dmas(self, pool):
        nums = [s.sem.num for s in self.pools]
        pool.dma_reset(range(min(nums), max(nums) + 1))

    def sb(self, name, shape, dt=F32):
        return self.ctx.enter_context(self.nc.sbuf_tensor(self.prefix + name, shape, dt))

    def ps(self, name, shape, dt=F32):
        return self.ctx.enter_context(self.nc.psum_tensor(self.prefix + name, shape, dt))

    def ready(self):
        nums = [s.sem.num for s in self.made]
        self.nc.sync.sem_clear(range(min(nums), max(nums) + 1))
        if self.pools:
            nums = [s.sem.num for s in self.pools]
            self.nc.sync.sem_clear(range(min(nums), max(nums) + 1))
        for s in self.made:
            if s.ahead:
                self.nc.sync.sem_inc(s.sem, s.ahead)
        self.nc.all_engine_barrier()


@contextmanager
def stage(nc):
    with ExitStack() as ctx:
        yield Stage(nc, ctx)


def rows(t, first, count=1):
    return t[:, bass.ds(first, count), :]


class Core:

    def __init__(self, nc, ctx, inputs, out):
        self.nc = nc
        self.w = inputs
        self.out = out

        def sb(name, shape, dt=F32):
            return ctx.enter_context(nc.sbuf_tensor(name, shape, dt))

        self.pool_dmas = [Signal(ctx.enter_context(nc.semaphore(f"pool_dma{n}")), 0) for n in range(6)]
        self.x = sb("x", [P, TILES, D])
        self.ident = sb("ident", [P, P])
        self.sums = sb("sums", [P, TILES, 6])
        self.mean = sb("mean", [P, TILES])
        self.rstd = sb("rstd", [P, TILES])
        self.power = sb("power", [P, TILES])
        self.ln_t = sb("ln_t", [P, 3, TILES])
        self.xn = sb("xn", [P, 2, CT, D])
        self.xnt = sb("xnt", [P, 2, CW])
        self.all_xn = sb("all_xn", [P, TILES, D])
        self.rows_dram = nc.dram_tensor("rows_dram", (TOKENS, D), F32, kind="Internal").ap()
        self.table_dram = nc.dram_tensor("table_dram", (TOKENS + 64, D + 64), F32, kind="Internal").ap()
        self.acc_dram = nc.dram_tensor("acc_dram", (2 * (TOKENS + 64), D), F32, kind="Internal").ap()
        self.maxima_dram = nc.dram_tensor("maxima_dram", (48, N), BF16, kind="Internal").ap()
        self.parts_dram = nc.dram_tensor("parts_dram", (2, 2, 3, D, CW), BF16, kind="Internal").ap()
        self.sorted_dram = nc.dram_tensor("sorted_dram", (40 * P, D + 1), F32, kind="Internal").ap()
        self.sums_dram = nc.dram_tensor("sums_dram", (TOKENS + 40 * P, D), F32, kind="Internal").ap()



def ln_signals(s, tp_banks=2):
    s.tp_banks = tp_banks
    s.xn_ready = s.sig("xn_ready")
    s.tp_ready = s.sig("tp_ready", 2)
    s.xnt_ready = s.sig("xnt_ready", 2)
    s.scale_ready = s.sig("scale_ready")
    s.var_ready = s.sig("var_ready")
    s.tp = s.ps("tp", [P, tp_banks, CW])


def ln_scales_dve(dve, core, s, ln_eps=1e-5):
    me, mo = core.sums[:, :, 1], core.sums[:, :, 4]
    t0, t1, t2 = (core.ln_t[:, i, :] for i in range(3))
    dve.tensor_tensor(t0, me, mo, ALU.add)
    dve.tensor_tensor(t1, me, mo, ALU.subtract)
    dve.tensor_tensor(t2, core.sums[:, :, 2], core.sums[:, :, 5], ALU.add)
    dve.drain()
    dve.tensor_scalar(core.mean[:, :], t0, 0.5, None, ALU.mult)
    dve.tensor_tensor(t1, t1, t1, ALU.mult)
    dve.tensor_scalar(t2, t2, 1.0 / D, ln_eps, ALU.mult, ALU.add)
    dve.drain()
    dve.scalar_tensor_tensor(t2, t1, 0.25, t2, ALU.mult, ALU.add).then_inc(s.var_ready.sem, 1)
    dve.drain()


def ln_scale_pool(pool, core, s, c):
    tiles = bass.ds(c * CT, CT)
    pool.tensor_tensor(core.rstd[:, tiles], core.ln_t[:, 2, tiles], core.power[:, 0:CT],
                       ALU.pow).then_inc(s.scale_ready.sem, 1)


def ln_scales_pool(pool, core, s, chunks=range(CHUNKS)):
    if 0 in chunks:
        pool.wait_ge(s.var_ready.sem, s.var_ready.past(0))
    for c in chunks:
        ln_scale_pool(pool, core, s, c)


def ln_dve(dve, core, s, c, u, copied=None):
    dve.wait_ge(s.scale_ready.sem, s.scale_ready.past(c))
    dve.wait_ge(s.tp_ready.sem, s.tp_ready.past(c - 2))
    if copied:
        dve.wait_ge(copied.sem, copied.past(c - 2))
    for j in range(CT):
        t = c * CT + j
        last = dve.tensor_scalar(core.xn[:, u, j, :], core.x[:, bass.ds(t, 1), :],
                                 core.mean[:, bass.ds(t, 1)], core.rstd[:, bass.ds(t, 1)],
                                 ALU.subtract, ALU.mult)
    last.then_inc(s.xn_ready.sem, 1)


def ln_pe(pe, core, s, c, u):
    pe.wait_ge(s.xn_ready.sem, s.xn_ready.past(c))
    pe.wait_ge(s.xnt_ready.sem, s.xnt_ready.past(c - s.tp_banks))
    for j in range(CT):
        last = pe.transpose(s.tp[:, u % s.tp_banks, j * P:(j + 1) * P], core.xn[:, u, j, :], core.ident[:, :])
    last.then_inc(s.tp_ready.sem, 1)


def ln_act(act, core, s, c, u):
    act.wait_ge(s.tp_ready.sem, s.tp_ready.past(c))
    act.activation(core.xnt[:, u, :], s.tp[:, u % s.tp_banks, :], ACT.Copy).then_inc(s.xnt_ready.sem, 1)


def new_sums_dve(dve, core, c, tiles=range(CT)):
    for j in tiles:
        t = c * CT + j
        last = dve.bn_stats(core.sums[:, bass.ds(t, 1), :], core.x[:, bass.ds(t, 1), :])
    return last


def each_pair(eng, first, last, body):
    assert first % 2 == 0 and last % 2 == 0
    with eng.Fori(first // 2, last // 2) as pair:
        for u in range(2):
            body(pair * 2 + u, u)


def each_chunk(eng, body):
    body(0, 0, 0, 2)
    body(1, 1, 1, 2)
    each_pair(eng, 2, CHUNKS - 2, lambda c, u: body(c, u, 2, 2))
    body(CHUNKS - 2, 0, 2, 1)
    body(CHUNKS - 1, 1, 2, 0)



HEADS = 16
DH = D // HEADS
GROUPS = 4
HW = DH + 1



def l0_ffn(core):
    nc, w = core.nc, core.w
    EXPERTS, _, WIDE = w["L0_ffn_w1"].shape
    HID = WIDE // 2
    HB = HID // P
    SLOTS = TILES + EXPERTS
    I32 = mybir.dt.int32
    with stage(nc) as s:
        ln_signals(s, 1)
        wr = s.sb("wr", [P, EXPERTS])
        rb = s.sb("rb", [P, EXPERTS])
        w1 = s.sb("w1", [P, EXPERTS, WIDE])
        b1 = s.sb("b1", [P, EXPERTS, WIDE])
        w2 = s.sb("w2", [P, EXPERTS, HB, P])
        b2 = s.sb("b2", [P, EXPERTS, P])
        earlier = s.sb("earlier", [P, P])
        ones = s.sb("ones", [P, P])
        rev_i = s.sb("rev_i", [P, EXPERTS], I32)
        rev = s.sb("rev", [P, EXPERTS])
        first_i = s.sb("first_i", [P, SLOTS], I32)
        first = s.sb("first", [P, SLOTS])
        zero = s.sb("zero", [P, EXPERTS, TILES])
        sent = s.sb("sent", [P, SLOTS, D + 1])
        pad = s.sb("pad", [P, SLOTS, D + 1])
        logits = s.sb("logits", [P, TILES, EXPERTS])
        best = s.sb("best", [P, TILES])
        hot = s.sb("hot", [P, TILES, EXPERTS])
        tot = s.sb("tot", [P, EXPERTS, TILES])
        run = s.sb("run", [P, EXPERTS, TILES])
        start = s.sb("start", [P, EXPERTS])
        padded_i = s.sb("padded_i", [P, EXPERTS], I32)
        padded = s.sb("padded", [P, EXPERTS])
        pad_end = s.sb("pad_end", [P, EXPERTS])
        later = s.sb("later", [P, SLOTS, EXPERTS])
        owner = s.sb("owner", [P, SLOTS])
        owner_i = s.sb("owner_i", [P, SLOTS], I32)
        pos = s.sb("pos", [P, TILES])
        pos_i = s.sb("pos_i", [P, TILES], U32)
        xs = s.sb("xs", [P, 2, D])
        xst = s.sb("xst", [P, 2, P])
        ab = s.sb("ab", [P, 2, HID])
        gb = s.sb("gb", [P, 2, HID])
        hs = s.sb("hs", [P, 2, HID])
        ht = s.sb("ht", [P, 2, HB, P])
        ha = s.ps("ha", [P, 2, HID])
        hg = s.ps("hg", [P, 2, HID])
        htp = s.ps("htp", [P, 2, HB, P])
        yp = s.ps("yp", [P, CW])
        w_loaded = s.sig("w_loaded")
        halved = s.sig("halved")
        router_loaded = s.sig("router_loaded")
        filled = s.sig("filled")
        cleared = s.sig("cleared")
        rows_zeroed = s.sig("rows_zeroed")
        copied = s.sig("copied", 2)
        routed = s.sig("routed")
        logits_kept = s.sig("logits_kept", 1)
        hot_ready = s.sig("hot_ready")
        counted = s.sig("counted")
        pos_ready = s.sig("pos_ready")
        owner_ready = s.sig("owner_ready")
        scattered, stored = s.pool_dmas(core)[0:2]
        sorted_loaded = [s.sig(f"sorted_loaded{n}") for n in range(2)]
        xs_ready = s.sig("xs_ready")
        xt_done = s.sig("xt_done", 2)
        xst_kept = s.sig("xst_kept", 1)
        h_done = s.sig("h_done")
        biased = s.sig("biased", 2)
        sig_done = s.sig("sig_done")
        gated = s.sig("gated")
        ht_done = s.sig("ht_done")
        ht_kept = s.sig("ht_kept", 2)
        y_done = s.sig("y_done")
        y_kept = s.sig("y_kept", 1)
        loaded_back = [s.sig(f"loaded_back{q}") for q in range(4)]
        s.ready()
        xt = s.tp[:, 0, 0:P]
        sorted_dram, sums_dram = core.sorted_dram, core.sums_dram
        block = s.ctx.enter_context(nc.Block())

        def run_slots(eng, body):
            for i in range(2):
                body(i, i, i, 3)
            with eng.Fori(1, SLOTS // 2 - 2) as pair:
                for u in range(2):
                    body(pair * 2 + u, u, 2, 3)
            for i in range(SLOTS - 4, SLOTS):
                body(i, i % 2, 2, SLOTS - 1 - i)

        @block.sync
        def _(sp):
            sp.dma_start(wr[:, :], w["L0_ffn_router_w"]).then_inc(router_loaded.sem, 16)
            sp.dma_start(rb[:, :], w["L0_ffn_router_b"].partition_broadcast(P)).then_inc(router_loaded.sem, 16)
            sp.dma_start(w1[:, :, :], w["L0_ffn_w1"].rearrange("e d f -> d e f")).then_inc(w_loaded.sem, 16)
            sp.dma_start(w2[:, :, :, :], w["L0_ffn_w2"].rearrange("e (a p) n -> p e a n", p=P)).then_inc(w_loaded.sem, 16)
            for e in range(EXPERTS):
                sp.dma_start(b1[:, e, :], w["L0_ffn_b1"][e].partition_broadcast(P)).then_inc(w_loaded.sem, 16)
                sp.dma_start(b2[:, e, :], w["L0_ffn_b2"][e].partition_broadcast(P)).then_inc(w_loaded.sem, 16)
            sp.wait_ge(cleared.sem, 8)
            for n in range(4):
                few = SLOTS // 4
                sp.dma_start(sorted_dram[n * few * P:(n + 1) * few * P, :].rearrange("(a p) d -> p a d", p=P),
                             pad[:, n * few:(n + 1) * few, :]).then_inc(rows_zeroed.sem, 16)
            sp.wait_ge(scattered.sem, 16 * TILES)
            few = SLOTS // 5
            for n in range(5):
                sp.dma_start(sent[:, n * few:(n + 1) * few, :],
                             sorted_dram[n * few * P:(n + 1) * few * P, :].rearrange("(a p) d -> p a d", p=P)).then_inc(sorted_loaded[n > 0].sem, 16)
            sp.wait_ge(stored.sem, 16 * SLOTS)
            for q in range(4):
                sp.dma_start(core.all_xn[:, q * 8:(q + 1) * 8, :],
                             sums_dram[q * 8 * P:(q + 1) * 8 * P, :].rearrange("(t p) d -> p t d", p=P)).then_inc(loaded_back[q].sem, 16)

        @block.gpsimd
        def _(pool):
            ln_scales_pool(pool, core, s, range(2))
            pool.memset(ones[:, :], 1.0).then_inc(cleared.sem, 1)
            pool.memset(earlier[:, :], 1.0).then_inc(cleared.sem, 1)
            pool.memset(zero[:, :, :], 0.0).then_inc(cleared.sem, 1)
            pool.iota(rev_i[:, :], pattern=[[-1, EXPERTS]], base=EXPERTS, channel_multiplier=0).then_inc(cleared.sem, 1)
            pool.iota(first_i[:, :], pattern=[[P, SLOTS]], base=0, channel_multiplier=0).then_inc(cleared.sem, 1)
            pool.memset(pad[:, :, 0:D], 0.0).then_inc(cleared.sem, 1)
            pool.iota(pad[:, :, D:D + 1].bitcast(I32), pattern=[[P, SLOTS], [0, 1]], base=TOKENS, channel_multiplier=1).then_inc(cleared.sem, 1)
            pool.iota(sent[:, 0:TILES, D:D + 1].bitcast(I32), pattern=[[P, TILES], [0, 1]], base=0, channel_multiplier=1).then_inc(cleared.sem, 1)
            pool.wait_ge(cleared.sem, 8)
            pool.affine_select(out=earlier[:, :], in_=earlier[:, :], compare_op=ALU.is_gt, fill=0.0,
                               base=0, pattern=[[1, P]], channel_multiplier=-1).then_inc(filled.sem, 1)

            def copy(c, u, more=True):
                if more:
                    ln_scale_pool(pool, core, s, c + 2)
                pool.wait_ge(s.xn_ready.sem, s.xn_ready.past(c))
                pool.tensor_copy(sent[:, bass.ds(c * CT, CT), 0:D], core.xn[:, u, :, :]).then_inc(copied.sem, 1)

            each_pair(pool, 0, CHUNKS - 2, copy)
            copy(CHUNKS - 2, 0, False)
            copy(CHUNKS - 1, 1, False)
            pool.wait_ge(rows_zeroed.sem, 64)
            pool.wait_ge(pos_ready.sem, 1)
            pool.wait_ge(copied.sem, copied.past(CHUNKS - 1))
            for t in range(TILES):
                pool.indirect_dma_start(sorted_dram, bass.IndirectOffsetOnAxis(ap=pos_i[:, t:t + 1], axis=0),
                                        sent[:, t, :], None).then_inc(scattered.sem, 16)

            for n in range(2):
                pool.wait_ge(sorted_loaded[n].sem, 16 * (1 + 3 * n))
            for i in range(SLOTS):
                pool.wait_ge(y_kept.sem, y_kept.past(i))
                pool.indirect_dma_start(sums_dram, bass.IndirectOffsetOnAxis(ap=sent[:, i, D:D + 1].bitcast(U32), axis=0),
                                        pad[:, i, 0:D], None).then_inc(stored.sem, 16)
            pool.wait_ge(stored.sem, 16 * SLOTS)
            pool.wait_ge(scattered.sem, 16 * TILES)
            s.reset_pool_dmas(pool)

        @block.vector
        def _(dve):
            ln_scales_dve(dve, core, s)
            ln_dve(dve, core, s, 0, 0, copied)
            ln_dve(dve, core, s, 1, 1, copied)
            dve.wait_ge(router_loaded.sem, 32)

            def route(c, u, more=True):
                if more:
                    ln_dve(dve, core, s, c + 2, u, copied)
                dve.wait_ge(routed.sem, routed.past(c))
                dve.tensor_tensor(rows(logits, c * CT, CT), yp[:, 0:CT * EXPERTS].rearrange("p (t e) -> p t e", e=EXPERTS),
                                  rb[:, :].unsqueeze(1).to_broadcast([P, CT, EXPERTS]), ALU.add).then_inc(logits_kept.sem, 1)

            each_pair(dve, 0, CHUNKS - 2, route)
            route(CHUNKS - 2, 0, False)
            route(CHUNKS - 1, 1, False)
            dve.drain()
            dve.wait_ge(filled.sem, 1)
            dve.tensor_copy(rev[:, :], rev_i[:, :])
            dve.tensor_copy(first[:, :], first_i[:, :])
            dve.tensor_reduce(best[:, :], logits[:, :, :], AX.X, ALU.max)
            dve.drain()

            def by_tile(v):
                return v[:, :].unsqueeze(2).to_broadcast([P, TILES, EXPERTS])

            def by_expert(v, n, last):
                return v[:, :].unsqueeze(1 if last else 2).to_broadcast([P, n, EXPERTS] if last else [P, EXPERTS, n])

            dve.tensor_tensor(hot[:, :, :], logits[:, :, :], by_tile(best), ALU.is_equal)
            dve.drain()
            dve.tensor_tensor(hot[:, :, :], hot[:, :, :], by_expert(rev, TILES, True), ALU.mult)
            dve.drain()
            dve.tensor_reduce(best[:, :], hot[:, :, :], AX.X, ALU.max)
            dve.drain()
            dve.tensor_tensor(hot[:, :, :], by_tile(best), by_expert(rev, TILES, True), ALU.is_equal).then_inc(hot_ready.sem, 1)
            dve.wait_ge(counted.sem, 1)
            dve.tensor_copy(tot[:, :, :], hg[:, 0, 0:TILES * EXPERTS].rearrange("p (t e) -> p e t", e=EXPERTS))
            dve.drain()
            flat = lambda t: t[:, :, :].rearrange("p a b -> p (a b)")
            dve.tensor_tensor_scan(flat(run), flat(tot), flat(zero), 0.0, ALU.add, ALU.add)
            dve.memset(start[:, 0:1], 0.0)
            dve.drain()
            dve.tensor_copy(start[:, 1:EXPERTS], run[:, 0:EXPERTS - 1, TILES - 1])
            dve.drain()
            dve.tensor_tensor(padded[:, :], run[:, :, TILES - 1], start[:, :], ALU.subtract)
            dve.drain()
            dve.tensor_scalar(padded_i[:, :], padded[:, :], float(P - 1), None, ALU.add)
            dve.drain()
            dve.tensor_scalar(padded_i[:, :], padded_i[:, :], -P, None, ALU.bitwise_and)
            dve.drain()
            dve.tensor_copy(padded[:, :], padded_i[:, :])
            dve.drain()
            dve.tensor_tensor_scan(pad_end[:, :], padded[:, :], zero[:, 0, 0:EXPERTS], 0.0, ALU.add, ALU.add)
            dve.drain()
            dve.tensor_tensor(padded[:, :], pad_end[:, :], padded[:, :], ALU.subtract)
            dve.drain()
            dve.tensor_tensor(padded[:, :], padded[:, :], start[:, :], ALU.subtract)
            dve.tensor_tensor(run[:, :, :], run[:, :, :], tot[:, :, :], ALU.subtract)
            dve.drain()
            dve.tensor_tensor(run[:, :, :], run[:, :, :], by_expert(padded, TILES, False), ALU.add)
            dve.drain()
            dve.tensor_tensor(run[:, :, :], run[:, :, :], ha[:, 0, 0:TILES * EXPERTS].rearrange("p (t e) -> p e t", e=EXPERTS), ALU.add)
            dve.drain()
            dve.tensor_tensor(hot[:, :, :], hot[:, :, :], run[:, :, :].rearrange("p e t -> p t e"), ALU.mult)
            dve.drain()
            dve.tensor_reduce(pos[:, :], hot[:, :, :], AX.X, ALU.add)
            dve.drain()
            dve.tensor_copy(pos_i[:, :], pos[:, :]).then_inc(pos_ready.sem, 1)
            dve.tensor_tensor(later[:, :, :], first[:, :].unsqueeze(2).to_broadcast([P, SLOTS, EXPERTS]),
                              by_expert(pad_end, SLOTS, True), ALU.is_ge)
            dve.drain()
            dve.tensor_reduce(owner[:, :], later[:, :, :], AX.X, ALU.add)
            dve.drain()
            dve.tensor_scalar(owner_i[:, :], owner[:, :], float(EXPERTS - 1), None, ALU.min).then_inc(owner_ready.sem, 1)
            dve.wait_ge(owner_ready.sem, 1)
            dve.wait_ge(halved.sem, 1)

            def bias(i, u):
                e = dve.value_load(owner_i[0:1, bass.ds(i, 1)], min_val=0, max_val=EXPERTS - 1)
                dve.wait_ge(h_done.sem, h_done.past(i))
                dve.tensor_tensor(gb[:, u, :], hg[:, u, :], b1[:, bass.ds(e, 1), HID:WIDE], ALU.add)
                dve.tensor_tensor(ab[:, u, :], ha[:, u, :], b1[:, bass.ds(e, 1), 0:HID], ALU.add).then_inc(biased.sem, 1)

            def gate(i, u):
                dve.wait_ge(sig_done.sem, sig_done.past(i))
                dve.tensor_tensor(hs[:, u, :], ab[:, u, :], gb[:, u, :], ALU.mult).then_inc(gated.sem, 1)

            def keep(i):
                e = dve.value_load(owner_i[0:1, bass.ds(i, 1)], min_val=0, max_val=EXPERTS - 1)
                dve.wait_ge(y_done.sem, y_done.past(i))
                dve.tensor_tensor(pad[:, bass.ds(i, 1), 0:D], yp[:, 0:P], b2[:, bass.ds(e, 1), :], ALU.add).then_inc(y_kept.sem, 1)

            bias(0, 0)
            gate(0, 0)

            def body(i, u, before, after):
                if after:
                    bias(i + 1, 1 - u)
                if before:
                    keep(i - 1)
                if after:
                    gate(i + 1, 1 - u)

            run_slots(dve, body)
            keep(SLOTS - 1)
            for q in range(4):
                dve.wait_ge(loaded_back[q].sem, 16)
                for c in (2 * q, 2 * q + 1):
                    xc = rows(core.x, c * CT, CT)
                    dve.tensor_tensor(xc, xc, rows(core.all_xn, c * CT, CT), ALU.add)
                    dve.drain()
                    new_sums_dve(dve, core, c)

        @block.scalar
        def _(act):
            each_pair(act, 0, CHUNKS, lambda c, u: ln_act(act, core, s, c, u))

            def fill_xs(i, u):
                act.wait_ge(xt_done.sem, xt_done.past(i - 2))
                act.activation(xs[:, u, :], sent[:, bass.ds(i, 1), 0:D], ACT.Copy).then_inc(xs_ready.sem, 1)

            def keep_xst(i, u):
                act.wait_ge(xt_done.sem, xt_done.past(i))
                act.activation(xst[:, u, :], xt, ACT.Copy).then_inc(xst_kept.sem, 1)

            def gate(i, u):
                act.wait_ge(biased.sem, biased.past(i))
                act.activation(gb[:, u, :], gb[:, u, :], ACT.Sigmoid).then_inc(sig_done.sem, 1)

            act.wait_ge(w_loaded.sem, 16 * (2 + 2 * EXPERTS))
            act.activation(w2[:, :, :, :], w2[:, :, :, :], ACT.Copy, scale=0.5)
            act.activation(b2[:, :, :], b2[:, :, :], ACT.Copy, scale=0.5).then_inc(halved.sem, 1)
            act.wait_ge(sorted_loaded[0].sem, 16)
            fill_xs(0, 0)
            fill_xs(1, 1)
            keep_xst(0, 0)
            fill_xs(2, 0)
            keep_xst(1, 1)
            gate(0, 0)

            def body(i, u, before, after):
                if before == 1:
                    act.wait_ge(sorted_loaded[1].sem, 64)
                if after > 2:
                    fill_xs(i + 3, 1 - u)
                if after > 1:
                    keep_xst(i + 2, u)
                if after:
                    gate(i + 1, 1 - u)
                act.wait_ge(ht_done.sem, ht_done.past(i))
                act.activation(ht[:, u, :, :], htp[:, u, :, :], ACT.Copy).then_inc(ht_kept.sem, 1)

            run_slots(act, body)
        @block.tensor
        def _(pe):
            ln_pe(pe, core, s, 0, 0)
            pe.wait_ge(router_loaded.sem, 32)

            def route(c, u, more=True):
                if more:
                    ln_pe(pe, core, s, c + 1, 1 - u)
                pe.wait_ge(s.xnt_ready.sem, s.xnt_ready.past(c))
                pe.wait_ge(logits_kept.sem, logits_kept.past(c - 1))
                for j in range(CT):
                    last = pe.matmul(yp[:, j * EXPERTS:(j + 1) * EXPERTS], core.xnt[:, u, j * P:(j + 1) * P], wr[:, :],
                                     start=True, stop=True)
                last.then_inc(routed.sem, 1)

            each_pair(pe, 0, CHUNKS - 2, route)
            route(CHUNKS - 2, 0)
            route(CHUNKS - 1, 1, False)
            pe.wait_ge(filled.sem, 1)
            pe.wait_ge(hot_ready.sem, 1)
            hot_flat = hot[:, :, :].rearrange("p t e -> p (t e)")
            pe.matmul(ha[:, 0, 0:TILES * EXPERTS], earlier[:, :], hot_flat, start=True, stop=True)
            pe.matmul(hg[:, 0, 0:TILES * EXPERTS], ones[:, :], hot_flat, start=True, stop=True).then_inc(counted.sem, 1)
            pe.wait_ge(owner_ready.sem, 1)
            pe.wait_ge(halved.sem, 1)

            def turn(i, u):
                pe.wait_ge(xs_ready.sem, xs_ready.past(i))
                pe.wait_ge(xst_kept.sem, xst_kept.past(i - 1))
                pe.transpose(xt, xs[:, u, 0:D], core.ident[:, :]).then_inc(xt_done.sem, 1)

            def up(i, u):
                e = pe.value_load(owner_i[0:1, bass.ds(i, 1)], min_val=0, max_val=EXPERTS - 1)
                pe.wait_ge(xst_kept.sem, xst_kept.past(i))
                pe.wait_ge(biased.sem, biased.past(i - 2))
                pe.matmul(hg[:, u, :], xst[:, u, :], w1[:, bass.ds(e, 1), HID:WIDE], start=True, stop=True)
                pe.matmul(ha[:, u, :], xst[:, u, :], w1[:, bass.ds(e, 1), 0:HID], start=True, stop=True).then_inc(h_done.sem, 1)

            def down(i, u):
                e = pe.value_load(owner_i[0:1, bass.ds(i, 1)], min_val=0, max_val=EXPERTS - 1)
                pe.wait_ge(ht_kept.sem, ht_kept.past(i))
                pe.wait_ge(y_kept.sem, y_kept.past(i - 1))
                for f in range(HB):
                    last = pe.matmul(yp[:, 0:P], ht[:, u, f, :], w2[:, bass.ds(e, 1), f, :], start=f == 0, stop=f == HB - 1)
                last.then_inc(y_done.sem, 1)

            turn(0, 0)
            turn(1, 1)
            up(0, 0)

            def body(i, u, before, after):
                if after > 1:
                    turn(i + 2, u)
                if after:
                    up(i + 1, 1 - u)
                if before:
                    down(i - 1, 1 - u)
                pe.wait_ge(gated.sem, gated.past(i))
                pe.wait_ge(ht_kept.sem, ht_kept.past(i - 2))
                for f in range(HB):
                    last = pe.transpose(htp[:, u, f, :], hs[:, u, f * P:(f + 1) * P], core.ident[:, :])
                last.then_inc(ht_done.sem, 1)

            run_slots(pe, body)
            down(SLOTS - 1, 1)



def l0_attn(core):
    nc, w = core.nc, core.w
    NT = N // P
    TERMS = 3
    STEPS = NT * GROUPS
    LAG = 2
    BLOCK = TERMS * DH
    ROWS = TERMS * BLOCK
    HALF = HEADS // 2
    VW = HALF * HW
    RING = 4
    T_STATE, T_V, T_K, T_TURN, T_KN, T_TURN2, T_LN, T_OUT, T_Q = 1, 2, 2, 3, 4, 5, 6, 7, 7
    with stage(nc) as s:
        ln_signals(s, 1)
        wm = {m: s.sb(f"w_{m}", [P, P]) for m in ("wq", "wk", "wv", "wo")}
        bq, bk = s.sb("bq", [P, 1]), s.sb("bk", [P, 1])
        bv, bo = s.sb("bv", [P, P]), s.sb("bo", [P, P])
        causal = s.sb("causal", [P, P])
        block_mask = s.sb("block_mask", [P, HEADS, HW])
        zero = s.sb("zero", [P, 1])
        low = s.sb("low", [P, 2, CW])
        kt = s.sb("kt", [P, CW])
        qt = s.sb("qt", [P, 2, CW])
        left = s.sb("left", [P, 2, CW])
        parts = s.sb("parts", [P, 2, TERMS, CW], BF16)
        kx = s.sb("kx", [ROWS, 2, HEADS, CW], BF16)
        qx = s.sb("qx", [ROWS, 2, HEADS, CW], BF16)
        kn = s.sb("kn", [P, 2, CT, P])
        vz = s.sb("vz", [P, 2, CT, 2, HALF, VW + HW])
        att = s.sb("att", [P, RING, GROUPS, P])
        state = s.sb("state", [P, HEADS, HW])
        oc = s.sb("oc", [VW, 2, N])
        den = s.sb("den", [P, NT, HEADS])
        o = s.sb("o", [P, NT, P])
        ot = s.sb("ot", [P, NT, P])
        pj = s.ps("pj", [P, 2, CW])
        sc = s.ps("sc", [P, 2, GROUPS, P])
        ob = s.ps("ob", [P, 2, CW])
        mb = s.ps("mb", [P, 2, NT * P])
        mt = s.tp[:, 0, 0:NT * HEADS * HW].rearrange("p (t h e) -> p t h e", t=NT, h=HEADS)
        st = s.tp[:, 0, 0:HEADS * HW].rearrange("p (h e) -> p h e", h=HEADS)
        w_loaded = s.sig("w_loaded")
        filled = s.sig("filled")
        cleared = s.sig("cleared")
        projected = s.sig("projected")
        low_ready = s.sig("low_ready")
        low_exp = s.sig("low_exp")
        feature_ready = s.sig("feature_ready")
        split_step = s.sig("split_step")
        split_done = s.sig("split_done", 4)
        parts_stored = [s.sig(f"parts_stored{n}", 16) for n in range(2)]
        kq_loaded = [s.sig(f"kq_loaded{u}") for u in range(2)]
        v_kept = s.sig("v_kept", 1)
        kn_kept = s.sig("kn_kept", 1)
        state_done = s.sig("state_done")
        state_kept = s.sig("state_kept")
        sc_done = s.sig("sc_done")
        att_ready = s.sig("att_ready", 2)
        av_done = s.sig("av_done", RING)
        ob_kept = s.sig("ob_kept", 2)
        o_turned = s.sig("o_turned", 1)
        o_ready = s.sig("o_ready", 2)
        o_turned2 = s.sig("o_turned2")
        ot_kept = s.sig("ot_kept")
        y_done = s.sig("y_done")
        x_added = s.sig("x_added", 2)
        s.ready()
        LOADS = 2 * TERMS * TERMS
        block = s.ctx.enter_context(nc.Block())

        @block.sync
        def _(sp):
            for m, t in wm.items():
                sp.dma_start(t[:, :], w[f"L0_attn_{m}"]).then_inc(w_loaded.sem, 16)
            for t, m in ((bq, "bq"), (bk, "bk")):
                sp.dma_start(t[:, :], w[f"L0_attn_{m}"].rearrange("(p a) -> p a", a=1)).then_inc(w_loaded.sem, 16)
            for t, m in ((bv, "bv"), (bo, "bo")):
                sp.dma_start(t[:, :], w[f"L0_attn_{m}"].partition_broadcast(P)).then_inc(w_loaded.sem, 16)

            def move(c, u, free=True):
                for n in range(2):
                    sp.wait_ge(split_done.sem, split_done.past(2 * c + n))
                    sp.dma_start(core.parts_dram[u, n].rearrange("a f t -> f a t"), parts[:, n, :, :]).then_inc(parts_stored[n].sem, 16)
                if free:
                    sp.wait_ge(sc_done.sem, sc_done.past(2 * STEPS * (c - 1) - 1))
                for n in range(2):
                    sp.wait_ge(parts_stored[n].sem, 32 + 16 * c)
                for a in range(TERMS):
                    for b in range(TERMS):
                        at = a * BLOCK + b * DH
                        for n, (t, part) in enumerate(((kx, a), (qx, b))):
                            sp.dma_start(t[at:at + DH, u, :, :],
                                         core.parts_dram[u, n, part].rearrange("(h d) t -> d h t", d=DH)).then_inc(kq_loaded[u].sem, 16)

            move(0, 0, False)
            move(1, 1, False)
            with sp.Fori(1, CHUNKS // 2) as pair:
                for u in range(2):
                    move(pair * 2 + u, u)

        @block.gpsimd
        def _(pool):
            ln_scales_pool(pool, core, s, range(2))
            pool.memset(causal[:, :], 1.0).then_inc(cleared.sem, 1)
            pool.memset(block_mask[:, :, :], 1.0).then_inc(cleared.sem, 1)
            pool.memset(vz[:, :, :, :, :, :], 0.0).then_inc(cleared.sem, 1)
            pool.memset(zero[:, :], 0.0).then_inc(cleared.sem, 1)
            pool.wait_ge(cleared.sem, 4)
            pool.affine_select(out=causal[:, :], in_=causal[:, :], compare_op=ALU.is_ge, fill=0.0,
                               base=0, pattern=[[1, P]], channel_multiplier=-1).then_inc(filled.sem, 1)
            pool.affine_select(out=block_mask[:, :, :], in_=block_mask[:, :, :], compare_op=ALU.is_ge, fill=0.0,
                               base=0, pattern=[[-DH, HEADS], [0, HW]], channel_multiplier=1).then_inc(cleared.sem, 1)
            pool.wait_ge(cleared.sem, 5)
            pool.affine_select(out=block_mask[:, :, :], in_=block_mask[:, :, :], compare_op=ALU.is_ge, fill=0.0,
                               base=DH - 1, pattern=[[DH, HEADS], [0, HW]], channel_multiplier=-1).then_inc(filled.sem, 1)
            pool.memset(vz[:, :, :, :, :, :].rearrange("p u j a h c -> p (u j a) (h c)").rearrange("p b (h c) -> p b h c", h=HALF)[:, :, :, DH:HW],
                        1.0).then_inc(filled.sem, 1)

            ln_scales_pool(pool, core, s, range(2, CHUNKS))

            def split(c, u):
                nothing = zero[:, :].to_broadcast([P, CW])
                for n, t in enumerate((kt[:, :], qt[:, u, :])):
                    at = 2 * (c - 2) + n
                    pool.wait_ge(feature_ready.sem, feature_ready.past(2 * c + n))
                    pool.wait_ge(parts_stored[n].sem, 16 + 16 * c)
                    pool.tensor_tensor(parts[:, n, 0, :], t, nothing, ALU.add).then_inc(split_step.sem, 1)
                    pool.wait_ge(split_step.sem, split_step.past(3 * at))
                    pool.tensor_tensor(left[:, n, :], t, parts[:, n, 0, :], ALU.subtract).then_inc(split_step.sem, 1)
                    pool.wait_ge(split_step.sem, split_step.past(3 * at + 1))
                    pool.tensor_tensor(parts[:, n, 1, :], left[:, n, :], nothing, ALU.add).then_inc(split_step.sem, 1)
                    pool.wait_ge(split_step.sem, split_step.past(3 * at + 2))
                    pool.tensor_tensor(parts[:, n, 2, :], left[:, n, :], parts[:, n, 1, :], ALU.subtract).then_inc(split_done.sem, 1)

            each_pair(pool, 2, CHUNKS, split)

        @block.vector
        def _(dve):
            def feature(c, u, n):
                bias, t = ((bk, kt[:, :]), (bq, qt[:, u, :]))[n]
                dve.wait_ge(split_done.sem, split_done.past(2 * c - 4 + n if n else 2 * c - 2))
                dve.wait_ge(projected.sem, projected.past(4 * c + n))
                dve.tensor_scalar(low[:, n, :], pj[:, n, :], bias[:, :], 0.0, ALU.add, ALU.min).then_inc(low_ready.sem, 1)
                dve.tensor_scalar(t, pj[:, n, :], bias[:, :], 0.0, ALU.add, ALU.max)
                dve.drain()
                dve.wait_ge(low_exp.sem, low_exp.past(2 * c + n))
                dve.tensor_tensor(t, t, low[:, n, :], ALU.add).then_inc(feature_ready.sem, 1)

            def split(c, u, n):
                t = (kt[:, :], qt[:, u, :])[n]
                dve.wait_ge(parts_stored[n].sem, 16 + 16 * c)
                dve.drain()
                dve.tensor_copy(parts[:, n, 0, :], t)
                dve.drain()
                dve.tensor_tensor(left[:, n, :], t, parts[:, n, 0, :], ALU.subtract)
                dve.drain()
                dve.tensor_copy(parts[:, n, 1, :], left[:, n, :])
                dve.drain()
                dve.tensor_tensor(parts[:, n, 2, :], left[:, n, :], parts[:, n, 1, :], ALU.subtract).then_inc(split_done.sem, 1)

            def keep_v(c, u):
                dve.wait_ge(projected.sem, projected.past(4 * c + 2))
                for j in range(CT):
                    last = dve.tensor_tensor(vz[:, u, j, :, :, 0:DH], pj[:, 0, j * P:(j + 1) * P].rearrange("p (a h e) -> p a h e", a=2, h=HALF),
                                             bv[:, :].rearrange("p (a h e) -> p a h e", a=2, h=HALF), ALU.add)
                last.then_inc(v_kept.sem, 1)

            def mask_scores(b, n):
                dve.wait_ge(sc_done.sem, sc_done.past(STEPS * b + n))
                dve.wait_ge(av_done.sem, av_done.past(STEPS * b + n - RING))
                dve.tensor_tensor(att[:, n % RING, :, :], sc[:, n % 2, :, :],
                                  causal[:, :].unsqueeze(1).to_broadcast([P, GROUPS, P]), ALU.mult).then_inc(att_ready.sem, 1)

            def keep_state(b):
                dve.wait_ge(state_done.sem, state_done.past(b))
                dve.tensor_tensor(state[:, :, :], st, block_mask[:, :, :], ALU.mult).then_inc(state_kept.sem, 1)

            def normalise(b):
                dve.wait_ge(o_turned.sem, o_turned.past(b))
                dve.tensor_scalar(den[:, :, :], mt[:, :, :, DH], 1e-6, None, ALU.add)
                dve.drain()
                dve.reciprocal(den[:, :, :], den[:, :, :])
                dve.drain()
                for t in range(NT):
                    last = dve.tensor_tensor(o[:, t, :].rearrange("p (h e) -> p h e", h=HEADS), mt[:, t, :, 0:DH],
                                             den[:, t, :].unsqueeze(2).to_broadcast([P, HEADS, DH]), ALU.mult)
                last.then_inc(o_ready.sem, 1)

            def add(b):
                xs = rows(core.x, b * NT, NT)
                dve.tensor_tensor(xs, xs, bo[:, :].unsqueeze(1).to_broadcast([P, NT, P]), ALU.add)
                dve.drain()
                dve.wait_ge(y_done.sem, y_done.past(b))
                dve.tensor_tensor(xs, xs, mb[:, 1, :].rearrange("p (t e) -> p t e", t=NT), ALU.add).then_inc(x_added.sem, 1)
                dve.drain()
                for t in range(NT):
                    dve.bn_stats(core.sums[:, bass.ds(b * NT + t, 1), :], core.x[:, bass.ds(b * NT + t, 1), :])

            ln_scales_dve(dve, core, s)
            ln_dve(dve, core, s, 0, 0)
            dve.wait_ge(w_loaded.sem, 128)
            for n in range(2):
                feature(0, 0, n)
                split(0, 0, n)
            dve.wait_ge(filled.sem, filled.past(2))
            keep_v(0, 0)
            ln_dve(dve, core, s, 1, 1)
            for n in range(2):
                feature(1, 1, n)
                split(1, 1, n)

            def body(c, u, before, after):
                for i in range(2):
                    b = 2 * c + i
                    prev = i or before
                    for n in range(STEPS):
                        mask_scores(b, n)
                        if n == T_STATE:
                            keep_state(b)
                        if n == T_V and i == 0 and after:
                            keep_v(c + 1, 1 - u)
                        if n == T_K and i == 1 and after > 1:
                            feature(c + 2, u, 0)
                        if n == T_TURN and prev:
                            normalise(b - 1)
                        if n == T_KN and i == 0 and after > 1:
                            ln_dve(dve, core, s, c + 2, u)
                        if n == T_OUT and prev:
                            add(b - 1)
                        if n == T_Q and i == 1 and after > 1:
                            feature(c + 2, u, 1)

            each_chunk(dve, body)
            normalise(2 * CHUNKS - 1)
            add(2 * CHUNKS - 1)

        @block.scalar
        def _(act):
            def low_part(c, n):
                act.wait_ge(low_ready.sem, low_ready.past(2 * c + n))
                act.activation(low[:, n, :], low[:, n, :], ACT.Exp).then_inc(low_exp.sem, 1)

            def keep_kn(c, u):
                act.wait_ge(projected.sem, projected.past(4 * c + 3))
                act.activation(kn[:, u, :, :], pj[:, 1, :].rearrange("p (t e) -> p t e", t=CT), ACT.Copy).then_inc(kn_kept.sem, 1)

            def keep_ob(b, half):
                act.wait_ge(av_done.sem, av_done.past(STEPS * b + GROUPS + 2 * half + 1))
                act.wait_ge(o_turned.sem, o_turned.past(b - 1))
                act.activation(oc[:, half, :], ob[0:VW, half, 0:N], ACT.Copy).then_inc(ob_kept.sem, 1)

            def keep_ot(b):
                act.wait_ge(o_turned2.sem, o_turned2.past(b))
                act.activation(ot[:, :, :], mb[:, 0, :].rearrange("p (t e) -> p t e", t=NT), ACT.Copy).then_inc(ot_kept.sem, 1)

            ln_act(act, core, s, 0, 0)
            low_part(0, 0)
            low_part(0, 1)
            keep_kn(0, 0)
            ln_act(act, core, s, 1, 1)
            low_part(1, 0)
            low_part(1, 1)

            def body(c, u, before, after):
                for i in range(2):
                    b = 2 * c + i
                    prev = i or before
                    if prev:
                        keep_ob(b - 1, 1)
                    if i == 1 and after > 1:
                        low_part(c + 2, 0)
                    if i == 0 and after:
                        keep_kn(c + 1, 1 - u)
                    if prev:
                        keep_ot(b - 1)
                    if i == 0 and after > 1:
                        ln_act(act, core, s, c + 2, u)
                    keep_ob(b, 0)
                    if i == 1 and after > 1:
                        low_part(c + 2, 1)

            each_chunk(act, body)
            keep_ob(2 * CHUNKS - 1, 1)
            keep_ot(2 * CHUNKS - 1)

        @block.tensor
        def _(pe):
            def project(c, u, n):
                bank = n % 2
                if n == 0:
                    pe.wait_ge(s.xnt_ready.sem, s.xnt_ready.past(c))
                    pe.wait_ge(v_kept.sem, v_kept.past(c - 1))
                    last = pe.matmul(pj[:, 0, :], wm["wk"][:, :], core.xnt[:, u, :], start=True, stop=True)
                elif n == 1:
                    pe.wait_ge(kn_kept.sem, kn_kept.past(c - 1))
                    last = pe.matmul(pj[:, 1, :], wm["wq"][:, :], core.xnt[:, u, :], start=True, stop=True)
                elif n == 2:
                    pe.wait_ge(feature_ready.sem, feature_ready.past(2 * c))
                    for j in range(CT):
                        last = pe.matmul(pj[:, 0, j * P:(j + 1) * P], core.xnt[:, u, j * P:(j + 1) * P], wm["wv"][:, :],
                                         start=True, stop=True)
                else:
                    pe.wait_ge(feature_ready.sem, feature_ready.past(2 * c + 1))
                    for j in range(CT):
                        last = pe.transpose(pj[:, 1, j * P:(j + 1) * P], kt[:, j * P:(j + 1) * P], core.ident[:, :])
                last.then_inc(projected.sem, 1)

            def scores(b, u, i, n):
                t, g = n // GROUPS, n % GROUPS
                cols = slice((i * NT + t) * P, (i * NT + t + 1) * P)
                pe.wait_ge(att_ready.sem, att_ready.past(STEPS * b + n - 2))
                for a in range(GROUPS):
                    h = g * GROUPS + a
                    last = pe.matmul(sc[:, n % 2, a, :], kx[:, u, h, cols], qx[:, u, h, cols], start=True, stop=True)
                last.then_inc(sc_done.sem, 1)

            def first_state(b, c, u, i, after):
                if i == 0:
                    pe.wait_ge(kn_kept.sem, kn_kept.past(c))
                    pe.wait_ge(v_kept.sem, v_kept.past(c))
                    if after:
                        pe.wait_ge(s.xnt_ready.sem, s.xnt_ready.past(c + 1))
                elif after > 1:
                    pe.wait_ge(s.xnt_ready.sem, s.xnt_ready.past(c + 2))
                pe.wait_ge(o_ready.sem, o_ready.past(b - 2))
                pe.matmul(st, kn[:, u, NT * i, :], vz[:, u, NT * i, :, :, :].rearrange("p a h c -> p a (h c)").rearrange(
                    "p a (h c) -> p a h c", h=HALF)[:, :, :, 0:HW], start=True, stop=True).then_inc(state_done.sem, 1)

            def values(b, u, i, n):
                t, g = n // GROUPS, n % GROUPS
                half, first = g // 2, g % 2 == 0
                if t == 0 and first:
                    pe.wait_ge(ob_kept.sem, ob_kept.past(2 * b + half - 2))
                j = i * NT + t
                if t == 1 and g == 0:
                    pe.wait_ge(state_kept.sem, state_kept.past(b))
                    for a in range(2):
                        pe.matmul(ob[0:VW, a, P:2 * P], state[:, a * HALF:(a + 1) * HALF, :].rearrange("p h e -> p (h e)"),
                                  qt[:, u, j * P:(j + 1) * P], start=True, stop=False, skip_group_check=True)
                pe.wait_ge(att_ready.sem, att_ready.past(STEPS * b + n))
                for a in range(GROUPS):
                    own = (g * GROUPS + a) % HALF
                    cols = vz[:, u, j, half, :, :].rearrange("p h c -> p (h c)")[:, own * VW:(own + 1) * VW]
                    last = pe.matmul(ob[0:VW, half, t * P:(t + 1) * P], cols, att[:, n % RING, a, :],
                                     start=t == 0 and first and a == 0, stop=not first and a == GROUPS - 1, skip_group_check=True)
                last.then_inc(av_done.sem, 1)

            def turn(b):
                pe.wait_ge(ob_kept.sem, ob_kept.past(2 * b + 1))
                for t in range(NT):
                    for half in range(2):
                        last = pe.transpose(mt[:, t, half * HALF:(half + 1) * HALF, :].rearrange("p h e -> p (h e)"),
                                            oc[:, half, t * P:(t + 1) * P], core.ident[0:VW, 0:VW])
                last.then_inc(o_turned.sem, 1)

            def turn2(b):
                pe.wait_ge(o_ready.sem, o_ready.past(b))
                pe.wait_ge(x_added.sem, x_added.past(b - 1))
                for t in range(NT):
                    last = pe.transpose(mb[:, 0, t * P:(t + 1) * P], o[:, t, :], core.ident[:, :])
                last.then_inc(o_turned2.sem, 1)

            def out_product(b):
                pe.wait_ge(ot_kept.sem, ot_kept.past(b))
                for t in range(NT):
                    last = pe.matmul(mb[:, 1, t * P:(t + 1) * P], ot[:, t, :], wm["wo"][:, :], start=True, stop=True)
                last.then_inc(y_done.sem, 1)

            ln_pe(pe, core, s, 0, 0)
            pe.wait_ge(w_loaded.sem, 128)
            for n in range(4):
                project(0, 0, n)
            ln_pe(pe, core, s, 1, 1)
            project(1, 1, 0)
            project(1, 1, 1)
            pe.wait_ge(filled.sem, filled.past(2))

            def body(c, u, before, after):
                for i in range(2):
                    b = 2 * c + i
                    prev = i or before
                    for n in range(STEPS):
                        if n == 0 and i == 0:
                            pe.wait_ge(kq_loaded[u].sem, ((c - u) * 8 + 16) * LOADS)
                        if n == T_STATE:
                            first_state(b, c, u, i, after)
                        if i == 0 and after:
                            if n == T_V:
                                project(c + 1, 1 - u, 2)
                            if n == T_KN:
                                project(c + 1, 1 - u, 3)
                        if i == 1 and after > 1:
                            if n == T_K:
                                project(c + 2, u, 0)
                            if n == T_Q:
                                project(c + 2, u, 1)
                        if prev:
                            if n == T_TURN:
                                pe.wait_ge(state_kept.sem, state_kept.past(b))
                                turn(b - 1)
                            if n == T_TURN2:
                                turn2(b - 1)
                            if n == T_OUT:
                                out_product(b - 1)
                        if n == T_LN and i == 0 and after > 1:
                            if prev:
                                pe.wait_ge(o_ready.sem, o_ready.past(b - 1))
                            else:
                                pe.wait_ge(state_kept.sem, state_kept.past(b))
                            ln_pe(pe, core, s, c + 2, u)
                        scores(b, u, i, n)
                        if n >= LAG:
                            values(b, u, i, n - LAG)
                        elif i == 1:
                            values(b - 1, u, 0, n - LAG + STEPS)
                        elif before:
                            values(b - 1, 1 - u, 1, n - LAG + STEPS)

            each_chunk(pe, body)
            last_b = 2 * CHUNKS - 1
            for n in range(STEPS - LAG, STEPS):
                values(last_b, 1, 1, n)
            turn(last_b)
            turn2(last_b)
            out_product(last_b)



def l1_ffn(core):
    nc, w = core.nc, core.w
    EXPERTS, _, F = w["L1_ffn_w_gate"].shape
    CAP = 64
    PAIRS = EXPERTS // 2
    TOP = 8
    RING = 4
    HALF = TILES // 2
    ROUNDS = CAP // TOP
    LOW = -3.0e38
    with stage(nc) as s:
        ln_signals(s, 1)
        wr_raw = s.sb("wr_raw", [EXPERTS, D])
        wr = s.sb("wr", [P, EXPERTS])
        wsgu = s.sb("wsgu", [P, 2 * F])
        wsd = s.sb("wsd", [F, P])
        tok_i = s.sb("tok_i", [P, TILES], mybir.dt.int32)
        order = s.sb("order", [P, TILES])
        part_i = s.sb("part_i", [P, 1], mybir.dt.int32)
        part = s.sb("part", [P, 1])
        upper = s.sb("upper", [P, 1])
        slot = s.sb("slot", [P, 1])
        region = s.sb("region", [P, 1])
        zero = s.sb("zero", [P, CT, 2 * D])
        lr = s.sb("lr", [P, CT, EXPERTS])
        top = s.sb("top", [P, CT, TOP])
        rest = s.sb("rest", [P, CT, EXPERTS])
        wts = s.sb("wts", [P, TILES, EXPERTS])
        mask = s.sb("mask", [P, TILES, EXPERTS])
        keys = s.sb("keys", [P, HALF, 2, EXPERTS])
        wsum = s.sb("wsum", [P, TILES])
        sg = s.sb("sg", [F, CW])
        hsh = s.sb("hsh", [F, 2, CW])
        keyt = s.sb("keyt", [P, HALF * P])
        found = s.sb("found", [P, CAP])
        both = s.sb("both", [EXPERTS, 2 * CAP])
        firsts = s.sb("firsts", [EXPERTS, 3 * CAP])
        token = s.sb("token", [P, PAIRS])
        empty = s.sb("empty", [P, PAIRS])
        from_i = s.sb("from_i", [P, PAIRS], U32)
        to_i = s.sb("to_i", [P, PAIRS], U32)
        wg = s.sb("wg", [P, RING, 2, F])
        wu = s.sb("wu", [P, RING, 2, F])
        wd = s.sb("wd", [F, RING, 2, P])
        xg = s.sb("xg", [P, RING, D + EXPERTS])
        xgt = s.sb("xgt", [P, 2, P])
        gs = s.sb("gs", [F, 2, P])
        hp = s.sb("hp", [F, 2, 2 * P])
        yo = s.sb("yo", [P, RING, D])
        acc_b = s.sb("acc_b", [P, TILES, D])
        gu = s.ps("gu", [P, 2, CW])
        ly = s.ps("ly", [P, 2, CW])
        kt = s.ps("kt", [P, 2, CW])
        lg, ysh = ly[:, 0, 0:CT * EXPERTS], ly[:, 1, :]
        w_loaded = s.sig("w_loaded")
        filled = s.sig("filled")
        hp_clear = s.sig("hp_clear")
        zeroed = s.sig("zeroed")
        wr_turned = s.sig("wr_turned")
        wr_kept = s.sig("wr_kept")
        copied = s.sig("copied", 2)
        routed = s.sig("routed")
        logits_kept = s.sig("logits_kept", 1)
        shared_up = s.sig("shared_up")
        silu_done = s.sig("silu_done", 1)
        shared_h = s.sig("shared_h", 1)
        shared_y = s.sig("shared_y")
        shared_added = s.sig("shared_added", 1)
        chosen = s.sig("chosen")
        exp_done = s.sig("exp_done")
        keys_turned = s.sig("keys_turned")
        keys_kept = s.sig("keys_kept", 2)
        exp_masked = s.sig("exp_masked")
        sums_inverted = s.sig("sums_inverted")
        weighted = s.sig("weighted")
        found_ready = s.sig("found_ready")
        moved = s.sig("moved")
        firsts_ready = s.sig("firsts_ready")
        listed = s.sig("listed")
        index_ready = s.sig("index_ready")
        rows_stored = s.sig("rows_stored")
        ring_loaded = [s.sig(f"ring_loaded{q}") for q in range(RING)]
        added, *xg_loaded = s.pool_dmas(core)[0:1 + RING]
        xt_done = s.sig("xt_done")
        xt_kept = s.sig("xt_kept", 1)
        gu_done = s.sig("gu_done")
        gated = s.sig("gated", 2)
        h_done = s.sig("h_done", 2)
        y_done = s.sig("y_done")
        y_kept = s.sig("y_kept", 2)
        acc_loaded = [s.sig(f"acc_loaded{q}") for q in range(4)]
        s.ready()
        table, sums = core.table_dram, core.acc_dram
        ROWS = TOKENS + CAP
        block = s.ctx.enter_context(nc.Block())

        @block.sync
        def _(sp):
            for t, m in ((wr_raw, "router_w"), (wsgu, "ws_gate_up"), (wsd, "ws_down")):
                sp.dma_start(t[:, :], w[f"L1_ffn_{m}"]).then_inc(w_loaded.sem, 16)

            def load(n, q):
                for t, m in ((wg, "w_gate"), (wu, "w_up"), (wd, "w_down")):
                    sp.dma_start(t[:, q, :, :], w[f"L1_ffn_{m}"].rearrange("(b n) i o -> n i b o", b=2)[bass.ds(n, 1)].rearrange("n i b o -> i (n b) o")).then_inc(ring_loaded[q].sem, 16)

            for q in range(RING):
                load(q, q)
            sp.wait_ge(filled.sem, 3)
            zrows = zero[:, :, :].rearrange("p a (b d) -> p (a b) d", d=D)
            for n in range(TILES // 8):
                sp.dma_start(sums[ROWS + n * 8 * P:ROWS + (n + 1) * 8 * P, :].rearrange("(a p) d -> p a d", p=P), zrows).then_inc(zeroed.sem, 16)
            for region in range(2):
                sp.dma_start(sums[region * ROWS + TOKENS:(region + 1) * ROWS, :], zrows[0:CAP, 0, :]).then_inc(zeroed.sem, 16)
            sp.dma_start(table[TOKENS:ROWS, :], zero[0:CAP, 0, 0:D + EXPERTS]).then_inc(zeroed.sem, 16)
            sp.wait_ge(copied.sem, copied.past(CHUNKS - 1))
            sp.dma_start(table[0:TOKENS, 0:D].rearrange("(t p) d -> p t d", p=P), core.all_xn[:, :, :]).then_inc(rows_stored.sem, 16)
            sp.wait_ge(shared_added.sem, shared_added.past(CHUNKS - 1))
            sp.dma_start(sums[0:TOKENS, :].rearrange("(t p) d -> p t d", p=P), core.x[:, :, :]).then_inc(zeroed.sem, 16)
            sp.wait_ge(weighted.sem, 1)
            with nc.allow_non_contiguous_dma("the weights of a token stand by its row"):
                sp.dma_start(table[0:TOKENS, D:D + EXPERTS].rearrange("(t p) d -> p t d", p=P), wts[:, :, :]).then_inc(rows_stored.sem, 16)

            with sp.Fori(0, PAIRS // RING - 1) as ring:
                for q in range(RING):
                    sp.wait_ge(y_done.sem, y_done.past(ring * RING + q))
                    load(ring * RING + q + RING, q)
            sp.wait_ge(added.sem, 16 * PAIRS)
            for q in range(4):
                for b, t in ((0, core.x), (1, acc_b)):
                    sp.dma_start(t[:, q * 8:(q + 1) * 8, :],
                                 sums[b * ROWS + q * 8 * P:b * ROWS + (q + 1) * 8 * P, :].rearrange("(t p) d -> p t d", p=P)).then_inc(acc_loaded[q].sem, 16)

        @block.gpsimd
        def _(pool):
            ln_scales_pool(pool, core, s, range(2))
            pool.memset(zero[:, :, :], 0.0).then_inc(filled.sem, 1)
            pool.iota(tok_i[:, :], pattern=[[-P, TILES]], base=TOKENS, channel_multiplier=-1).then_inc(filled.sem, 1)
            pool.iota(part_i[:, :], pattern=[[0, 1]], base=0, channel_multiplier=1).then_inc(filled.sem, 1)
            pool.memset(hp[:, :, :], 0.0).then_inc(hp_clear.sem, 1)

            def copy(c, u, more=True):
                if more:
                    ln_scale_pool(pool, core, s, c + 2)
                pool.wait_ge(s.xn_ready.sem, s.xn_ready.past(c))
                pool.tensor_copy(rows(core.all_xn, c * CT, CT), core.xn[:, u, :, :]).then_inc(copied.sem, 1)

            each_pair(pool, 0, CHUNKS - 2, copy)
            copy(CHUNKS - 2, 0, False)
            copy(CHUNKS - 1, 1, False)
            flat = lambda t: t[:, :, :].rearrange("p a b -> p (a b)")
            pool.wait_ge(exp_done.sem, 1)
            pool.tensor_tensor(flat(wts), flat(wts), flat(mask), ALU.mult).then_inc(exp_masked.sem, 1)
            pool.wait_ge(sums_inverted.sem, 1)
            pool.tensor_tensor(wts[:, :, :], wts[:, :, :], wsum[:, :].unsqueeze(2).to_broadcast([P, TILES, EXPERTS]), ALU.mult).then_inc(weighted.sem, 1)
            pool.wait_ge(index_ready.sem, 1)
            pool.wait_ge(rows_stored.sem, 32)
            pool.wait_ge(zeroed.sem, 16 * (TILES // 8 + 4))

            def gather(n):
                if n >= RING:
                    pool.wait_ge(y_kept.sem, y_kept.past(n - RING))
                pool.indirect_dma_start(xg[:, n % RING, :], None, table,
                                        bass.IndirectOffsetOnAxis(ap=from_i[:, n:n + 1], axis=0)).then_inc(xg_loaded[n % RING].sem, 16)

            for n in range(RING):
                gather(n)
            for n in range(PAIRS):
                pool.wait_ge(y_kept.sem, y_kept.past(n))
                if n + RING < PAIRS:
                    gather(n + RING)
                if n > 0:
                    pool.wait_ge(added.sem, 16 * n)
                pool.indirect_dma_start(sums, bass.IndirectOffsetOnAxis(ap=to_i[:, n:n + 1], axis=0),
                                        yo[:, n % RING, :], None, compute_op=ALU.add).then_inc(added.sem, 16)
            for q in range(RING):
                pool.wait_ge(xg_loaded[q].sem, 16 * (PAIRS // RING))
            pool.wait_ge(added.sem, 16 * PAIRS)
            s.reset_pool_dmas(pool)

        @block.vector
        def _(dve):
            ln_scales_dve(dve, core, s)
            ln_dve(dve, core, s, 0, 0, copied)
            ln_dve(dve, core, s, 1, 1, copied)
            dve.wait_ge(filled.sem, 3)
            dve.tensor_copy(order[:, :], tok_i[:, :])
            dve.tensor_copy(part[:, :], part_i[:, :])
            dve.drain()
            dve.tensor_scalar(upper[:, :], part[:, :], float(CAP), None, ALU.is_ge)
            dve.drain()
            dve.scalar_tensor_tensor(slot[:, :], upper[:, :], -float(CAP), part[:, :], ALU.mult, ALU.add)
            dve.tensor_scalar(region[:, :], upper[:, :], float(ROWS), None, ALU.mult)

            def add_shared(c):
                dve.wait_ge(shared_y.sem, shared_y.past(c))
                xc = rows(core.x, c * CT, CT).rearrange("p a b -> p (a b)")
                dve.scalar_tensor_tensor(xc, ysh, 0.5, xc, ALU.mult, ALU.add).then_inc(shared_added.sem, 1)

            def route(c, u, half, more=True, before=True):
                if more:
                    ln_dve(dve, core, s, c + 2, u, copied)
                dve.wait_ge(routed.sem, routed.past(c))
                dve.tensor_copy(lr[:, :, :], lg.rearrange("p (t e) -> p t e", e=EXPERTS)).then_inc(logits_kept.sem, 1)
                dve.drain()
                for j in range(CT):
                    dve.max(top[:, j, :], lr[:, j, :])
                dve.drain()
                for j in range(CT):
                    dve.match_replace(rest[:, j, :], top[:, j, :], lr[:, j, :], LOW)
                dve.tensor_tensor(rows(wts, c * CT, CT), lr[:, :, :], top[:, :, 0:1].to_broadcast([P, CT, EXPERTS]), ALU.subtract)
                dve.drain()
                dve.tensor_tensor(rows(mask, c * CT, CT), rest[:, :, :], lr[:, :, :], ALU.not_equal)
                dve.drain()
                dve.wait_ge(silu_done.sem, silu_done.past(c))
                dve.tensor_tensor(hsh[:, u, :], sg[:, :], gu[0:F, 1, :], ALU.mult).then_inc(shared_h.sem, 1)
                dve.tensor_tensor(keys[:, bass.ds(c * CT - half * HALF, CT), half, :], rows(mask, c * CT, CT),
                                  order[:, bass.ds(c * CT, CT)].unsqueeze(2).to_broadcast([P, CT, EXPERTS]), ALU.mult).then_inc(chosen.sem, 1)
                if before:
                    add_shared(c - 1)

            route(0, 0, 0, before=False)
            route(1, 1, 0)
            each_pair(dve, 2, CHUNKS // 2, lambda c, u: route(c, u, 0))
            each_pair(dve, CHUNKS // 2, CHUNKS - 2, lambda c, u: route(c, u, 1))
            route(CHUNKS - 2, 0, 1, False)
            route(CHUNKS - 1, 1, 1, False)
            add_shared(CHUNKS - 1)
            dve.drain()
            dve.wait_ge(keys_kept.sem, keys_kept.past(3))
            for r in range(ROUNDS):
                if r == ROUNDS // 2:
                    dve.wait_ge(exp_masked.sem, 1)
                    dve.tensor_reduce(wsum[:, :], wts[:, :, :], AX.X, ALU.add)
                    dve.drain()
                    dve.reciprocal(wsum[:, :], wsum[:, :])
                    dve.drain()
                    dve.tensor_scalar(wsum[:, :], wsum[:, :], 0.5, None, ALU.mult).then_inc(sums_inverted.sem, 1)
                dve.max(found[:, r * TOP:(r + 1) * TOP], keyt[:, :])
                dve.drain()
                if r < ROUNDS - 1:
                    dve.match_replace(keyt[:, :], found[:, r * TOP:(r + 1) * TOP], keyt[:, :], 0.0)
                    dve.drain()
            dve.memset(firsts[:, :], 0.0).then_inc(found_ready.sem, 1)
            dve.wait_ge(moved.sem, 1)
            dve.tensor_copy(both[:, :], kt[0:EXPERTS, 0, 0:2 * CAP])
            dve.drain()
            dve.tensor_tensor(firsts[:, CAP:2 * CAP], both[:, 0:CAP], both[:, CAP:2 * CAP][:, ::-1], ALU.max).then_inc(firsts_ready.sem, 1)
            dve.wait_ge(listed.sem, 1)
            dve.tensor_scalar(token[:, :], kt[:, 1, 0:PAIRS], -1.0, float(TOKENS), ALU.mult, ALU.add)
            dve.tensor_scalar(empty[:, :], kt[:, 1, 0:PAIRS], 0.0, slot[:, 0:1], ALU.is_equal, ALU.mult)
            dve.drain()
            dve.tensor_tensor(token[:, :], token[:, :], empty[:, :], ALU.add)
            dve.drain()
            dve.tensor_copy(from_i[:, :], token[:, :])
            dve.tensor_scalar(to_i[:, :], token[:, :], region[:, 0:1], None, ALU.add).then_inc(index_ready.sem, 1)
            dve.wait_ge(hp_clear.sem, 1)

            def gate(n, q):
                dve.wait_ge(gated.sem, gated.past(n))
                u = q % 2
                dve.tensor_tensor(hp[:, u, 0:CAP], gs[:, u, 0:CAP], gu[0:F, u, P:P + CAP], ALU.mult)
                dve.tensor_tensor(hp[:, u, P + CAP:2 * P], gs[:, u, CAP:P], gu[0:F, u, P + CAP:2 * P], ALU.mult).then_inc(h_done.sem, 1)

            def keep(n, q, reuse):
                dve.wait_ge(y_done.sem, y_done.past(n))
                if reuse:
                    dve.wait_ge(added.sem, (n - RING + 1) * 16)
                e = D + n
                dve.tensor_scalar(yo[0:CAP, q, :], ly[0:CAP, q % 2, 0:P], xg[0:CAP, q, bass.ds(e, 1)], None, ALU.mult)
                dve.tensor_scalar(yo[CAP:P, q, :], ly[CAP:P, q % 2, 0:P], xg[CAP:P, q, bass.ds(e + PAIRS, 1)], None, ALU.mult).then_inc(y_kept.sem, 1)

            def ring_body(n0, reuse, last=False):
                for q in range(RING):
                    if not (last and q == RING - 1):
                        gate(n0 + q + 1, (q + 1) % RING)
                    keep(n0 + q, q, reuse)

            gate(0, 0)
            ring_body(0, False)
            with dve.Fori(1, PAIRS // RING - 1) as ring:
                ring_body(ring * RING, True)
            ring_body(PAIRS - RING, True, True)
            for q in range(4):
                dve.wait_ge(acc_loaded[q].sem, 32)
                c8 = slice(q * 8, (q + 1) * 8)
                dve.tensor_tensor(core.x[:, c8, :], core.x[:, c8, :], acc_b[:, c8, :], ALU.add)
                dve.drain()
                for c in (2 * q, 2 * q + 1):
                    new_sums_dve(dve, core, c)

        @block.scalar
        def _(act):
            act.wait_ge(wr_turned.sem, 1)
            act.activation(wr[:, :], kt[:, 0, 0:EXPERTS], ACT.Copy).then_inc(wr_kept.sem, 1)
            ln_act(act, core, s, 0, 0)

            def body(c, u, more=True):
                if more:
                    ln_act(act, core, s, c + 1, 1 - u)
                act.wait_ge(shared_up.sem, shared_up.past(c))
                act.wait_ge(shared_h.sem, shared_h.past(c - 1))
                act.activation(sg[:, :], gu[0:F, 0, :], ACT.Silu).then_inc(silu_done.sem, 1)

            each_pair(act, 0, CHUNKS - 2, body)
            body(CHUNKS - 2, 0)
            body(CHUNKS - 1, 1, False)
            for g in range(4):
                act.wait_ge(keys_turned.sem, keys_turned.past(g))
                act.activation(keyt[:, g * CW:(g + 1) * CW], kt[:, g % 2, :], ACT.Copy).then_inc(keys_kept.sem, 1)
            act.wait_ge(chosen.sem, chosen.past(CHUNKS - 1))
            act.activation(wts[:, :, :], wts[:, :, :], ACT.Exp).then_inc(exp_done.sem, 1)

            def turn(n, q):
                act.wait_ge(xt_done.sem, xt_done.past(n))
                act.activation(xgt[:, q % 2, :], s.tp[:, 0, 0:P], ACT.Copy).then_inc(xt_kept.sem, 1)

            def gate(n, q):
                u = q % 2
                act.wait_ge(gu_done.sem, gu_done.past(n))
                act.wait_ge(h_done.sem, h_done.past(n - 2))
                act.activation(gs[:, u, :], gu[0:F, u, 0:P], ACT.Silu).then_inc(gated.sem, 1)

            turn(0, 0)

            def ring_body(n0, last=False):
                for q in range(RING):
                    if not (last and q == RING - 1):
                        turn(n0 + q + 1, q + 1)
                    gate(n0 + q, q)

            with act.Fori(0, PAIRS // RING - 1) as ring:
                ring_body(ring * RING)
            ring_body(PAIRS - RING, True)

        @block.tensor
        def _(pe):
            pe.wait_ge(w_loaded.sem, 48)
            pe.transpose(kt[:, 0, 0:EXPERTS], wr_raw[:, :], core.ident[0:EXPERTS, 0:EXPERTS]).then_inc(wr_turned.sem, 1)
            ln_pe(pe, core, s, 0, 0)
            pe.wait_ge(wr_kept.sem, 1)

            def shared_down(c, u):
                pe.wait_ge(shared_h.sem, shared_h.past(c))
                pe.wait_ge(shared_added.sem, shared_added.past(c - 1))
                for j in range(CT):
                    last = pe.matmul(ysh[:, j * P:(j + 1) * P], hsh[:, u, j * P:(j + 1) * P], wsd[:, :], start=True, stop=True)
                last.then_inc(shared_y.sem, 1)

            def body(c, u, more=True, before=True):
                if more:
                    ln_pe(pe, core, s, c + 1, 1 - u)
                pe.wait_ge(s.xnt_ready.sem, s.xnt_ready.past(c))
                pe.wait_ge(logits_kept.sem, logits_kept.past(c - 1))
                for j in range(CT):
                    last = pe.matmul(lg[:, j * EXPERTS:(j + 1) * EXPERTS], core.xnt[:, u, j * P:(j + 1) * P], wr[:, :],
                                     start=True, stop=True)
                last.then_inc(routed.sem, 1)
                pe.wait_ge(shared_h.sem, shared_h.past(c - 1))
                pe.matmul(gu[0:F, 0, :], wsgu[:, 0:F], core.xnt[:, u, :], start=True, stop=True)
                pe.matmul(gu[0:F, 1, :], wsgu[:, F:2 * F], core.xnt[:, u, :], start=True, stop=True).then_inc(shared_up.sem, 1)
                if before:
                    shared_down(c - 1, 1 - u)

            body(0, 0, before=False)
            body(1, 1)
            each_pair(pe, 2, CHUNKS - 2, body)
            body(CHUNKS - 2, 0)
            body(CHUNKS - 1, 1, False)
            shared_down(CHUNKS - 1, 1)
            pe.wait_ge(chosen.sem, chosen.past(CHUNKS - 1))
            for g in range(4):
                pe.wait_ge(keys_kept.sem, keys_kept.past(g - 2))
                for j in range(CT):
                    last = pe.transpose(kt[:, g % 2, j * P:(j + 1) * P], keys[:, g * CT + j, :, :].rearrange("p h e -> p (h e)"), core.ident[:, :])
                last.then_inc(keys_turned.sem, 1)
            pe.wait_ge(found_ready.sem, 1)
            pe.wait_ge(keys_kept.sem, keys_kept.past(3))
            for half in range(2):
                last = pe.matmul(kt[0:EXPERTS, 0, half * CAP:(half + 1) * CAP], core.ident[:, half * EXPERTS:(half + 1) * EXPERTS],
                                 found[:, :], start=True, stop=True)
            last.then_inc(moved.sem, 1)
            pe.wait_ge(firsts_ready.sem, 1)
            pe.matmul(kt[:, 1, 0:PAIRS], firsts[:, CAP:3 * CAP], core.ident[0:EXPERTS, 0:PAIRS], start=True, stop=False)
            pe.matmul(kt[:, 1, 0:PAIRS], firsts[:, 0:2 * CAP], core.ident[0:EXPERTS, PAIRS:2 * PAIRS], start=False, stop=True).then_inc(listed.sem, 1)
            pe.wait_ge(index_ready.sem, 1)

            def turn(n, ring, q):
                pe.wait_ge(xg_loaded[q].sem, ring * 16 + 16)
                pe.wait_ge(xt_kept.sem, xt_kept.past(n - 1))
                pe.transpose(s.tp[:, 0, 0:P], xg[:, q, 0:D], core.ident[:, :]).then_inc(xt_done.sem, 1)

            def up(n, ring, q):
                u = q % 2
                pe.wait_ge(ring_loaded[q].sem, ring * 48 + 48)
                pe.wait_ge(xt_kept.sem, xt_kept.past(n))
                pe.wait_ge(h_done.sem, h_done.past(n - 2))
                for b in range(2):
                    cols = xgt[:, u, b * CAP:(b + 1) * CAP]
                    pe.matmul(gu[0:F, u, b * CAP:(b + 1) * CAP], wg[:, q, b, :], cols, start=True, stop=True)
                    last = pe.matmul(gu[0:F, u, P + b * CAP:P + (b + 1) * CAP], wu[:, q, b, :], cols, start=True, stop=True)
                last.then_inc(gu_done.sem, 1)

            def down(n, q):
                u = q % 2
                pe.wait_ge(h_done.sem, h_done.past(n))
                pe.wait_ge(y_kept.sem, y_kept.past(n - 2))
                for b in range(2):
                    last = pe.matmul(ly[:, u, 0:P], hp[:, u, b * P:(b + 1) * P], wd[:, q, b, :], start=b == 0, stop=b == 1)
                last.then_inc(y_done.sem, 1)

            turn(0, 0, 0)
            up(0, 0, 0)
            turn(1, 0, 1)

            def ring_body(n0, ring, last=False):
                for q in range(RING):
                    if not (last and q == RING - 1):
                        up(n0 + q + 1, ring + (q + 1) // RING, (q + 1) % RING)
                    if not (last and q >= RING - 2):
                        turn(n0 + q + 2, ring + (q + 2) // RING, (q + 2) % RING)
                    down(n0 + q, q)

            with pe.Fori(0, PAIRS // RING - 1) as ring:
                ring_body(ring * RING, ring)
            ring_body(PAIRS - RING, PAIRS // RING - 1, True)



def l1_attn(core):
    nc, w = core.nc, core.w
    BATCHES = CW // N
    CTX_SCALE = 1.0 / (8.0 ** 0.5) / D
    with stage(nc) as s:
        ln_signals(s)
        wm = {m: s.sb(f"w_{m}", [P, P]) for m in ("Wq", "Wk", "Wv", "Wo")}
        bias = s.sb("bias", [P, P])
        ke = s.sb("ke", [P, BATCHES, N])
        qe = s.sb("qe", [P, CT, P])
        kn = s.sb("kn", [P, CT, P])
        qt = s.sb("qt", [P, CT, P])
        vs = s.sb("vs", [P, 2, CT, P])
        ctxt = s.sb("ctxt", [P, BATCHES, P])
        mix = s.sb("mix", [P, BATCHES, P])
        kmax = s.sb("kmax", [P, BATCHES])
        qmax = s.sb("qmax", [P, CT])
        ksum = s.sb("ksum", [P, 2, BATCHES])
        qsum = s.sb("qsum", [P, 2, CT])
        kp, qp, vp, ktp, qtp = (s.ps(n, [P, CT, P]) for n in ("kp", "qp", "vp", "ktp", "qtp"))
        cm = s.ps("cm", [P, 2, BATCHES, P])
        w_loaded = s.sig("w_loaded")
        projected = s.sig("projected")
        max_ready = s.sig("max_ready")
        exp_done = s.sig("exp_done", 2)
        turned = s.sig("turned")
        turn_kept = s.sig("turn_kept", 2)
        v_kept = s.sig("v_kept", 1)
        sums_inverted = s.sig("sums_inverted")
        ctx_done = s.sig("ctx_done")
        ctx_kept = s.sig("ctx_kept")
        mix_done = s.sig("mix_done")
        mix_kept = s.sig("mix_kept", 1)
        y_done = s.sig("y_done")
        x_added = s.sig("x_added", 1)
        s.ready()
        block = s.ctx.enter_context(nc.Block())

        @block.sync
        def _(sp):
            for m, t in wm.items():
                sp.dma_start(t[:, :], w[f"L1_attn_{m}"]).then_inc(w_loaded.sem, 16)
            sp.dma_start(bias[:, :], w["L1_attn_bo"].partition_broadcast(P)).then_inc(w_loaded.sem, 16)

        @block.gpsimd
        def _(pool):
            ln_scales_pool(pool, core, s)

        @block.vector
        def _(dve):
            def maxima(c, u):
                dve.wait_ge(projected.sem, projected.past(3 * c))
                dve.tensor_reduce(kmax[:, :], kp[:, :, :].rearrange("p (b t) n -> p b (t n)", b=BATCHES), AX.X, ALU.max,
                                  negate=True).then_inc(max_ready.sem, 1)
                dve.wait_ge(projected.sem, projected.past(3 * c + 1))
                dve.tensor_reduce(qmax[:, :], qp[:, :, :], AX.X, ALU.max, negate=True).then_inc(max_ready.sem, 1)
                dve.wait_ge(projected.sem, projected.past(3 * c + 2))
                dve.tensor_copy(vs[:, u, :, :], vp[:, :, :]).then_inc(v_kept.sem, 1)

            def invert(c, u):
                dve.wait_ge(exp_done.sem, exp_done.past(2 * c + 1))
                dve.reciprocal(ksum[:, u, :], ksum[:, u, :])
                dve.reciprocal(qsum[:, u, :], qsum[:, u, :])
                dve.drain()
                dve.tensor_scalar(ksum[:, u, :], ksum[:, u, :], CTX_SCALE, None, ALU.mult)

            ln_scales_dve(dve, core, s)
            ln_dve(dve, core, s, 0, 0)
            ln_dve(dve, core, s, 1, 1)
            maxima(0, 0)
            invert(0, 0)
            dve.wait_ge(w_loaded.sem, 80)

            def body(c, u, ahead=2):
                if ahead > 0:
                    maxima(c + 1, 1 - u)
                dve.wait_ge(ctx_done.sem, ctx_done.past(c))
                dve.tensor_copy(ctxt[:, :, :], cm[:, 0, :, :]).then_inc(ctx_kept.sem, 1)
                dve.wait_ge(mix_done.sem, mix_done.past(c))
                for b in range(BATCHES):
                    last = dve.tensor_scalar(mix[:, b, :], cm[:, 1, b, :], ksum[:, u, b:b + 1], None, ALU.mult)
                last.then_inc(mix_kept.sem, 1)
                if ahead > 0:
                    invert(c + 1, 1 - u)
                if ahead > 1:
                    ln_dve(dve, core, s, c + 2, u)
                xs = rows(core.x, c * CT, CT)
                dve.tensor_tensor(xs, xs, bias[:, :].unsqueeze(1).to_broadcast([P, CT, P]), ALU.add)
                dve.drain()
                dve.wait_ge(y_done.sem, y_done.past(c))
                for j in range(CT):
                    xj = core.x[:, bass.ds(c * CT + j, 1), :]
                    last = dve.scalar_tensor_tensor(xj, vp[:, j:j + 1, :], qsum[:, u, j:j + 1], xj, ALU.mult, ALU.add)
                last.then_inc(x_added.sem, 1)
                dve.drain()
                new_sums_dve(dve, core, c)

            each_pair(dve, 0, CHUNKS - 2, body)
            body(CHUNKS - 2, 0, 1)
            body(CHUNKS - 1, 1, 0)

        @block.scalar
        def _(act):
            def exps(c, u):
                act.wait_ge(max_ready.sem, max_ready.past(2 * c))
                kv = kp[:, :, :].rearrange("p (b t) n -> p b (t n)", b=BATCHES)
                for b in range(BATCHES):
                    last = act.activation(ke[:, b, :], kv[:, b, :], ACT.Exp, bias=kmax[:, b:b + 1],
                                          accum_out=ksum[:, u, b:b + 1])
                last.then_inc(exp_done.sem, 1)
                act.wait_ge(max_ready.sem, max_ready.past(2 * c + 1))
                for j in range(CT):
                    last = act.activation(qe[:, j, :], qp[:, j, :], ACT.Exp, bias=qmax[:, j:j + 1],
                                          accum_out=qsum[:, u, j:j + 1])
                last.then_inc(exp_done.sem, 1)

            ln_act(act, core, s, 0, 0)
            exps(0, 0)
            ln_act(act, core, s, 1, 1)

            def body(c, u, ahead=2):
                act.wait_ge(turned.sem, turned.past(2 * c))
                act.activation(kn[:, :, :], ktp[:, :, :], ACT.Copy).then_inc(turn_kept.sem, 1)
                act.wait_ge(turned.sem, turned.past(2 * c + 1))
                act.activation(qt[:, :, :], qtp[:, :, :], ACT.Copy).then_inc(turn_kept.sem, 1)
                if ahead > 0:
                    act.wait_ge(x_added.sem, x_added.past(c - 1))
                    exps(c + 1, 1 - u)
                if ahead > 1:
                    ln_act(act, core, s, c + 2, u)

            each_pair(act, 0, CHUNKS - 2, body)
            body(CHUNKS - 2, 0, 1)
            body(CHUNKS - 1, 1, 0)

        @block.tensor
        def _(pe):
            def project(c, u):
                pe.wait_ge(s.xnt_ready.sem, s.xnt_ready.past(c))
                pe.wait_ge(exp_done.sem, exp_done.past(2 * c - 2))
                pe.matmul(kp[:, :, :].rearrange("p t n -> p (t n)"), wm["Wk"][:, :], core.xnt[:, u, :],
                          start=True, stop=True).then_inc(projected.sem, 1)
                pe.wait_ge(exp_done.sem, exp_done.past(2 * c - 1))
                for j in range(CT):
                    last = pe.matmul(qp[:, j, :], core.xnt[:, u, j * P:(j + 1) * P], wm["Wq"][:, :],
                                     start=True, stop=True)
                last.then_inc(projected.sem, 1)
                pe.wait_ge(v_kept.sem, v_kept.past(c - 1))
                pe.wait_ge(x_added.sem, x_added.past(c - 2))
                for j in range(CT):
                    last = pe.matmul(vp[:, j, :], core.xnt[:, u, j * P:(j + 1) * P], wm["Wv"][:, :],
                                     start=True, stop=True)
                last.then_inc(projected.sem, 1)

            ln_pe(pe, core, s, 0, 0)
            pe.wait_ge(w_loaded.sem, 80)
            project(0, 0)
            ln_pe(pe, core, s, 1, 1)

            def body(c, u, ahead=2):
                pe.wait_ge(exp_done.sem, exp_done.past(2 * c))
                for j in range(CT):
                    last = pe.transpose(ktp[:, j, :], ke[:, :, :].rearrange("p b n -> p (b n)")[:, j * P:(j + 1) * P], core.ident[:, :])
                last.then_inc(turned.sem, 1)
                pe.wait_ge(exp_done.sem, exp_done.past(2 * c + 1))
                for j in range(CT):
                    last = pe.transpose(qtp[:, j, :], qe[:, j, :], core.ident[:, :])
                last.then_inc(turned.sem, 1)
                if ahead > 0:
                    project(c + 1, 1 - u)
                pe.wait_ge(turn_kept.sem, turn_kept.past(2 * c))
                pe.wait_ge(v_kept.sem, v_kept.past(c))
                pe.wait_ge(mix_kept.sem, mix_kept.past(c - 1))
                for b in range(BATCHES):
                    for t in range(N // P):
                        j = b * (N // P) + t
                        last = pe.matmul(cm[:, 0, b, :], vs[:, u, j, :], kn[:, j, :], start=t == 0, stop=t == N // P - 1)
                last.then_inc(ctx_done.sem, 1)
                pe.wait_ge(ctx_kept.sem, ctx_kept.past(c))
                for b in range(BATCHES):
                    last = pe.matmul(cm[:, 1, b, :], ctxt[:, b, :], wm["Wo"][:, :], start=True, stop=True)
                last.then_inc(mix_done.sem, 1)
                pe.wait_ge(mix_kept.sem, mix_kept.past(c))
                pe.wait_ge(turn_kept.sem, turn_kept.past(2 * c + 1))
                if ahead > 0:
                    pe.wait_ge(v_kept.sem, v_kept.past(c + 1))
                for j in range(CT):
                    last = pe.matmul(vp[:, j, :], qt[:, j, :], mix[:, j // (N // P), :], start=True, stop=True)
                last.then_inc(y_done.sem, 1)
                if ahead > 1:
                    ln_pe(pe, core, s, c + 2, u)

            each_pair(pe, 0, CHUNKS - 2, body)
            body(CHUNKS - 2, 0, 1)
            body(CHUNKS - 1, 1, 0)



def l2_ffn(core):
    nc, w = core.nc, core.w
    EXPERTS, S, _, _ = w["L2_ffn_W1"].shape
    K = D // S
    CAP = int(1.5 * TOKENS / EXPERTS)
    assert CAP == P
    TOP = 8
    RING = 4
    UP = 64
    HALF = TOKENS // 2
    LOW = -3.0e38
    with stage(nc) as s:
        ln_signals(s, 1)
        wr_raw = s.sb("wr_raw", [EXPERTS, D])
        wr = s.sb("wr", [P, P])
        b1_raw = s.sb("b1_raw", [EXPERTS, S * P])
        b1 = s.sb("b1", [P, S, EXPERTS])
        b2 = s.sb("b2", [P, EXPERTS, D])
        zero = s.sb("zero", [P, 8, D])
        own = s.sb("own", [P, S])
        lt = s.sb("lt", [P, HALF])
        vals = s.sb("vals", [P, CAP])
        poss = s.sb("poss", [P, CAP], U32)
        posf = s.sb("posf", [P, CAP])
        vals1 = s.sb("vals1", [EXPERTS, CAP])
        posf1 = s.sb("posf1", [EXPERTS, CAP])
        first = s.sb("first", [EXPERTS, CAP])
        big = s.sb("big", [EXPERTS, 1])
        esum = s.sb("esum", [EXPERTS, 1])
        prob = s.sb("prob", [EXPERTS, CAP])
        prob_s = s.sb("prob_s", [P, EXPERTS])
        from_i = s.sb("from_i", [P, EXPERTS], U32)
        to_i = s.sb("to_i", [P, EXPERTS], U32)
        w1 = s.sb("w1", [P, RING, S, P])
        w2 = s.sb("w2", [P, RING, S, K])
        w2b = s.sb("w2b", [P, RING, S, D])
        xg = s.sb("xg", [P, RING, D])
        xgt = s.sb("xgt", [P, 2, P])
        h = s.sb("h", [P, 2, S, P])
        yb = s.sb("yb", [P, 2, D])
        yo = s.sb("yo", [P, RING, D])
        acc_b = s.sb("acc_b", [P, TILES, D])
        lp = s.ps("lp", [P, 2, CW])
        hu = s.ps("hu", [P, 2, CW])
        yp = s.ps("yp", [P, 2, CW])
        w_loaded = s.sig("w_loaded")
        b2_loaded = s.sig("b2_loaded")
        filled = s.sig("filled")
        zeroed = s.sig("zeroed")
        wr_turned = s.sig("wr_turned")
        wr_kept = s.sig("wr_kept")
        copied = s.sig("copied", 2)
        routed = s.sig("routed")
        logits_kept = s.sig("logits_kept", 2)
        best_found = s.sig("best_found")
        moved = s.sig("moved")
        merged = s.sig("merged")
        exp_done = s.sig("exp_done")
        listed = s.sig("listed")
        slots_turned = s.sig("slots_turned")
        index_ready = s.sig("index_ready")
        rows_stored = s.sig("rows_stored")
        ring_loaded = [s.sig(f"ring_loaded{q}") for q in range(RING)]
        dmas = s.pool_dmas(core)
        added, xg_loaded = dmas[0:2], dmas[2:2 + RING]
        w2_spread = s.sig("w2_spread")
        xt_done = s.sig("xt_done")
        xt_kept = s.sig("xt_kept", 1)
        h_done = s.sig("h_done")
        gelu_done = s.sig("gelu_done", 2)
        y_done = s.sig("y_done", RING)
        y_kept = s.sig("y_kept", 2)
        acc_loaded = [s.sig(f"acc_loaded{q}") for q in range(4)]
        s.ready()
        table, sums = core.rows_dram, core.acc_dram
        ROWS = TOKENS
        block = s.ctx.enter_context(nc.Block())

        @block.sync
        def _(sp):
            sp.dma_start(wr_raw[:, :], w["L2_ffn_Wr"]).then_inc(w_loaded.sem, 16)
            sp.dma_start(b1_raw[:, :], w["L2_ffn_b1"].rearrange("e s m -> e (s m)")).then_inc(w_loaded.sem, 16)

            def load(n, q):
                sp.dma_start(w1[:, q, :, :], w["L2_ffn_W1"][bass.ds(n, 1)].rearrange("n s d m -> d (n s) m")).then_inc(ring_loaded[q].sem, 16)
                sp.dma_start(w2[:, q, :, :].rearrange("p j k -> p (j k)"),
                             w["L2_ffn_W2"][bass.ds(n, 1)].rearrange("n s (a j) k -> (n s a) (j k)", j=S)).then_inc(ring_loaded[q].sem, 16)

            for q in range(RING):
                load(q, q)
            sp.dma_start(b2[:, :, :].rearrange("p e d -> p (e d)"),
                         w["L2_ffn_b2"].rearrange("e s k -> (e s k)").partition_broadcast(P)).then_inc(b2_loaded.sem, 16)
            sp.wait_ge(filled.sem, 1)
            for n in range(TILES // 8):
                sp.dma_start(sums[ROWS + n * 8 * P:ROWS + (n + 1) * 8 * P, :].rearrange("(a p) d -> p a d", p=P), zero[:, :, :]).then_inc(zeroed.sem, 16)
            sp.dma_start(sums[0:ROWS, :].rearrange("(t p) d -> p t d", p=P), core.x[:, :, :]).then_inc(zeroed.sem, 16)
            sp.wait_ge(copied.sem, copied.past(CHUNKS - 1))
            sp.dma_start(table.rearrange("(t p) d -> p t d", p=P), core.all_xn[:, :, :]).then_inc(rows_stored.sem, 16)
            sp.wait_ge(best_found.sem, 1)
            sp.dma_start(vals1[:, :], vals[UP:UP + EXPERTS, :]).then_inc(moved.sem, 16)
            sp.dma_start(posf1[:, :], posf[UP:UP + EXPERTS, :]).then_inc(moved.sem, 16)

            with sp.Fori(0, EXPERTS // RING - 1) as ring:
                for q in range(RING):
                    sp.wait_ge(y_done.sem, y_done.past(ring * RING + q))
                    load(ring * RING + q + RING, q)
            for q in range(2):
                sp.wait_ge(added[q].sem, 16 * EXPERTS // 2)
            for q in range(4):
                for b, t in ((0, core.x), (1, acc_b)):
                    sp.dma_start(t[:, q * 8:(q + 1) * 8, :],
                                 sums[b * ROWS + q * 8 * P:b * ROWS + (q + 1) * 8 * P, :].rearrange("(t p) d -> p t d", p=P)).then_inc(acc_loaded[q].sem, 16)

        @block.gpsimd
        def _(pool):
            ln_scales_pool(pool, core, s, range(2))
            pool.memset(zero[:, :, :], 0.0).then_inc(filled.sem, 1)
            pool.memset(own[:, :], 1.0).then_inc(filled.sem, 1)
            pool.wait_ge(filled.sem, 2)
            pool.affine_select(out=own[:, :], in_=own[:, :], compare_op=ALU.is_ge, fill=0.0,
                               base=0, pattern=[[-K, S]], channel_multiplier=1).then_inc(filled.sem, 1)
            pool.wait_ge(filled.sem, 3)
            pool.affine_select(out=own[:, :], in_=own[:, :], compare_op=ALU.is_ge, fill=0.0,
                               base=K - 1, pattern=[[K, S]], channel_multiplier=-1).then_inc(filled.sem, 1)

            def copy(c, u, more=True):
                if more:
                    ln_scale_pool(pool, core, s, c + 2)
                pool.wait_ge(s.xn_ready.sem, s.xn_ready.past(c))
                pool.tensor_copy(rows(core.all_xn, c * CT, CT), core.xn[:, u, :, :]).then_inc(copied.sem, 1)

            each_pair(pool, 0, CHUNKS - 2, copy)
            copy(CHUNKS - 2, 0, False)
            copy(CHUNKS - 1, 1, False)
            pool.wait_ge(index_ready.sem, 1)
            pool.wait_ge(rows_stored.sem, 16)
            pool.wait_ge(zeroed.sem, 16 * (TILES // 8 + 1))

            def gather(n):
                if n >= RING:
                    pool.wait_ge(xt_done.sem, xt_done.past(n - RING))
                pool.indirect_dma_start(xg[:, n % RING, :], None, table,
                                        bass.IndirectOffsetOnAxis(ap=from_i[:, n:n + 1], axis=0)).then_inc(xg_loaded[n % RING].sem, 16)

            for n in range(RING):
                gather(n)
            for n in range(EXPERTS):
                if n + RING < EXPERTS:
                    gather(n + RING)
                pool.wait_ge(y_kept.sem, y_kept.past(n))
                q = n % 2
                if n > 1:
                    pool.wait_ge(added[q].sem, 16 * (n // 2))
                pool.indirect_dma_start(sums, bass.IndirectOffsetOnAxis(ap=to_i[:, n:n + 1], axis=0),
                                        yo[:, n % RING, :], None, compute_op=ALU.add).then_inc(added[q].sem, 16)
            for q in range(RING):
                pool.wait_ge(xg_loaded[q].sem, 16 * (EXPERTS // RING))
            for q in range(2):
                pool.wait_ge(added[q].sem, 16 * (EXPERTS // 2))
            s.reset_pool_dmas(pool)

        @block.vector
        def _(dve):
            ln_scales_dve(dve, core, s)
            ln_dve(dve, core, s, 0, 0, copied)
            ln_dve(dve, core, s, 1, 1, copied)
            dve.wait_ge(wr_kept.sem, 1)
            dve.memset(lt[32:64, :], LOW)
            dve.memset(lt[96:P, :], LOW).then_inc(wr_kept.sem, 1)

            each_pair(dve, 2, CHUNKS, lambda c, u: ln_dve(dve, core, s, c, u, copied))
            dve.wait_ge(logits_kept.sem, logits_kept.past(CHUNKS - 1))
            for r in range(CAP // TOP):
                got = vals[:, r * TOP:(r + 1) * TOP]
                dve.max(got, lt[:, :])
                dve.drain()
                dve.max_index(poss[:, r * TOP:(r + 1) * TOP], got, lt[:, :])
                if r < CAP // TOP - 1:
                    dve.match_replace(lt[:, :], got, lt[:, :], LOW)
                    dve.drain()
            dve.drain()
            dve.tensor_copy(posf[0:UP, :], poss[0:UP, :])
            dve.tensor_scalar(posf[UP:P, :], poss[UP:P, :], float(HALF), None, ALU.add).then_inc(best_found.sem, 1)
            dve.wait_ge(moved.sem, 32)
            v0, p0 = vals[0:EXPERTS, :], posf[0:EXPERTS, :]
            v1, p1 = vals1[:, ::-1], posf1[:, ::-1]
            dve.tensor_tensor(first[:, :], v0, v1, ALU.is_ge)
            dve.tensor_tensor(big[:, :], vals[0:EXPERTS, 0:1], vals1[:, 0:1], ALU.max)
            dve.tensor_tensor(prob[:, :], v0, v1, ALU.max)
            dve.tensor_tensor(p0, p0, p1, ALU.subtract)
            dve.drain()
            dve.tensor_tensor(p0, p0, first[:, :], ALU.mult)
            dve.tensor_scalar(big[:, :], big[:, :], -1.0, None, ALU.mult).then_inc(merged.sem, 1)
            dve.drain()
            dve.tensor_tensor(p0, p0, p1, ALU.add)
            dve.wait_ge(exp_done.sem, 1)
            dve.reciprocal(esum[:, :], esum[:, :])
            dve.drain()
            dve.tensor_scalar(prob[:, :], prob[:, :], esum[:, 0:1], 0.5, ALU.mult, ALU.mult).then_inc(listed.sem, 1)
            dve.wait_ge(slots_turned.sem, 1)
            dve.tensor_copy(from_i[:, :], lp[:, 0, 0:EXPERTS])
            dve.tensor_copy(to_i[:, ::2], lp[:, 0, 0:EXPERTS:2])
            dve.tensor_scalar(to_i[:, 1::2], lp[:, 0, 1:EXPERTS:2], float(ROWS), None, ALU.add).then_inc(index_ready.sem, 1)
            dve.tensor_copy(prob_s[:, :], lp[:, 1, 0:EXPERTS])
            dve.drain()
            dve.wait_ge(filled.sem, 4)

            def spread(n, ring, q):
                dve.wait_ge(ring_loaded[q].sem, ring * 32 + 32)
                dve.wait_ge(y_done.sem, y_done.past(n - RING))
                dve.tensor_tensor(w2b[:, q, :, :].rearrange("p j (s k) -> p j s k", s=S),
                                  w2[:, q, :, :].unsqueeze(2).to_broadcast([P, S, S, K]),
                                  own[:, :].unsqueeze(1).unsqueeze(3).to_broadcast([P, S, S, K]), ALU.mult).then_inc(w2_spread.sem, 1)

            def keep(n, ring, q, reuse):
                u = q % 2
                dve.wait_ge(y_done.sem, y_done.past(n))
                dve.tensor_tensor(yb[:, u, :], yp[:, u, 0:D], b2[:, bass.ds(n, 1), :], ALU.add)
                dve.drain()
                if reuse:
                    dve.wait_ge(added[u].sem, (ring * (RING // 2) + q // 2 - 1) * 16)
                dve.tensor_scalar(yo[:, q, :], yb[:, u, :], prob_s[:, bass.ds(n, 1)], None, ALU.mult).then_inc(y_kept.sem, 1)

            def ring_body(ring, reuse=True, last=False):
                for q in range(RING):
                    if not (last and q == RING - 1):
                        spread(ring * RING + q + 1, ring + (q + 1) // RING, (q + 1) % RING)
                    keep(ring * RING + q, ring, q, reuse)

            dve.wait_ge(b2_loaded.sem, 16)
            spread(0, 0, 0)
            ring_body(0, False)
            with dve.Fori(1, EXPERTS // RING - 1) as ring:
                ring_body(ring)
            ring_body(EXPERTS // RING - 1, last=True)
            for q in range(4):
                dve.wait_ge(acc_loaded[q].sem, 32)
                c8 = slice(q * 8, (q + 1) * 8)
                dve.tensor_tensor(core.x[:, c8, :], core.x[:, c8, :], acc_b[:, c8, :], ALU.add)
                dve.drain()
                for c in (2 * q, 2 * q + 1):
                    new_sums_dve(dve, core, c)

        @block.scalar
        def _(act):
            act.wait_ge(wr_turned.sem, 1)
            act.activation(wr[:, 0:UP], lp[:, 0, 0:UP], ACT.Copy)
            act.activation(wr[:, UP:P], lp[:, 0, 0:UP], ACT.Copy)
            act.activation(b1[:, :, :], lp[:, 1, 0:S * UP].rearrange("p (j e) -> p j e", e=UP)[:, :, 0:EXPERTS], ACT.Copy).then_inc(wr_kept.sem, 1)
            ln_act(act, core, s, 0, 0)

            def body(c, u, half, more=True):
                if more:
                    ln_act(act, core, s, c + 1, 1 - u)
                act.wait_ge(routed.sem, routed.past(c))
                lo = half * UP
                act.activation(lt[lo:lo + EXPERTS, bass.ds((c - half * (CHUNKS // 2)) * CW, CW)], lp[lo:lo + EXPERTS, u, :],
                               ACT.Copy).then_inc(logits_kept.sem, 1)

            act.wait_ge(wr_kept.sem, 2)
            each_pair(act, 0, CHUNKS // 2, lambda c, u: body(c, u, 0))
            each_pair(act, CHUNKS // 2, CHUNKS - 2, lambda c, u: body(c, u, 1))
            body(CHUNKS - 2, 0, 1)
            body(CHUNKS - 1, 1, 1, False)
            act.wait_ge(merged.sem, 1)
            act.activation(prob[:, :], prob[:, :], ACT.Exp, bias=big[:, 0:1], accum_out=esum[:, 0:1]).then_inc(exp_done.sem, 1)

            def turn(n, q):
                act.wait_ge(xt_done.sem, xt_done.past(n))
                act.activation(xgt[:, q % 2, :], s.tp[:, 0, 0:P], ACT.Copy).then_inc(xt_kept.sem, 1)

            def gelu(n, q):
                u = q % 2
                act.wait_ge(h_done.sem, h_done.past(n))
                act.wait_ge(y_done.sem, y_done.past(n - 2))
                for j in range(S):
                    last = act.activation(h[:, u, j, :], hu[:, u, j * P:(j + 1) * P], ACT.Gelu, bias=b1[:, j, bass.ds(n, 1)])
                last.then_inc(gelu_done.sem, 1)

            turn(0, 0)

            def ring_body(n0, last=False):
                for q in range(RING):
                    if not (last and q == RING - 1):
                        turn(n0 + q + 1, q + 1)
                    gelu(n0 + q, q)

            with act.Fori(0, EXPERTS // RING - 1) as ring:
                ring_body(ring * RING)
            ring_body(EXPERTS - RING, True)

        @block.tensor
        def _(pe):
            pe.wait_ge(w_loaded.sem, 32)
            pe.transpose(lp[:, 0, 0:EXPERTS], wr_raw[:, :], core.ident[0:EXPERTS, 0:EXPERTS])
            pe.matmul(lp[:, 0, EXPERTS:UP], wr_raw[:, :], core.ident[0:EXPERTS, 0:UP - EXPERTS], start=True, stop=True)
            for j in range(S):
                last = pe.transpose(lp[:, 1, j * UP:j * UP + EXPERTS], b1_raw[:, j::S], core.ident[0:EXPERTS, 0:EXPERTS])
            last.then_inc(wr_turned.sem, 1)
            ln_pe(pe, core, s, 0, 0)
            pe.wait_ge(wr_kept.sem, 1)

            def body(c, u, more=True):
                if more:
                    ln_pe(pe, core, s, c + 1, 1 - u)
                pe.wait_ge(s.xnt_ready.sem, s.xnt_ready.past(c))
                pe.wait_ge(logits_kept.sem, logits_kept.past(c - 2))
                pe.matmul(lp[:, u, :], wr[:, :], core.xnt[:, u, :], start=True, stop=True).then_inc(routed.sem, 1)

            each_pair(pe, 0, CHUNKS - 2, body)
            body(CHUNKS - 2, 0)
            body(CHUNKS - 1, 1, False)
            pe.wait_ge(logits_kept.sem, logits_kept.past(CHUNKS - 1))
            pe.wait_ge(listed.sem, 1)
            pe.transpose(lp[:, 0, 0:EXPERTS], posf[0:EXPERTS, :], core.ident[0:EXPERTS, 0:EXPERTS])
            pe.transpose(lp[:, 1, 0:EXPERTS], prob[:, :], core.ident[0:EXPERTS, 0:EXPERTS]).then_inc(slots_turned.sem, 1)

            def turn(n, ring, q):
                pe.wait_ge(xg_loaded[q].sem, ring * 16 + 16)
                pe.wait_ge(xt_kept.sem, xt_kept.past(n - 1))
                pe.transpose(s.tp[:, 0, 0:P], xg[:, q, :], core.ident[:, :]).then_inc(xt_done.sem, 1)

            def up(n, ring, q):
                u = q % 2
                pe.wait_ge(ring_loaded[q].sem, ring * 32 + 32)
                pe.wait_ge(xt_kept.sem, xt_kept.past(n))
                pe.wait_ge(gelu_done.sem, gelu_done.past(n - 2))
                for j in range(S):
                    last = pe.matmul(hu[:, u, j * P:(j + 1) * P], w1[:, q, :, :].rearrange("p s m -> p (s m)")[:, j::S],
                                     xgt[:, u, :], start=True, stop=True)
                last.then_inc(h_done.sem, 1)

            def down(n, q):
                u = q % 2
                pe.wait_ge(w2_spread.sem, w2_spread.past(n))
                pe.wait_ge(gelu_done.sem, gelu_done.past(n))
                pe.wait_ge(y_kept.sem, y_kept.past(n - 2))
                for j in range(S):
                    last = pe.matmul(yp[:, u, 0:D], h[:, u, j, :], w2b[:, q, j, :], start=j == 0, stop=j == S - 1)
                last.then_inc(y_done.sem, 1)

            turn(0, 0, 0)
            up(0, 0, 0)
            turn(1, 0, 1)

            def ring_body(n0, ring, last=False):
                for q in range(RING):
                    if not (last and q == RING - 1):
                        up(n0 + q + 1, ring + (q + 1) // RING, (q + 1) % RING)
                    if not (last and q >= RING - 2):
                        turn(n0 + q + 2, ring + (q + 2) // RING, (q + 2) % RING)
                    down(n0 + q, q)

            with pe.Fori(0, EXPERTS // RING - 1) as ring:
                ring_body(ring * RING, ring)
            ring_body(EXPERTS - RING, EXPERTS // RING - 1, True)



def l2_attn(core):
    nc, w = core.nc, core.w
    HV = 64
    PAIRS = w["L2_attn_W_Q"].shape[1] // P
    HALVES = PAIRS * P // CW
    PH = CW // P
    NT = N // P
    KV_GROUPS = ((0, 1, 2), (3, 4, 5), (6, 7))
    GW = P + 2
    with stage(nc) as s:
        ln_signals(s, 1)
        wq = s.sb("wq", [P, PAIRS * P])
        wk = s.sb("wk", [P, PAIRS * P])
        wv = s.sb("wv", [P, PAIRS * P])
        wfc = s.sb("wfc", [P, PAIRS, P])
        gamma = s.sb("gamma", [P, P])
        beta = s.sb("beta", [P, P])
        same = s.sb("same_head", [P, P])
        which = s.sb("which", [P, 2])
        qt = s.sb("qt", [P, 2, PAIRS, CW])
        ks = s.sb("ks", [P, NT, PAIRS * P])
        vs = s.sb("vs", [P, NT, PAIRS, P + 1])
        kvs = s.sb("kvs", [P, PAIRS, GW])
        den = s.sb("den", [P, 2, 3, 2])
        o = s.sb("o", [P, NT, PAIRS, P])
        ot = s.sb("ot", [P, PAIRS, N])
        r = s.sb("r", [P, 2, NT, P])
        rs = s.sb("rs", [P, NT, 6])
        rm = s.sb("rm", [P, NT, 2])
        rv = s.sb("rv", [P, NT])
        rd = s.sb("rd", [P, NT])
        power = s.sb("power", [P, NT])
        pj = s.ps("pj", [P, 2, CW])
        kn = s.ps("kn", [P, 4, CW])
        y = s.ps("y", [P, 2, NT, P])
        w_loaded = s.sig("w_loaded")
        vectors_loaded = s.sig("vectors_loaded")
        filled = s.sig("filled")
        masked = s.sig("masked")
        projected = s.sig("projected")
        act_kept = s.sig("act_kept", 1)
        v_kept = s.sig("v_kept", 1)
        kv_done = s.sig("kv_done")
        kvs_ready = s.sig("kvs_ready", 2)
        nd_done = s.sig("nd_done")
        o_turned = s.sig("o_turned")
        ot_kept = s.sig("ot_kept", 1)
        o_ready = s.sig("o_ready", 2)
        y_done = s.sig("y_done")
        x_added = s.sig("x_added", 1)
        rv_ready = s.sig("rv_ready")
        rd_ready = s.sig("rd_ready")
        s.ready()
        block = s.ctx.enter_context(nc.Block())

        @block.sync
        def _(sp):
            for t, m in ((wq, "W_Q"), (wk, "W_K"), (wv, "W_V")):
                sp.dma_start(t[:, :], w[f"L2_attn_{m}"]).then_inc(w_loaded.sem, 16)
            sp.dma_start(wfc[:, :, :], w["L2_attn_W_fc"].rearrange("(a p) n -> p a n", p=P)).then_inc(w_loaded.sem, 16)
            for t, m in ((gamma, "gamma"), (beta, "beta")):
                sp.dma_start(t[:, :], w[f"L2_attn_{m}"].partition_broadcast(P)).then_inc(vectors_loaded.sem, 16)

        @block.gpsimd
        def _(pool):
            ln_scales_pool(pool, core, s)
            pool.memset(vs[:, :, :, P:P + 1], 1.0).then_inc(filled.sem, 1)
            pool.memset(same[:, :], 0.0).then_inc(masked.sem, 1)
            pool.memset(which[:, :], 0.0).then_inc(masked.sem, 1)
            pool.wait_ge(masked.sem, masked.past(1))
            pool.memset(which[0:HV, 0:1], 1.0).then_inc(filled.sem, 1)
            pool.memset(which[HV:P, 1:2], 1.0).then_inc(filled.sem, 1)
            pool.memset(same[0:HV, 0:HV], 1.0).then_inc(filled.sem, 1)
            pool.memset(same[HV:P, HV:P], 1.0).then_inc(filled.sem, 1)
            pool.wait_ge(filled.sem, filled.past(4))
            pool.memset(power[:, :], -0.5)
            pool.drain()
            with pool.Fori(0, B) as b:
                pool.wait_ge(rv_ready.sem, rv_ready.past(b))
                pool.tensor_tensor(rd[:, :], rv[:, :], power[:, :], ALU.pow).then_inc(rd_ready.sem, 1)

        @block.vector
        def _(dve):
            def keep_kv(c, i, g):
                m = 6 * c + 3 * i + g
                pairs = KV_GROUPS[g]
                bank = (3 * i + g) % 2
                dve.wait_ge(kv_done.sem, kv_done.past(m))
                src = kn[:, bank, 0:len(pairs) * (P + 1)].rearrange("p (a v) -> p a v", v=P + 1)
                to = kvs[:, pairs[0]:pairs[-1] + 1, :]
                dve.tensor_tensor(to[:, :, 0:P], src[:, :, 0:P],
                                  same[:, :].unsqueeze(1).to_broadcast([P, len(pairs), P]), ALU.mult)
                dve.tensor_tensor(to[:, :, P:GW], src[:, :, P:P + 1].to_broadcast([P, len(pairs), 2]),
                                  which[:, :].unsqueeze(1).to_broadcast([P, len(pairs), 2]), ALU.mult).then_inc(kvs_ready.sem, 1)

            def divide(c, i, m):
                pairs, t = KV_GROUPS[m // NT], m % NT
                width = len(pairs)
                dve.wait_ge(nd_done.sem, nd_done.past(6 * (2 * c + i) + m))
                src = kn[:, (m + 2) % 4, 0:width * GW].rearrange("p (a v) -> p a v", v=GW)
                dve.tensor_scalar(den[:, m % 2, 0:width, :], src[:, :, P:GW], 1e-8, None, ALU.add)
                dve.drain()
                dve.reciprocal(den[:, m % 2, 0:width, :], den[:, m % 2, 0:width, :])
                dve.drain()
                dve.tensor_tensor(o[:, t, pairs[0]:pairs[-1] + 1, :].rearrange("p a (h v) -> p a h v", h=2),
                                  src[:, :, 0:P].rearrange("p a (h v) -> p a h v", h=2),
                                  den[:, m % 2, 0:width, :].unsqueeze(3).to_broadcast([P, width, 2, HV]), ALU.mult).then_inc(o_ready.sem, 1)

            def add(n, i):
                for t in range(NT):
                    j = n * NT + t
                    dve.tensor_scalar(r[:, i, t, :], core.x[:, bass.ds(j, 1), :], core.mean[:, bass.ds(j, 1)],
                                      core.rstd[:, bass.ds(j, 1)], ALU.subtract, ALU.mult)
                dve.drain()
                dve.wait_ge(y_done.sem, y_done.past(n))
                dve.tensor_tensor(r[:, i, :, :], r[:, i, :, :], y[:, i, :, :], ALU.add).then_inc(x_added.sem, 1)
                dve.drain()
                for t in range(NT):
                    dve.bn_stats(rs[:, t, :], r[:, i, t, :])
                dve.drain()
                for t in range(NT):
                    dve.bn_aggr(rm[:, t, :], rs[:, t, :])
                dve.drain()
                dve.tensor_scalar(rv[:, :], rm[:, :, 1], 1e-5, None, ALU.add).then_inc(rv_ready.sem, 1)
                dve.wait_ge(rd_ready.sem, rd_ready.past(n))
                for t in range(NT):
                    dve.tensor_scalar(r[:, i, t, :], r[:, i, t, :], rm[:, t, 0:1], rd[:, t:t + 1], ALU.subtract, ALU.mult)
                dve.drain()
                for v, op in ((gamma, ALU.mult), (beta, ALU.add)):
                    dve.tensor_tensor(r[:, i, :, :], r[:, i, :, :], v[:, :].unsqueeze(1).to_broadcast([P, NT, P]), op)
                    dve.drain()
                xs = rows(core.x, n * NT, NT)
                dve.tensor_tensor(xs, xs, r[:, i, :, :], ALU.add)
                dve.drain()
                for t in range(NT):
                    dve.bn_stats(core.sums[:, bass.ds(n * NT + t, 1), :], core.x[:, bass.ds(n * NT + t, 1), :])

            ln_scales_dve(dve, core, s)
            ln_dve(dve, core, s, 0, 0)
            dve.wait_ge(vectors_loaded.sem, 32)
            dve.wait_ge(filled.sem, filled.past(4))

            def body(c, u, before, after):
                for i in range(2):
                    for g in range(3):
                        keep_kv(c, i, g)
                    for m in range(6):
                        divide(c, i, m)
                    if i == 0 and after:
                        ln_dve(dve, core, s, c + 1, 1 - u)
                    if i or before:
                        add(2 * c + i - 1, 1 - i)

            each_chunk(dve, body)
            add(2 * CHUNKS - 1, 1)

        @block.scalar
        def _(act):
            def keep_q(c, u):
                for p in range(PAIRS):
                    act.wait_ge(projected.sem, projected.past(24 * c + p))
                    act.activation(qt[:, u, p, :], pj[:, p % 2, :], ACT.Sigmoid).then_inc(act_kept.sem, 1)

            ln_act(act, core, s, 0, 0)
            keep_q(0, 0)

            def body(c, u, before, after):
                for i in range(2):
                    for t in range(NT):
                        for h in range(HALVES):
                            n = t * HALVES + h
                            act.wait_ge(projected.sem, projected.past(24 * c + 8 + 8 * i + 2 * n))
                            act.activation(ks[:, t, h * CW:(h + 1) * CW], pj[:, 0, :], ACT.Sigmoid).then_inc(act_kept.sem, 1)
                            if i or before:
                                act.wait_ge(o_turned.sem, o_turned.past(4 * (2 * c + i - 1) + n))
                                act.activation(ot[:, h * PH:(h + 1) * PH, t * P:(t + 1) * P],
                                               s.tp[:, 0, :].rearrange("p (a n) -> p a n", n=P), ACT.Copy).then_inc(ot_kept.sem, 1)
                            act.wait_ge(projected.sem, projected.past(24 * c + 8 + 8 * i + 2 * n + 1))
                            act.activation(vs[:, t, h * PH:(h + 1) * PH, 0:P],
                                           pj[:, 1, :].rearrange("p (a v) -> p a v", v=P), ACT.Copy).then_inc(v_kept.sem, 1)
                if after:
                    ln_act(act, core, s, c + 1, 1 - u)
                    keep_q(c + 1, 1 - u)

            each_chunk(act, body)
            for n in range(4):
                act.wait_ge(o_turned.sem, o_turned.past(4 * (2 * CHUNKS - 1) + n))
                act.activation(ot[:, n % HALVES * PH:(n % HALVES + 1) * PH, n // HALVES * P:(n // HALVES + 1) * P],
                               s.tp[:, 0, :].rearrange("p (a n) -> p a n", n=P), ACT.Copy).then_inc(ot_kept.sem, 1)

        @block.tensor
        def _(pe):
            def q_groups(c, u, pairs=range(PAIRS)):
                if 0 in pairs:
                    pe.wait_ge(s.xnt_ready.sem, s.xnt_ready.past(c))
                for p in pairs:
                    if p == 1:
                        pe.wait_ge(v_kept.sem, v_kept.past(8 * c - 1))
                    else:
                        pe.wait_ge(act_kept.sem, act_kept.past(16 * c + max(p - 2, -1)))
                    pe.matmul(pj[:, p % 2, :], wq[:, p * P:(p + 1) * P], core.xnt[:, u, :],
                              start=True, stop=True).then_inc(projected.sem, 1)

            def turn_quad(b, n):
                t, h = n // HALVES, n % HALVES
                if n == 0:
                    pe.wait_ge(o_ready.sem, o_ready.past(6 * b + 5))
                pe.wait_ge(ot_kept.sem, ot_kept.past(4 * b + n - 1))
                for a in range(PH):
                    last = pe.transpose(s.tp[:, 0, a * P:(a + 1) * P], o[:, t, h * PH + a, :], core.ident[:, :])
                last.then_inc(o_turned.sem, 1)

            def kv_groups(c, u, i, prev):
                for t in range(NT):
                    x_tile = core.xnt[:, u, (i * NT + t) * P:(i * NT + t + 1) * P]
                    for h in range(HALVES):
                        n = t * HALVES + h
                        pe.wait_ge(act_kept.sem, act_kept.past(16 * c + 8 + 4 * i + n - 1 - (i == 0 and n == 0)))
                        pe.matmul(pj[:, 0, :], x_tile, wk[:, h * CW:(h + 1) * CW], start=True, stop=True).then_inc(projected.sem, 1)
                        if prev:
                            turn_quad(2 * c + i - 1, n)
                        if i == 0 and n == 0:
                            pe.wait_ge(act_kept.sem, act_kept.past(16 * c + 7))
                        else:
                            pe.wait_ge(v_kept.sem, v_kept.past(8 * c + 4 * i + n - 1))
                        pe.matmul(pj[:, 1, :], x_tile, wv[:, h * CW:(h + 1) * CW], start=True, stop=True).then_inc(projected.sem, 1)

            def kv_products(c, i, g):
                m = 6 * c + 3 * i + g
                pe.wait_ge(kvs_ready.sem, kvs_ready.past(m - 2))
                for n, p in enumerate(KV_GROUPS[g]):
                    for t in range(NT):
                        last = pe.matmul(kn[:, (3 * i + g) % 2, n * (P + 1):(n + 1) * (P + 1)],
                                         ks[:, t, p * P:(p + 1) * P], vs[:, t, p, :], start=t == 0, stop=t == NT - 1)
                last.then_inc(kv_done.sem, 1)

            def q_products(c, u, i, m):
                g, t = m // NT, m % NT
                pe.wait_ge(kvs_ready.sem, kvs_ready.past(6 * c + 3 * i + (2 if m > 1 else 0)))
                if m < 2 or m > 3:
                    pe.wait_ge(o_ready.sem, o_ready.past(6 * (2 * c + i) + m - (2 if m < 2 else 4)))
                for n, p in enumerate(KV_GROUPS[g]):
                    last = pe.matmul(kn[:, (m + 2) % 4, n * GW:(n + 1) * GW], qt[:, u, p, i * N + t * P:i * N + (t + 1) * P],
                                     kvs[:, p, :], start=True, stop=True)
                last.then_inc(nd_done.sem, 1)

            def out_product(b, i, t, pairs=range(PAIRS)):
                if t == 0:
                    pe.wait_ge(ot_kept.sem, ot_kept.past(4 * b + 3))
                    pe.wait_ge(x_added.sem, x_added.past(b - 1))
                for p in pairs:
                    last = pe.matmul(y[:, i, t, :], ot[:, p, t * P:(t + 1) * P], wfc[:, p, :],
                                     start=p == 0, stop=p == PAIRS - 1)
                if t == NT - 1 and PAIRS - 1 in pairs:
                    last.then_inc(y_done.sem, 1)

            ln_pe(pe, core, s, 0, 0)
            pe.wait_ge(w_loaded.sem, 64)
            q_groups(0, 0)
            pe.wait_ge(filled.sem, filled.past(4))

            def body(c, u, before, after):
                for i in range(2):
                    b = 2 * c + i
                    prev = i or before
                    kv_groups(c, u, i, prev)
                    if prev:
                        out_product(b - 1, 1 - i, 0)
                    pe.wait_ge(act_kept.sem, act_kept.past(16 * c + 11 + 4 * i))
                    pe.wait_ge(v_kept.sem, v_kept.past(8 * c + 3 + 4 * i))
                    for g in range(3):
                        kv_products(c, i, g)
                    if i and after:
                        ln_pe(pe, core, s, c + 1, 1 - u)
                    for m in range(6):
                        q_products(c, u, i, m)
                        if prev and m < 4:
                            out_product(b - 1, 1 - i, 1, range(2 * m, 2 * m + 2))
                        if i and after:
                            q_groups(c + 1, 1 - u, range(m, m + 1) if m < 4 else range(2 * m - 4, 2 * m - 2))

            each_chunk(pe, body)
            last_b = 2 * CHUNKS - 1
            for n in range(4):
                turn_quad(last_b, n)
            for t in range(NT):
                out_product(last_b, 1, t)



def l3_ffn(core):
    nc, w = core.nc, core.w
    HID = 512
    HB = HID // P
    mats = [("w1", HB, P, 1.0), ("w2", HB, P, 1.0), ("h1", HB, HID, 1.0), ("h2", HB, HID, 1.0),
            ("w3", 1, HID, 0.5)]
    with stage(nc) as s:
        ln_signals(s)
        raw = {m: s.sb(f"raw_{m}", [P, ob, width]) for m, ob, width, _ in mats}
        scl = {m: s.sb(f"scl_{m}", [P, ob]) for m, ob, _, _ in mats}
        wt = {m: s.sb(f"wt_{m}", [P, width // P, ob * P]) for m, ob, width, _ in mats}
        g = s.sb("g", [P, HB, CW])
        ha = s.sb("ha", [P, HB, CW])
        hb = s.sb("hb", [P, HB, CW])
        hc = s.sb("hc", [P, HB, CW])
        z = s.ps("z", [P, 4, CW])
        y = s.ps("y", [P, 2, CT, P])
        w_loaded = [s.sig(f"w_loaded_{m}") for m, *_ in mats]
        w_scaled = s.sig("w_scaled")
        wt_turned = s.sig("wt_turned", 4)
        wt_kept = s.sig("wt_kept", 4)
        group_done = s.sig("group_done")
        act_done = s.sig("act_done", 12)
        gated = s.sig("gated", 4)
        y_done = s.sig("y_done")
        x_added = s.sig("x_added", 2)
        s.ready()
        blocks = [(m, o, i) for m, ob, width, _ in mats for o in range(ob) for i in range(width // P)]
        quads = [blocks[n:n + 4] for n in range(0, len(blocks), 4)]
        block = s.ctx.enter_context(nc.Block())

        @block.sync
        def _(sp):
            for (m, ob, _, _), loaded in zip(mats, w_loaded):
                sp.dma_start(raw[m][:, :, :], w[f"L3_ffn_{m}_w"].rearrange("(a p) i -> p a i", p=P)).then_inc(loaded.sem, 16)
                with nc.allow_non_contiguous_dma("one scale a row"):
                    sp.dma_start(scl[m][:, :], w[f"L3_ffn_{m}_s"].rearrange("(a p) -> p a", p=P)).then_inc(loaded.sem, 16)

        @block.gpsimd
        def _(pool):
            ln_scales_pool(pool, core, s)

        @block.vector
        def _(dve):
            ln_scales_dve(dve, core, s)
            ln_dve(dve, core, s, 0, 0)
            for (m, ob, _, half), loaded in zip(mats, w_loaded):
                dve.wait_ge(loaded.sem, 32)
                for o in range(ob):
                    last = dve.tensor_scalar(raw[m][:, o, :], raw[m][:, o, :], scl[m][:, o:o + 1], half,
                                             ALU.mult, ALU.mult)
                last.then_inc(w_scaled.sem, 1)

            def body(c, u, more=True):
                if more:
                    ln_dve(dve, core, s, c + 1, 1 - u)
                for f in range(HB):
                    dve.wait_ge(act_done.sem, act_done.past(12 * c + f))
                    dve.wait_ge(group_done.sem, group_done.past(16 * c + 2 * f + 1))
                    dve.tensor_tensor(ha[:, f, :], g[:, f, :], z[:, (2 * f + 1) % 4, :],
                                      ALU.mult).then_inc(gated.sem, 1)
                dve.wait_ge(y_done.sem, y_done.past(c))
                xs = rows(core.x, c * CT, CT)
                dve.tensor_tensor(xs, xs, y[:, u, :, :], ALU.add).then_inc(x_added.sem, 1)
                dve.wait_ge(x_added.sem, x_added.past(c))
                new_sums_dve(dve, core, c)

            each_pair(dve, 0, CHUNKS - 2, body)
            body(CHUNKS - 2, 0)
            body(CHUNKS - 1, 1, False)

        @block.scalar
        def _(act):
            ln_act(act, core, s, 0, 0)
            for n, quad in enumerate(quads):
                act.wait_ge(wt_turned.sem, wt_turned.past(n))
                for q, (m, o, i) in enumerate(quad):
                    last = act.activation(wt[m][:, i, o * P:(o + 1) * P], z[:, n % 4, q * P:(q + 1) * P], ACT.Copy)
                last.then_inc(wt_kept.sem, 1)

            def body(c, u, more=True):
                for f in range(HB):
                    act.wait_ge(group_done.sem, group_done.past(16 * c + 2 * f))
                    act.activation(g[:, f, :], z[:, 2 * f % 4, :], ACT.Silu).then_inc(act_done.sem, 1)
                if more:
                    ln_act(act, core, s, c + 1, 1 - u)
                for layer, h in ((8, hb), (12, hc)):
                    for o in range(HB):
                        act.wait_ge(group_done.sem, group_done.past(16 * c + layer + o))
                        act.activation(h[:, o, :], z[:, o, :], ACT.Gelu).then_inc(act_done.sem, 1)

            each_pair(act, 0, CHUNKS - 2, body)
            body(CHUNKS - 2, 0)
            body(CHUNKS - 1, 1, False)

        @block.tensor
        def _(pe):
            ln_pe(pe, core, s, 0, 0)
            for n, quad in enumerate(quads):
                names = [m for m, *_ in mats]
                pe.wait_ge(w_scaled.sem, w_scaled.past(max(names.index(m) for m, _, _ in quad)))
                pe.wait_ge(wt_kept.sem, wt_kept.past(n - 4))
                for q, (m, o, i) in enumerate(quad):
                    last = pe.transpose(z[:, n % 4, q * P:(q + 1) * P], raw[m][:, o, i * P:(i + 1) * P], core.ident[:, :])
                last.then_inc(wt_turned.sem, 1)
            pe.wait_ge(wt_kept.sem, wt_kept.past(len(quads) - 1))

            def body(c, u, more=True):
                pe.wait_ge(s.xnt_ready.sem, s.xnt_ready.past(c))
                for f in range(HB):
                    for half, m in enumerate(("w1", "w2")):
                        if f < 2:
                            pe.wait_ge(act_done.sem, act_done.past(12 * (c - 1) + 8 + 2 * f + half))
                        elif half == 0:
                            pe.wait_ge(act_done.sem, act_done.past(12 * c + f - 2))
                        else:
                            pe.wait_ge(gated.sem, gated.past(4 * c + f - 2))
                        pe.matmul(z[:, (2 * f + half) % 4, :], wt[m][:, 0, f * P:(f + 1) * P], core.xnt[:, u, :],
                                  start=True, stop=True).then_inc(group_done.sem, 1)
                if more:
                    ln_pe(pe, core, s, c + 1, 1 - u)
                pe.wait_ge(act_done.sem, act_done.past(12 * c + 2))
                for o in range(HB):
                    for f in range(HB):
                        if o == 0:
                            pe.wait_ge(gated.sem, gated.past(4 * c + f))
                        last = pe.matmul(z[:, o, :], wt["h1"][:, f, o * P:(o + 1) * P], ha[:, f, :],
                                         start=f == 0, stop=f == HB - 1)
                    last.then_inc(group_done.sem, 1)
                for o in range(HB):
                    for f in range(HB):
                        if o == 0:
                            pe.wait_ge(act_done.sem, act_done.past(12 * c + 4 + f))
                        last = pe.matmul(z[:, o, :], wt["h2"][:, f, o * P:(o + 1) * P], hb[:, f, :],
                                         start=f == 0, stop=f == HB - 1)
                    last.then_inc(group_done.sem, 1)
                pe.wait_ge(x_added.sem, x_added.past(c - 2))
                for j in range(CT):
                    for f in range(HB):
                        if j == 0:
                            pe.wait_ge(act_done.sem, act_done.past(12 * c + 8 + f))
                        last = pe.matmul(y[:, u, j, :], hc[:, f, j * P:(j + 1) * P], wt["w3"][:, f, :],
                                         start=f == 0, stop=f == HB - 1)
                last.then_inc(y_done.sem, 1)

            each_pair(pe, 0, CHUNKS - 2, body)
            body(CHUNKS - 2, 0)
            body(CHUNKS - 1, 1, False)



def l3_attn(core):
    nc, w = core.nc, core.w
    NT = N // P
    TERMS = 3
    STEPS = NT * HEADS // 2
    LAG = 2
    BLOCK = TERMS * DH
    ROWS = TERMS * BLOCK
    ALL_ROWS = ROWS + TERMS
    HALF = HEADS // 2
    VW = HALF * HW
    RING = 4
    T_LN, T_K, T_Q, T_SPLIT, T_V, T_MAX, T_TURN, T_PLACE, T_TURN2, T_OUT = 1, 3, 6, 8, 9, 9, 10, 11, 12, 14
    with stage(nc) as s:
        ln_signals(s, 1)
        names = ("W_q", "W_k", "W_v", "W_o")
        raw = {m: s.sb(f"raw_{m}", [P, P]) for m in names}
        wt = {m: s.sb(f"wt_{m}", [P, P]) for m in names}
        ident_b = s.sb("ident_b", [P, P], BF16)
        ones = s.sb("ones", [TERMS, CW], BF16)
        proj = s.sb("proj", [P, 2, CW])
        left = s.sb("left", [P, 2, CW])
        zero = s.sb("zero", [P, 1])
        parts = s.sb("parts", [P, 2, TERMS, CW], BF16)
        kx = s.sb("kx", [ALL_ROWS, 2, HEADS, CW], BF16)
        qx = s.sb("qx", [ALL_ROWS, 2, HEADS, CW], BF16)
        vz = s.sb("vz", [P, 2, CT, 2, HALF, VW + HW])
        mx = s.sb("mx", [P, 2, NT, HEADS])
        rest = s.sb("rest", [P, 2, NT, HEADS])
        m3 = s.sb("m3", [P, 2, NT, P // HEADS, HEADS], BF16)
        nm = s.sb("nm", [P, 2, N], BF16)
        e = s.sb("e", [P, RING, 2, N])
        oc = s.sb("oc", [VW, 2, N])
        den = s.sb("den", [P, NT, HEADS])
        o = s.sb("o", [P, NT, P])
        ot = s.sb("ot", [P, NT, P])
        pj = s.ps("pj", [P, CW])
        sa = s.ps("sa", [P, 2, 2, N])
        sc = s.ps("sc", [P, 2, 2, N])
        ob = s.ps("ob", [P, 2, CW])
        mb = pj[:, :].rearrange("p (a n) -> p a n", a=2)
        nm_ps = s.tp[:, 0, 0:P].bitcast(BF16)
        mt = s.tp[:, 0, 0:NT * HEADS * HW].rearrange("p (t h e) -> p t h e", t=NT, h=HEADS)
        w_loaded = s.sig("w_loaded")
        w_turned = s.sig("w_turned")
        w_kept = s.sig("w_kept")
        ident_ready = s.sig("ident_ready")
        ones_ready = s.sig("ones_ready")
        ones_loaded = s.sig("ones_loaded")
        v_clear = s.sig("v_clear")
        projected = s.sig("projected")
        pj_kept = s.sig("pj_kept", 1)
        split_step = s.sig("split_step")
        split_done = s.sig("split_done", 2)
        parts_stored = [s.sig(f"parts_stored{n}", 16) for n in range(2)]
        kq_loaded = [s.sig(f"kq_loaded{u}") for u in range(2)]
        sa_done = s.sig("sa_done")
        max_done = s.sig("max_done", 2)
        m3_ready = s.sig("m3_ready")
        nm_turned = s.sig("nm_turned")
        nm_kept = s.sig("nm_kept", 1)
        nm_stored = s.sig("nm_stored")
        nm_moved = s.sig("nm_moved")
        sc_done = s.sig("sc_done")
        exp_done = s.sig("exp_done", 2)
        av_done = s.sig("av_done", RING)
        ob_kept = s.sig("ob_kept", 2)
        o_turned = s.sig("o_turned", 1)
        o_ready = s.sig("o_ready", 3)
        o_turned2 = s.sig("o_turned2")
        ot_kept = s.sig("ot_kept")
        y_done = s.sig("y_done")
        x_added = s.sig("x_added", 2)
        s.ready()
        LOADS = 2 * TERMS * TERMS
        block = s.ctx.enter_context(nc.Block())

        def groups(n):
            return (2 * n, 2 * n + 1) if n < STEPS // 2 else ()

        @block.sync
        def _(sp):
            for m in names:
                sp.dma_start(raw[m][:, :], w[f"L3_attn_{m}"]).then_inc(w_loaded.sem, 16)

            def store(c, u):
                for n in range(2):
                    sp.wait_ge(split_done.sem, split_done.past(2 * c + n))
                    sp.dma_start(core.parts_dram[u, n].rearrange("a f t -> f a t"), parts[:, n, :, :]).then_inc(parts_stored[n].sem, 16)

            def load(c, u, free=True):
                if free:
                    sp.wait_ge(sc_done.sem, sc_done.past(2 * STEPS * (c - 1) - 1))
                for n in range(2):
                    sp.wait_ge(parts_stored[n].sem, 32 + 16 * c)
                for a in range(TERMS):
                    for b in range(TERMS):
                        at = a * BLOCK + b * DH
                        for n, (t, part) in enumerate(((kx, a), (qx, b))):
                            sp.dma_start(t[at:at + DH, u, :, :],
                                         core.parts_dram[u, n, part].rearrange("(h d) t -> d h t", d=DH)).then_inc(kq_loaded[u].sem, 16)

            sp.wait_ge(ones_ready.sem, 1)
            sp.dma_start(kx[ROWS:ALL_ROWS, :, :, :].rearrange("p u h t -> p (u h) t"),
                         ones[:, :].unsqueeze(1).to_broadcast([TERMS, 2 * HEADS, CW])).then_inc(ones_loaded.sem, 16)
            store(0, 0)
            load(0, 0, False)
            store(1, 1)
            load(1, 1, False)
            with sp.Fori(1, CHUNKS // 2) as pair:
                for u in range(2):
                    store(pair * 2 + u, u)
                    load(pair * 2 + u, u)

        @block.gpsimd
        def _(pool):
            ln_scales_pool(pool, core, s, range(2))
            pool.memset(vz[:, :, :, :, :, :], 0.0).then_inc(v_clear.sem, 1)
            pool.wait_ge(v_clear.sem, 1)
            pool.memset(vz[:, :, :, :, :, :].rearrange("p u j a h c -> p (u j a) (h c)").rearrange("p b (h c) -> p b h c", h=HALF)[:, :, :, DH:HW],
                        1.0).then_inc(v_clear.sem, 1)
            pool.memset(zero[:, :], 0.0).then_inc(v_clear.sem, 1)
            pool.wait_ge(v_clear.sem, 3)

            ln_scales_pool(pool, core, s, range(2, CHUNKS))

            def split(c, u):
                nothing = zero[:, :].to_broadcast([P, CW])
                for n in range(2):
                    at = 2 * (c - 2) + n
                    pool.wait_ge(pj_kept.sem, pj_kept.past(3 * c + n))
                    pool.wait_ge(parts_stored[n].sem, 16 + 16 * c)
                    pool.tensor_tensor(parts[:, n, 0, :], proj[:, n, :], nothing, ALU.add).then_inc(split_step.sem, 1)
                    pool.wait_ge(split_step.sem, split_step.past(3 * at))
                    pool.tensor_tensor(left[:, n, :], proj[:, n, :], parts[:, n, 0, :], ALU.subtract).then_inc(split_step.sem, 1)
                    pool.wait_ge(split_step.sem, split_step.past(3 * at + 1))
                    pool.tensor_tensor(parts[:, n, 1, :], left[:, n, :], nothing, ALU.add).then_inc(split_step.sem, 1)
                    pool.wait_ge(split_step.sem, split_step.past(3 * at + 2))
                    pool.tensor_tensor(parts[:, n, 2, :], left[:, n, :], parts[:, n, 1, :], ALU.subtract).then_inc(split_done.sem, 1)

            each_pair(pool, 2, CHUNKS, split)

        @block.vector
        def _(dve):
            def split(c, n):
                dve.wait_ge(pj_kept.sem, pj_kept.past(3 * c + n))
                dve.wait_ge(parts_stored[n].sem, 16 + 16 * c)
                dve.tensor_copy(parts[:, n, 0, :], proj[:, n, :])
                dve.drain()
                dve.tensor_tensor(left[:, n, :], proj[:, n, :], parts[:, n, 0, :], ALU.subtract)
                dve.drain()
                dve.tensor_copy(parts[:, n, 1, :], left[:, n, :])
                dve.drain()
                dve.tensor_tensor(parts[:, n, 2, :], left[:, n, :], parts[:, n, 1, :], ALU.subtract).then_inc(split_done.sem, 1)

            def keep_v(c, u):
                dve.wait_ge(projected.sem, projected.past(3 * c + 2))
                for j in range(CT):
                    last = dve.tensor_copy(vz[:, u, j, :, :, 0:DH], pj[:, j * P:(j + 1) * P].rearrange("p (a h e) -> p a h e", a=2, h=HALF))
                last.then_inc(pj_kept.sem, 1)

            def largest(b, i, n):
                t, pairs = n // HALF, n % HALF
                dve.wait_ge(sa_done.sem, sa_done.past(STEPS * b + n))
                dve.tensor_reduce(mx[:, i, t, 2 * pairs:2 * pairs + 2], sa[:, n % 2, :, :], AX.X, ALU.max).then_inc(max_done.sem, 1)

            def split_maxima(i):
                m = mx[:, i, :, :]
                dve.drain()
                dve.tensor_scalar(m3[:, i, :, 0, :], m, -1.0, None, ALU.mult)
                dve.drain()
                dve.scalar_tensor_tensor(rest[:, i, :, :], m, -1.0, m3[:, i, :, 0, :], ALU.mult, ALU.subtract)
                dve.drain()
                dve.tensor_copy(m3[:, i, :, 1, :], rest[:, i, :, :])
                dve.drain()
                dve.tensor_tensor(m3[:, i, :, 2, :], rest[:, i, :, :], m3[:, i, :, 1, :], ALU.subtract).then_inc(m3_ready.sem, 1)

            def normalise(b):
                dve.wait_ge(o_turned.sem, o_turned.past(b))
                dve.reciprocal(den[:, :, :], mt[:, :, :, DH])
                dve.drain()
                for t in range(NT):
                    last = dve.tensor_tensor(o[:, t, :].rearrange("p (h e) -> p h e", h=HEADS), mt[:, t, :, 0:DH],
                                             den[:, t, :].unsqueeze(2).to_broadcast([P, HEADS, DH]), ALU.mult)
                last.then_inc(o_ready.sem, 1)

            def add(b):
                xs = rows(core.x, b * NT, NT)
                dve.wait_ge(y_done.sem, y_done.past(b))
                dve.tensor_tensor(xs, xs, mb[:, 1, :].rearrange("p (t e) -> p t e", t=NT), ALU.add).then_inc(x_added.sem, 1)
                dve.drain()
                for t in range(NT):
                    dve.bn_stats(core.sums[:, bass.ds(b * NT + t, 1), :], core.x[:, bass.ds(b * NT + t, 1), :])

            dve.memset(ones[:, :], 1.0).then_inc(ones_ready.sem, 1)
            dve.memset(m3[:, :, :, TERMS:, :], 0.0)
            dve.tensor_copy(ident_b[:, :], core.ident[:, :]).then_inc(ident_ready.sem, 1)
            ln_scales_dve(dve, core, s)
            ln_dve(dve, core, s, 0, 0)
            ln_dve(dve, core, s, 1, 1)
            split(0, 0)
            split(0, 1)
            dve.wait_ge(v_clear.sem, 2)
            keep_v(0, 0)
            split(1, 0)
            split(1, 1)
            for n in range(STEPS):
                largest(0, 0, n)
            split_maxima(0)

            def body(c, u, before, after):
                for i in range(2):
                    b = 2 * c + i
                    prev, more = i or before, i == 0 or after
                    for n in range(STEPS):
                        if more:
                            for g in groups(n):
                                largest(b + 1, 1 - i, g)
                        if n == T_V and i == 0 and after:
                            keep_v(c + 1, 1 - u)
                        if n == T_TURN and prev:
                            normalise(b - 1)
                        if n == T_SPLIT and more:
                            split_maxima(1 - i)
                        if n == T_OUT and prev:
                            add(b - 1)
                        if n == STEPS - 1 and i == 0 and after > 1:
                            ln_dve(dve, core, s, c + 2, u)

            each_chunk(dve, body)
            normalise(2 * CHUNKS - 1)
            add(2 * CHUNKS - 1)

        @block.scalar
        def _(act):
            def keep(c, n):
                act.wait_ge(projected.sem, projected.past(3 * c + n))
                act.wait_ge(split_done.sem, split_done.past(2 * c + n - 2))
                act.activation(proj[:, n, :], pj[:, :], ACT.Copy, scale=1.0 / DH ** 0.5 if n else 1.0).then_inc(pj_kept.sem, 1)

            def exp(b, n):
                act.wait_ge(sc_done.sem, sc_done.past(STEPS * b + n))
                act.wait_ge(av_done.sem, av_done.past(STEPS * b + n - RING))
                act.activation(e[:, n % RING, :, :], sc[:, n % 2, :, :], ACT.Exp).then_inc(exp_done.sem, 1)

            def keep_nm(b, i):
                act.wait_ge(nm_turned.sem, nm_turned.past(b))
                act.activation(nm[:, i, :], nm_ps[:, :], ACT.Copy).then_inc(nm_kept.sem, 1)
                act.wait_ge(nm_kept.sem, nm_kept.past(b))
                act.dma_start(core.maxima_dram, nm[0:TERMS * HEADS, i, :]).then_inc(nm_stored.sem, 16)

            def place_nm(b, u, i):
                act.wait_ge(nm_stored.sem, (b + 1) * 16)
                act.dma_start(qx[ROWS:ALL_ROWS, u, :, i * N:(i + 1) * N],
                              core.maxima_dram.rearrange("(a h) q -> a h q", h=HEADS)).then_inc(nm_moved.sem, 16)

            def keep_ob(b, half):
                act.wait_ge(av_done.sem, av_done.past(STEPS * b + (half + 1) * (STEPS // 2) - 1))
                act.wait_ge(o_turned.sem, o_turned.past(b - 1))
                act.activation(oc[:, half, :], ob[0:VW, half, 0:N], ACT.Copy).then_inc(ob_kept.sem, 1)

            def keep_ot(b):
                act.wait_ge(o_turned2.sem, o_turned2.past(b))
                act.activation(ot[:, :, :], mb[:, 0, :].rearrange("p (t e) -> p t e", t=NT), ACT.Copy).then_inc(ot_kept.sem, 1)

            act.wait_ge(w_turned.sem, 1)
            for n, m in enumerate(names):
                last = act.activation(wt[m][:, :], sa[:, 0, :, :].rearrange("p a n -> p (a n)")[:, n * P:(n + 1) * P], ACT.Copy)
            last.then_inc(w_kept.sem, 1)
            for c in range(2):
                ln_act(act, core, s, c, c)
                keep(c, 0)
                keep(c, 1)
            keep_nm(0, 0)
            place_nm(0, 0, 0)

            def body(c, u, before, after):
                for i in range(2):
                    b = 2 * c + i
                    prev, more = i or before, i == 0 or after
                    for n in range(STEPS):
                        exp(b, n)
                        if n == T_LN and i == 1 and after > 1:
                            ln_act(act, core, s, c + 2, u)
                        if n == LAG and prev:
                            keep_ob(b - 1, 1)
                        if n == T_K and i == 1 and after > 1:
                            keep(c + 2, 0)
                        if n == T_Q and i == 1 and after > 1:
                            keep(c + 2, 1)
                        if n == T_TURN2 and prev:
                            keep_ot(b - 1)
                        if n == STEPS // 2 + LAG:
                            keep_ob(b, 0)
                        if n == T_MAX and more:
                            keep_nm(b + 1, 1 - i)
                        if n == T_PLACE and more:
                            place_nm(b + 1, u if i == 0 else 1 - u, 1 - i)

            each_chunk(act, body)
            keep_ob(2 * CHUNKS - 1, 1)
            keep_ot(2 * CHUNKS - 1)

        @block.tensor
        def _(pe):
            def project(c, u, n):
                pe.wait_ge(pj_kept.sem, pj_kept.past(3 * c + n - 1))
                if n < 2:
                    pe.wait_ge(s.xnt_ready.sem, s.xnt_ready.past(c))
                    pe.matmul(pj[:, :], wt["W_q" if n else "W_k"][:, :], core.xnt[:, u, :], start=True, stop=True).then_inc(projected.sem, 1)
                else:
                    for j in range(CT):
                        last = pe.matmul(pj[:, j * P:(j + 1) * P], core.xnt[:, u, j * P:(j + 1) * P], wt["W_v"][:, :],
                                         start=True, stop=True)
                    last.then_inc(projected.sem, 1)

            def row_scores(b, u, i, n):
                t, pairs = n // HALF, n % HALF
                pe.wait_ge(max_done.sem, max_done.past(STEPS * b + n - 2))
                for a in range(2):
                    h = 2 * pairs + a
                    last = pe.matmul(sa[:, n % 2, a, :], qx[0:ROWS, u, h, (i * NT + t) * P:(i * NT + t + 1) * P],
                                     kx[0:ROWS, u, h, i * N:(i + 1) * N], start=True, stop=True)
                last.then_inc(sa_done.sem, 1)

            def turn_maxima(b, i):
                pe.wait_ge(o_ready.sem, o_ready.past(b - 3))
                pe.wait_ge(m3_ready.sem, m3_ready.past(b))
                for t in range(NT):
                    last = pe.transpose(nm_ps[:, t * P:(t + 1) * P],
                                        m3[:, i, t, :, :].rearrange("p a h -> p (a h)"), ident_b[:, :])
                last.then_inc(nm_turned.sem, 1)

            def key_scores(b, u, i, n):
                h, k = n // NT * 2, n % NT
                pe.wait_ge(exp_done.sem, exp_done.past(STEPS * b + n - 2))
                for a in range(2):
                    last = pe.matmul(sc[:, n % 2, a, :], kx[:, u, h + a, (i * NT + k) * P:(i * NT + k + 1) * P],
                                     qx[:, u, h + a, i * N:(i + 1) * N], start=True, stop=True)
                last.then_inc(sc_done.sem, 1)

            def values(b, u, i, n):
                h, k = n // NT * 2, n % NT
                half, at = n // (STEPS // 2), n % (STEPS // 2)
                if at == 0:
                    pe.wait_ge(ob_kept.sem, ob_kept.past(2 * b + half - 2))
                pe.wait_ge(exp_done.sem, exp_done.past(STEPS * b + n))
                for a in range(2):
                    own = (h + a) % HALF
                    cols = vz[:, u, i * NT + k, half, :, :].rearrange("p h c -> p (h c)")[:, own * VW:(own + 1) * VW]
                    last = pe.matmul(ob[0:VW, half, 0:N], cols, e[:, n % RING, a, :],
                                     start=at == 0 and a == 0, stop=at == STEPS // 2 - 1 and a == 1)
                last.then_inc(av_done.sem, 1)

            def turn(b):
                pe.wait_ge(ob_kept.sem, ob_kept.past(2 * b + 1))
                for t in range(NT):
                    for half in range(2):
                        last = pe.transpose(mt[:, t, half * HALF:(half + 1) * HALF, :].rearrange("p h e -> p (h e)"),
                                            oc[:, half, t * P:(t + 1) * P], core.ident[0:VW, 0:VW])
                last.then_inc(o_turned.sem, 1)

            def turn2(b):
                pe.wait_ge(o_ready.sem, o_ready.past(b))
                for t in range(NT):
                    last = pe.transpose(mb[:, 0, t * P:(t + 1) * P], o[:, t, :], core.ident[:, :])
                last.then_inc(o_turned2.sem, 1)

            def out_product(b):
                pe.wait_ge(ot_kept.sem, ot_kept.past(b))
                for t in range(NT):
                    last = pe.matmul(mb[:, 1, t * P:(t + 1) * P], ot[:, t, :], wt["W_o"][:, :], start=True, stop=True)
                last.then_inc(y_done.sem, 1)

            pe.wait_ge(w_loaded.sem, 16 * len(names))
            for n, m in enumerate(names):
                last = pe.transpose(sa[:, 0, :, :].rearrange("p a n -> p (a n)")[:, n * P:(n + 1) * P], raw[m][:, :], core.ident[:, :])
            last.then_inc(w_turned.sem, 1)
            ln_pe(pe, core, s, 0, 0)
            pe.wait_ge(w_kept.sem, 1)
            for n in range(3):
                project(0, 0, n)
            ln_pe(pe, core, s, 1, 1)
            for n in range(2):
                project(1, 1, n)
            pe.wait_ge(kq_loaded[0].sem, 16 * LOADS)
            for n in range(STEPS):
                row_scores(0, 0, 0, n)
            pe.wait_ge(s.xnt_ready.sem, s.xnt_ready.past(1))
            pe.wait_ge(ident_ready.sem, 1)
            turn_maxima(0, 0)
            pe.wait_ge(ones_loaded.sem, 16)

            def body(c, u, before, after):
                for i in range(2):
                    b = 2 * c + i
                    prev, more = i or before, i == 0 or after
                    for n in range(STEPS):
                        if n == 0:
                            if i == 1 and after:
                                pe.wait_ge(kq_loaded[1 - u].sem, ((c + 1 - (1 - u)) * 8 + 16) * LOADS)
                            pe.wait_ge(nm_moved.sem, (b + 1) * 16)
                        if more:
                            for g in groups(n):
                                row_scores(b + 1, u if i == 0 else 1 - u, 1 - i, g)
                        if i == 1 and after > 1:
                            if n == T_LN:
                                ln_pe(pe, core, s, c + 2, u)
                            if n == T_K:
                                pe.wait_ge(x_added.sem, x_added.past(2 * c - 1))
                                project(c + 2, u, 0)
                            if n == T_Q:
                                project(c + 2, u, 1)
                        if i == 0 and after and n == T_V:
                            pe.wait_ge(x_added.sem, x_added.past(2 * c - 2))
                            project(c + 1, 1 - u, 2)
                        if n == T_MAX and more:
                            if i == 1 and after > 1:
                                pe.wait_ge(s.xnt_ready.sem, s.xnt_ready.past(c + 2))
                            turn_maxima(b + 1, 1 - i)
                        if prev:
                            if n == T_TURN:
                                if more:
                                    pe.wait_ge(nm_kept.sem, nm_kept.past(b + 1))
                                turn(b - 1)
                            if n == T_TURN2:
                                if i == 1 and after > 1:
                                    pe.wait_ge(pj_kept.sem, pj_kept.past(3 * (c + 2) + 1))
                                elif i == 0 and after:
                                    pe.wait_ge(pj_kept.sem, pj_kept.past(3 * (c + 1) + 2))
                                pe.wait_ge(x_added.sem, x_added.past(b - 2))
                                turn2(b - 1)
                            if n == T_OUT:
                                out_product(b - 1)
                        key_scores(b, u, i, n)
                        if n >= LAG:
                            values(b, u, i, n - LAG)
                        elif i == 1:
                            values(b - 1, u, 0, n - LAG + STEPS)
                        elif before:
                            values(b - 1, 1 - u, 1, n - LAG + STEPS)

            each_chunk(pe, body)
            last_b = 2 * CHUNKS - 1
            for n in range(STEPS - LAG, STEPS):
                values(last_b, 1, 1, n)
            turn(last_b)
            pe.wait_ge(x_added.sem, x_added.past(last_b - 1))
            turn2(last_b)
            out_product(last_b)



def begin(core):
    nc = core.nc
    with stage(nc) as s:
        PIECES = 4
        x_loaded = [s.sig(f"x_loaded{n}") for n in range(PIECES)]
        id_clear = s.sig("id_clear")
        s.ready()
        block = s.ctx.enter_context(nc.Block())

        @block.sync
        def _(sp):
            x_rows = core.w["L0_attn_x"].rearrange("b (n p) d -> p (b n) d", p=P)
            for n in range(PIECES):
                tiles = slice(n * TILES // PIECES, (n + 1) * TILES // PIECES)
                sp.dma_start(core.x[:, tiles, :], x_rows[:, tiles, :]).then_inc(x_loaded[n].sem, 16)

        @block.gpsimd
        def _(pool):
            pool.memset(core.power[:, :], -0.5)
            pool.memset(core.ident[:, :], 0.0).then_inc(id_clear.sem, 1)
            pool.wait_ge(id_clear.sem, 1)
            pool.affine_select(out=core.ident[:, :], in_=core.ident[:, :], compare_op=ALU.not_equal, fill=1.0,
                               base=0, pattern=[[-1, P]], channel_multiplier=1)

        @block.vector
        def _(dve):
            for n in range(PIECES):
                dve.wait_ge(x_loaded[n].sem, 16)
                for c in range(n * CHUNKS // PIECES, (n + 1) * CHUNKS // PIECES):
                    new_sums_dve(dve, core, c)


def end(core):
    nc = core.nc
    with stage(nc) as s:
        out_stored = s.sig("out_stored")
        s.ready()
        block = s.ctx.enter_context(nc.Block())

        @block.sync
        def _(sp):
            sp.dma_start(core.out.rearrange("b (n p) d -> p (b n) d", p=P), core.x[:, :, :]).then_inc(out_stored.sem, 16)
            sp.wait_ge(out_stored.sem, 16)


STAGES = [l0_ffn, l0_attn, l0_ffn, l1_ffn, l1_attn, l1_ffn, l2_ffn, l2_attn, l2_ffn, l3_ffn, l3_attn, l3_ffn]


def build(nc, inputs, out):
    with ExitStack() as ctx:
        core = Core(nc, ctx, inputs, out)
        begin(core)
        for run in STAGES:
            run(core)
        end(core)



def kernel(**inputs):
    import numpy as _np
    import concourse.bacc as _bacc
    from concourse import mybir as _mybir
    from concourse.bass_utils import run_bass_kernel_spmd as _run

    nc = _bacc.Bacc("TRN2", target_bir_lowering=False, num_devices=1)
    arrays, aps = {}, {}
    for name, value in inputs.items():
        a = _np.ascontiguousarray(value)
        arrays[f"in_{name}_dram"] = a
        aps[name] = nc.dram_tensor(f"in_{name}_dram", a.shape, _mybir.dt.from_np(a.dtype), kind="ExternalInput").ap()
    shape = inputs["L0_attn_x"].shape
    out = nc.dram_tensor("out_0_dram", shape, _mybir.dt.float32, kind="ExternalOutput").ap()
    build(nc, aps, out)
    r = _run(nc, [arrays], core_ids=[0])
    return r.results[0]["out_0_dram"]
```
